# Optimizing a Trainium2 kernel written in Bass

```python
import numpy as np
import jax
import jax.numpy as jnp

def _softmax(x, axis=-1):
    return jax.nn.softmax(x, axis=axis)

def _gelu(x):
    return jax.nn.gelu(x, approximate=True)

def _silu(x):
    return jax.nn.silu(x)

def _sigmoid(x):
    return jax.nn.sigmoid(x)

def _layernorm(x, axis=-1, eps=1e-05):
    m = jnp.mean(x, axis=axis, keepdims=True)
    v = jnp.var(x, axis=axis, keepdims=True)
    return (x - m) / jnp.sqrt(v + eps)

def _scatter_add(tgt, idx, src, axis=0):
    return tgt.at[idx].add(src)

def _segment_sum(src, seg, n):
    return jax.ops.segment_sum(src, seg, n)
kernel_name = 'mk_vit_tower_d2_tok_img256_r4_19ad4b'

def setup_inputs(seed: int=0):
    np.random.seed(seed)
    _w = jnp.asarray

    def _rec_inputs():
        import jax
        import jax.numpy as jnp
        _rk = jax.random.key(seed)
        x = 7.22013e-05 + 1.00017 * jax.random.normal(jax.random.fold_in(_rk, 1), (2, 64, 64, 64), jnp.float32)
        return x
    x = _rec_inputs()

    def _L0_tok_setup():
        import jax, jax.numpy as jnp
        import numpy as np
        K = 3
        PAD = (K - 1) // 2
        BN_EPS = 1e-05

        def _unfold(x):
            b, c, h, w = x.shape
            xp = jnp.pad(x, ((0, 0), (0, 0), (PAD, PAD), (PAD, PAD)))
            shifts = [xp[:, :, i:i + h, j:j + w] for i in range(K) for j in range(K)]
            return jnp.stack(shifts, axis=2)
        key = jax.random.key(seed)
        ks = jax.random.split(key, 4)
        b, c, h, w = (8, 64, 64, 64)
        cr = c // 4
        x = jax.random.normal(ks[0], (b, c, h, w), dtype=jnp.float32)
        conv1_w = jax.random.normal(ks[1], (cr, c), dtype=jnp.float32) * (1.0 / np.sqrt(c))
        conv1_b = jnp.zeros((cr,), dtype=jnp.float32)
        bn_gamma = jnp.ones((cr,), dtype=jnp.float32)
        bn_beta = jnp.zeros((cr,), dtype=jnp.float32)
        bn_mean = jnp.zeros((cr,), dtype=jnp.float32)
        bn_var = jnp.ones((cr,), dtype=jnp.float32)
        conv2_w = jax.random.normal(ks[2], (K * K, cr), dtype=jnp.float32) * (1.0 / np.sqrt(cr))
        conv2_b = jnp.zeros((K * K,), dtype=jnp.float32)
        return {'x': x, 'conv1_w': conv1_w, 'conv1_b': conv1_b, 'bn_gamma': bn_gamma, 'bn_beta': bn_beta, 'bn_mean': bn_mean, 'bn_var': bn_var, 'conv2_w': conv2_w, 'conv2_b': conv2_b}
    _L0_tok_all = _L0_tok_setup()
    _L0_tok_in = {k: v for k, v in _L0_tok_all.items() if k in ('conv1_w', 'conv1_b', 'bn_gamma', 'bn_beta', 'bn_mean', 'bn_var', 'conv2_w', 'conv2_b')}
    del _L0_tok_all

    def _L0_attn_setup():
        import jax, jax.numpy as jnp
        import numpy as np
        import math
        EMBED_DIM = 64
        SEQ_LEN = 1024
        BATCH = 4
        NUM_SCALES = (24.0, 720.0)
        key = jax.random.key(seed)
        ks = jax.random.split(key, 8)
        d = EMBED_DIM
        x = jax.random.normal(ks[0], (BATCH, SEQ_LEN, d), dtype=jnp.float32)
        s = 1.0 / math.sqrt(d)
        Wq = jax.random.uniform(ks[1], (d, d), jnp.float32, -s, s)
        bq = jax.random.uniform(ks[2], (d,), jnp.float32, -s, s)
        Wk = jax.random.uniform(ks[3], (d, d), jnp.float32, -s, s)
        bk = jax.random.uniform(ks[4], (d,), jnp.float32, -s, s)
        Wv = jax.random.uniform(ks[5], (d, d), jnp.float32, -s, s)
        bv = jax.random.uniform(ks[6], (d,), jnp.float32, -s, s)
        beta = jnp.ones((len(NUM_SCALES),), dtype=jnp.float32)
        return {'x': x, 'Wq': Wq, 'bq': bq, 'Wk': Wk, 'bk': bk, 'Wv': Wv, 'bv': bv, 'beta': beta}
    _L0_attn_all = _L0_attn_setup()
    _L0_attn_in = {k: v for k, v in _L0_attn_all.items() if k in ('Wq', 'bq', 'Wk', 'bk', 'Wv', 'bv', 'beta')}
    del _L0_attn_all

    def _L0_ffn_setup():
        import jax, jax.numpy as jnp
        import numpy as np
        B, S, D, F, E, K = (8, 512, 64, 256, 8, 2)
        key = jax.random.key(seed)
        ks = jax.random.split(key, 10)
        s = 0.02
        return {'x': jax.random.normal(ks[0], (B, S, D), dtype=jnp.float32), 'Wr': jax.random.normal(ks[1], (D, E), dtype=jnp.float32) * s, 'W1s': jax.random.normal(ks[2], (D, F), dtype=jnp.float32) * s, 'b1s': jnp.zeros((F,), dtype=jnp.float32), 'W2s': jax.random.normal(ks[3], (F, D), dtype=jnp.float32) * s, 'b2s': jnp.zeros((D,), dtype=jnp.float32), 'W1p': jax.random.normal(ks[4], (E, D, F), dtype=jnp.float32) * s, 'b1p': jnp.zeros((E, F), dtype=jnp.float32), 'W2p': jax.random.normal(ks[5], (E, F, D), dtype=jnp.float32) * s, 'b2p': jnp.zeros((E, D), dtype=jnp.float32)}
    _L0_ffn_all = _L0_ffn_setup()
    _L0_ffn_in = {k: v for k, v in _L0_ffn_all.items() if k in ('Wr', 'W1s', 'b1s', 'W2s', 'b2s', 'W1p', 'b1p', 'W2p', 'b2p')}
    del _L0_ffn_all

    def _L1_attn_setup():
        import jax, jax.numpy as jnp
        import numpy as np
        EMBED_DIM = 64
        SEQ_LEN = 1024
        BATCH = 8
        ALPHA = 0.99
        key = jax.random.key(seed)
        k_x, k_w, k_b = jax.random.split(key, 3)
        x = jax.random.normal(k_x, (BATCH, SEQ_LEN, EMBED_DIM), dtype=jnp.float32)
        Wqkv = jax.random.normal(k_w, (EMBED_DIM, 3 * EMBED_DIM), dtype=jnp.float32) * EMBED_DIM ** (-0.5)
        bqkv = jax.random.normal(k_b, (3 * EMBED_DIM,), dtype=jnp.float32) * 0.02
        return {'x': x, 'Wqkv': Wqkv, 'bqkv': bqkv}
    _L1_attn_all = _L1_attn_setup()
    _L1_attn_in = {k: v for k, v in _L1_attn_all.items() if k in ('Wqkv', 'bqkv')}
    del _L1_attn_all

    def _L1_ffn_setup():
        import jax, jax.numpy as jnp
        import numpy as np
        B, T, C = (64, 96, 64)
        NH, NKV = (4, 2)
        HD = C // NH
        NREP = NH // NKV
        NE, TOPK = (8, 2)
        HID = int(8 / 3 * C)
        EPS_RMS = 1e-06

        def _rope_tables(t_len):
            inv_freq = 1.0 / 10000.0 ** (np.arange(0, HD, 2, dtype=np.float32) / HD)
            t = np.arange(t_len, dtype=np.float32)
            freqs = np.outer(t, inv_freq)
            emb = np.concatenate([freqs, freqs], axis=-1)
            return (jnp.asarray(np.cos(emb)), jnp.asarray(np.sin(emb)))

        def _rotate_half(x):
            h = x.shape[-1] // 2
            return jnp.concatenate([-x[..., h:], x[..., :h]], axis=-1)

        def _rmsnorm(v, w):
            return v * jax.lax.rsqrt(jnp.mean(v * v, axis=-1, keepdims=True) + EPS_RMS) * w
        key = jax.random.key(seed)
        ks = jax.random.split(key, 10)
        s = lambda k, shape: jax.random.normal(k, shape, jnp.float32) * 0.02
        return {'x': jax.random.normal(ks[0], (B, T, C), jnp.float32), 'ln1_w': jnp.ones((C,), jnp.float32), 'ln2_w': jnp.ones((C,), jnp.float32), 'wq': s(ks[1], (NH * HD, C)), 'wk': s(ks[2], (NKV * HD, C)), 'wv': s(ks[3], (NKV * HD, C)), 'wo': s(ks[4], (C, C)), 'router_w': s(ks[5], (NE, C)), 'w1': s(ks[6], (NE, HID, C)), 'w2': s(ks[7], (NE, C, HID)), 'w3': s(ks[8], (NE, HID, C))}
    _L1_ffn_all = _L1_ffn_setup()
    _L1_ffn_in = {k: v for k, v in _L1_ffn_all.items() if k in ('ln1_w', 'ln2_w', 'wq', 'wk', 'wv', 'wo', 'router_w', 'w1', 'w2', 'w3')}
    del _L1_ffn_all
    return {'x': x, 'L0_tok_conv1_w': _L0_tok_in['conv1_w'], 'L0_tok_conv1_b': _L0_tok_in['conv1_b'], 'L0_tok_bn_gamma': _L0_tok_in['bn_gamma'], 'L0_tok_bn_beta': _L0_tok_in['bn_beta'], 'L0_tok_bn_mean': _L0_tok_in['bn_mean'], 'L0_tok_bn_var': _L0_tok_in['bn_var'], 'L0_tok_conv2_w': _L0_tok_in['conv2_w'], 'L0_tok_conv2_b': _L0_tok_in['conv2_b'], 'L0_attn_Wq': _L0_attn_in['Wq'], 'L0_attn_bq': _L0_attn_in['bq'], 'L0_attn_Wk': _L0_attn_in['Wk'], 'L0_attn_bk': _L0_attn_in['bk'], 'L0_attn_Wv': _L0_attn_in['Wv'], 'L0_attn_bv': _L0_attn_in['bv'], 'L0_attn_beta': _L0_attn_in['beta'], 'L0_ffn_Wr': _L0_ffn_in['Wr'], 'L0_ffn_W1s': _L0_ffn_in['W1s'], 'L0_ffn_b1s': _L0_ffn_in['b1s'], 'L0_ffn_W2s': _L0_ffn_in['W2s'], 'L0_ffn_b2s': _L0_ffn_in['b2s'], 'L0_ffn_W1p': _L0_ffn_in['W1p'], 'L0_ffn_b1p': _L0_ffn_in['b1p'], 'L0_ffn_W2p': _L0_ffn_in['W2p'], 'L0_ffn_b2p': _L0_ffn_in['b2p'], 'L1_attn_Wqkv': _L1_attn_in['Wqkv'], 'L1_attn_bqkv': _L1_attn_in['bqkv'], 'L1_ffn_ln1_w': _L1_ffn_in['ln1_w'], 'L1_ffn_ln2_w': _L1_ffn_in['ln2_w'], 'L1_ffn_wq': _L1_ffn_in['wq'], 'L1_ffn_wk': _L1_ffn_in['wk'], 'L1_ffn_wv': _L1_ffn_in['wv'], 'L1_ffn_wo': _L1_ffn_in['wo'], 'L1_ffn_router_w': _L1_ffn_in['router_w'], 'L1_ffn_w1': _L1_ffn_in['w1'], 'L1_ffn_w2': _L1_ffn_in['w2'], 'L1_ffn_w3': _L1_ffn_in['w3']}

def reference(x, L0_tok_conv1_w, L0_tok_conv1_b, L0_tok_bn_gamma, L0_tok_bn_beta, L0_tok_bn_mean, L0_tok_bn_var, L0_tok_conv2_w, L0_tok_conv2_b, L0_attn_Wq, L0_attn_bq, L0_attn_Wk, L0_attn_bk, L0_attn_Wv, L0_attn_bv, L0_attn_beta, L0_ffn_Wr, L0_ffn_W1s, L0_ffn_b1s, L0_ffn_W2s, L0_ffn_b2s, L0_ffn_W1p, L0_ffn_b1p, L0_ffn_W2p, L0_ffn_b2p, L1_attn_Wqkv, L1_attn_bqkv, L1_ffn_ln1_w, L1_ffn_ln2_w, L1_ffn_wq, L1_ffn_wk, L1_ffn_wv, L1_ffn_wo, L1_ffn_router_w, L1_ffn_w1, L1_ffn_w2, L1_ffn_w3):
    import jax
    import jax.numpy as jnp

    def _L0_tok_ref(x, conv1_w, conv1_b, bn_gamma, bn_beta, bn_mean, bn_var, conv2_w, conv2_b):
        import jax, jax.numpy as jnp
        import numpy as np
        K = 3
        PAD = (K - 1) // 2
        BN_EPS = 1e-05

        def _unfold(x):
            b, c, h, w = x.shape
            xp = jnp.pad(x, ((0, 0), (0, 0), (PAD, PAD), (PAD, PAD)))
            shifts = [xp[:, :, i:i + h, j:j + w] for i in range(K) for j in range(K)]
            return jnp.stack(shifts, axis=2)
        b, c, h, w = x.shape
        y = jnp.einsum('oc,bchw->bohw', conv1_w, x) + conv1_b[None, :, None, None]
        y = (y - bn_mean[None, :, None, None]) * (bn_gamma[None, :, None, None] * jax.lax.rsqrt(bn_var + BN_EPS)[None, :, None, None]) + bn_beta[None, :, None, None]
        y = jax.nn.relu(y)
        wdyn = jnp.einsum('ok,bkhw->bohw', conv2_w, y) + conv2_b[None, :, None, None]
        patches = _unfold(x)
        out = jnp.einsum('bckhw,bkhw->bchw', patches, wdyn)
        return out.reshape(b, h * w, c)

    def _L0_attn_ref(x, Wq, bq, Wk, bk, Wv, bv, beta):
        import jax, jax.numpy as jnp
        import numpy as np
        import math
        EMBED_DIM = 64
        SEQ_LEN = 1024
        BATCH = 4
        NUM_SCALES = (24.0, 720.0)
        d = x.shape[-1]
        seq_len = x.shape[1]
        sqrt_d = jnp.asarray(math.sqrt(d), x.dtype)
        Q = jnp.einsum('bsd,ed->bse', x, Wq) + bq
        K = jnp.einsum('bsd,ed->bse', x, Wk) + bk
        V = jnp.einsum('bsd,ed->bse', x, Wv) + bv
        attn = jnp.einsum('bse,bte->bst', Q, K) / sqrt_d
        idx = jnp.arange(seq_len, dtype=jnp.float32)
        absdiff = jnp.abs(idx[:, None] - idx[None, :])
        two_pi = jnp.asarray(2.0 * math.pi, jnp.float32)
        bias = jnp.zeros((seq_len, seq_len), dtype=jnp.float32)
        for n, T in enumerate(NUM_SCALES):
            bias = bias + beta[n] * jnp.cos(two_pi * absdiff / T)
        scores = jax.nn.softmax(attn + bias[None, :, :], axis=-1)
        return jnp.einsum('bst,bte->bse', scores, V)

    def _L0_ffn_ref(x, Wr, W1s, b1s, W2s, b2s, W1p, b1p, W2p, b2p):
        import jax, jax.numpy as jnp
        import numpy as np
        B, S, D, F, E, K = (8, 512, 64, 256, 8, 2)
        gelu = lambda t: jax.nn.gelu(t, approximate=False)
        shared = gelu(x @ W1s + b1s) @ W2s + b2s
        rw = jax.nn.softmax(x @ Wr, axis=-1)
        topw, topi = jax.lax.top_k(rw, K)
        topw = topw / jnp.sum(topw, axis=-1, keepdims=True)
        mask = jnp.sum(jax.nn.one_hot(topi, E, dtype=topw.dtype) * topw[..., None], axis=-2)
        h = gelu(jnp.einsum('bsd,edf->bsef', x, W1p) + b1p)
        priv = jnp.einsum('bsef,efd->bsed', h, W2p) + b2p
        routed = jnp.einsum('bsed,bse->bsd', priv, mask)
        return shared + routed

    def _L1_attn_ref(x, Wqkv, bqkv):
        import jax, jax.numpy as jnp
        import numpy as np
        EMBED_DIM = 64
        SEQ_LEN = 1024
        BATCH = 8
        ALPHA = 0.99
        bs, sl, d = x.shape
        qkv = x @ Wqkv + bqkv
        q, k, v = jnp.split(qkv, 3, axis=-1)
        i = jnp.arange(sl, dtype=jnp.float32)
        M = jnp.where(i[:, None] >= i[None, :], jnp.power(jnp.float32(ALPHA), i[:, None] - i[None, :]), 0.0)
        scores = jnp.einsum('bqd,bkd->bqk', q, k) / jnp.sqrt(jnp.float32(d))
        out = jnp.einsum('bqk,bkd->bqd', scores * M, v)
        return out

    def _L1_ffn_ref(x, ln1_w, ln2_w, wq, wk, wv, wo, router_w, w1, w2, w3):
        import jax, jax.numpy as jnp
        import numpy as np
        B, T, C = (64, 96, 64)
        NH, NKV = (4, 2)
        HD = C // NH
        NREP = NH // NKV
        NE, TOPK = (8, 2)
        HID = int(8 / 3 * C)
        EPS_RMS = 1e-06

        def _rope_tables(t_len):
            inv_freq = 1.0 / 10000.0 ** (np.arange(0, HD, 2, dtype=np.float32) / HD)
            t = np.arange(t_len, dtype=np.float32)
            freqs = np.outer(t, inv_freq)
            emb = np.concatenate([freqs, freqs], axis=-1)
            return (jnp.asarray(np.cos(emb)), jnp.asarray(np.sin(emb)))

        def _rotate_half(x):
            h = x.shape[-1] // 2
            return jnp.concatenate([-x[..., h:], x[..., :h]], axis=-1)

        def _rmsnorm(v, w):
            return v * jax.lax.rsqrt(jnp.mean(v * v, axis=-1, keepdims=True) + EPS_RMS) * w
        Bx, Tx, Cx = x.shape
        h = _rmsnorm(x, ln1_w)
        q = (h @ wq.T).reshape(Bx, Tx, NH, HD).transpose(0, 2, 1, 3)
        k = (h @ wk.T).reshape(Bx, Tx, NKV, HD).transpose(0, 2, 1, 3)
        v = (h @ wv.T).reshape(Bx, Tx, NKV, HD).transpose(0, 2, 1, 3)
        cos, sin = _rope_tables(Tx)
        cos, sin = (cos[None, None], sin[None, None])
        q = q * cos + _rotate_half(q) * sin
        k = k * cos + _rotate_half(k) * sin
        k = jnp.repeat(k, NREP, axis=1)
        v = jnp.repeat(v, NREP, axis=1)
        scores = jnp.einsum('bhtd,bhsd->bhts', q, k) / jnp.sqrt(jnp.float32(HD))
        causal = jnp.tril(jnp.ones((Tx, Tx), dtype=bool))
        scores = jnp.where(causal[None, None], scores, jnp.float32(-1e+30))
        att = jax.nn.softmax(scores, axis=-1)
        y = jnp.einsum('bhts,bhsd->bhtd', att, v).transpose(0, 2, 1, 3).reshape(Bx, Tx, Cx)
        x = x + y @ wo.T
        flat = _rmsnorm(x, ln2_w).reshape(-1, Cx)
        probs = jax.nn.softmax(flat @ router_w.T, axis=-1)
        tp, ti = jax.lax.top_k(probs, TOPK)
        tp = tp / (jnp.sum(tp, axis=-1, keepdims=True) + 1e-09)
        weights = jnp.sum(tp[..., None] * jax.nn.one_hot(ti, NE, dtype=flat.dtype), axis=1)
        out = jnp.zeros_like(flat)
        for e in range(NE):
            hh = jax.nn.silu(flat @ w1[e].T) * (flat @ w3[e].T)
            out = out + weights[:, e:e + 1] * (hh @ w2[e].T)
        return x + out.reshape(Bx, Tx, Cx)
    h = _L0_tok_ref(x, L0_tok_conv1_w, L0_tok_conv1_b, L0_tok_bn_gamma, L0_tok_bn_beta, L0_tok_bn_mean, L0_tok_bn_var, L0_tok_conv2_w, L0_tok_conv2_b)
    h = h + _L0_attn_ref(_layernorm(h, axis=-1), L0_attn_Wq, L0_attn_bq, L0_attn_Wk, L0_attn_bk, L0_attn_Wv, L0_attn_bv, L0_attn_beta)
    h = h + _L0_ffn_ref(_layernorm(h, axis=-1), L0_ffn_Wr, L0_ffn_W1s, L0_ffn_b1s, L0_ffn_W2s, L0_ffn_b2s, L0_ffn_W1p, L0_ffn_b1p, L0_ffn_W2p, L0_ffn_b2p)
    h = h + _L1_attn_ref(_layernorm(h, axis=-1), L1_attn_Wqkv, L1_attn_bqkv)
    h = h + _L1_ffn_ref(_layernorm(h, axis=-1), L1_ffn_ln1_w, L1_ffn_ln2_w, L1_ffn_wq, L1_ffn_wk, L1_ffn_wv, L1_ffn_wo, L1_ffn_router_w, L1_ffn_w1, L1_ffn_w2, L1_ffn_w3)
    return h

_drawn_inputs = setup_inputs


def setup_inputs(seed=0):
    import zlib

    import numpy as np

    out = dict(_drawn_inputs(seed))
    spreads = {'L0_tok_conv1_b': (0.0, 0.1),
     'L0_tok_bn_gamma': (1.0, 0.2),
     'L0_tok_bn_beta': (0.0, 0.1),
     'L0_tok_bn_mean': (0.0, 0.1),
     'L0_tok_bn_var': (1.0, 0.2),
     'L0_tok_conv2_b': (0.0, 0.1),
     'L0_attn_beta': (1.0, 0.6),
     'L0_ffn_b1s': (0.0, 0.612),
     'L0_ffn_b2s': (0.0, 0.1),
     'L0_ffn_b1p': (0.0, 0.8),
     'L0_ffn_b2p': (0.0, 0.1),
     'L1_ffn_ln1_w': (1.0, 0.6),
     'L1_ffn_ln2_w': (1.0, 0.6)}
    factors = {'L0_attn_bq': 8.0,
     'L0_attn_Wk': 2.743,
     'L0_attn_bk': 8.0,
     'L0_ffn_W1p': 4.609,
     'L0_ffn_W2p': 3.703,
     'L1_ffn_wq': 8.0,
     'L1_ffn_wk': 8.0,
     'L1_ffn_wv': 8.0,
     'L1_ffn_wo': 8.0,
     'L1_ffn_router_w': 8.0,
     'L1_ffn_w1': 8.0,
     'L1_ffn_w2': 8.0,
     'L1_ffn_w3': 8.0}
    for name, (base, spread) in spreads.items():
        noise = np.random.default_rng([zlib.crc32(name.encode()), seed]).standard_normal(out[name].shape)
        drawn = base * np.exp(spread * noise) if base else spread * noise
        out[name] = jnp.asarray(drawn.astype(out[name].dtype))
    for name, factor in factors.items():
        out[name] = (out[name] * factor).astype(out[name].dtype)
    return out
```

```python
from contextlib import ExitStack

import numpy as np

import concourse.bass as bass
from concourse import mybir

ALU = mybir.AluOpType
ACT = mybir.ActivationFunctionType
F32 = mybir.dt.float32
BF16 = mybir.dt.bfloat16
AX = mybir.AxisListType

P = 128
B = 2
C = 64
S = 64
N = C * S
NT = N // P
T = B * NT
QB = 512
NQ = N // QB
SUB = QB // P
CR = 16
TAPS = 9
NE = 8
F0 = 256
F1 = 170
NH, NKV, HD = 4, 2, 16
ALPHA = float(np.float32(0.99))
NEG = -1e30


def stage_semaphores(nc, ctx, prefix):
    taken = []

    def zero():
        nc.clear_and_free_semaphores(taken)
        nc.all_engine_barrier()

    ctx.callback(zero)

    def sem(name):
        taken.append(nc.alloc_semaphore(prefix + name))
        return taken[-1]

    return sem


def involution_stage(nc, t, H):
    POOL_T = 10
    DVE_T = NT - POOL_T
    CH = B * N // QB
    with ExitStack() as ctx:
        sb = lambda n, s, d=F32: ctx.enter_context(nc.sbuf_tensor(n, s, d))
        ps = lambda n, s, d=F32: ctx.enter_context(nc.psum_tensor(n, s, d))
        sem = stage_semaphores(nc, ctx, "")
        rows = [sb(f"x_rows{i}", [P, B, NT, S + 2]) for i in range(3)]
        xc = sb("x_chan", [C, B * N // 2])
        w1 = sb("conv1", [C, CR])
        w2 = sb("conv2", [CR, TAPS])
        bn = sb("bn", [CR, 8])
        b2 = sb("conv2_bias", [TAPS, 1])
        y = sb("bottleneck", [CR, 2, QB])
        wd = sb("tap_weights", [TAPS, B, N])
        wdt = sb("tap_weights_tok", [P, B, TAPS, S])
        prod_v = sb("prod_v", [P, 2, B, DVE_T, S])
        prod_g = sb("prod_g", [P, 2, B, POOL_T, S])
        y_ps = [ps(f"y_ps{i}", [CR, QB]) for i in range(2)]
        wd_ps = [ps(f"wd_ps{i}", [TAPS, QB]) for i in range(2)]

        zeroed = sem("zeroed")
        rows_in = sem("rows_in")
        small_in = sem("small_in")
        xc_in = [sem("xc_in0"), sem("xc_in1")]
        bn_ready = sem("bn_ready")
        y_mm, y_ready, wd_mm, wd_ready = sem("y_mm"), sem("y_ready"), sem("wd_mm"), sem("wd_ready")
        wd_out, wdt_in = sem("wd_out"), sem("wdt_in")
        v_step, g_step = sem("inv_v_step"), sem("inv_g_step")
        half = CH // 2

        with nc.Block() as block:
            @block.sync
            def _(sp):
                sp.dma_start(w1[:, :], t["conv1T"]).then_inc(small_in, 16)
                sp.dma_start(w2[:, :], t["conv2T"]).then_inc(small_in, 16)
                sp.dma_start(bn[:, 0:5], t["bn"]).then_inc(small_in, 16)
                sp.dma_start(b2[:, :], t["conv2_b"]).then_inc(small_in, 16)
                sp.dma_start(xc[:, :], t["x_chan"][:, 0:N]).then_inc(xc_in[0], 16)
                sp.wait_ge(zeroed, 3)
                for i in range(3):
                    for half_p in range(2):
                        lo, hi = max(0, 1 - i), min(S, S + 1 - i)
                        src = t["x_rows"][half_p * S + lo + i - 1:half_p * S + hi + i - 1]
                        sp.dma_start(rows[i][half_p * S + lo:half_p * S + hi, :, :, 1:S + 1],
                                     src).then_inc(rows_in, 16)
                sp.wait_ge(y_mm, half)
                sp.dma_start(xc[:, :], t["x_chan"][:, N:2 * N]).then_inc(xc_in[1], 16)
                sp.wait_ge(wd_ready, CH)
                sp.dma_start(t["wd_dram"], wd[:, :, :].rearrange("k b n -> k (b n)")).then_inc(wd_out, 16)
                sp.wait_ge(wd_out, 16)
                for half_p in range(2):
                    for b in range(B):
                        sp.dma_start(wdt[half_p * S:(half_p + 1) * S, b, :, :],
                                     t["wd_dram"].rearrange("k (b h w) -> b h k w", b=B, h=S)[b])\
                          .then_inc(wdt_in, 16)

            @block.tensor
            def _(pe):
                pe.wait_ge(small_in, 64)
                for im in range(B):
                    pe.wait_ge(xc_in[im], 16)
                    for c in range(half):
                        n = im * half + c
                        if n >= 2:
                            pe.wait_ge(y_ready, n - 1)
                        pe.matmul(y_ps[n % 2][:, :], w1[:, :], xc[:, c * QB:(c + 1) * QB],
                                  start=True, stop=True).then_inc(y_mm, 1)
                        if n >= 2:
                            pe.wait_ge(wd_ready, n - 1)
                        pe.wait_ge(y_ready, n + 1)
                        pe.matmul(wd_ps[n % 2][:, :], w2[:, :], y[:, n % 2, :],
                                  start=True, stop=True).then_inc(wd_mm, 1)

            @block.scalar
            def _(act):
                act.wait_ge(bn_ready, 1)
                act.activation(bn[:, 6:7], bn[:, 5:6], ACT.Sqrt).then_inc(bn_ready, 1)
                act.wait_ge(bn_ready, 5)
                for n in range(CH):
                    act.wait_ge(y_mm, n + 1)
                    if n >= 2:
                        act.wait_ge(wd_mm, n - 1)
                    act.activation(y[:, n % 2, :], y_ps[n % 2][:, :], ACT.Relu, bias=bn[:, 7:8],
                                   scale=bn[:, 6:7]).then_inc(y_ready, 1)

            def taps(eng, step, prod, acc, t0, t1):
                n = 0
                for k in range(TAPS):
                    x = rows[k // 3][:, :, t0:t1, k % 3:k % 3 + S]
                    w = wdt[:, :, k:k + 1, :].broadcast_to([P, B, t1 - t0, S])
                    if k >= 3:
                        eng.wait_ge(step, n - 2)
                    eng.tensor_tensor(acc if k == 0 else prod[:, k % 2, :, :, :], x, w,
                                      ALU.mult).then_inc(step, 1)
                    n += 1
                    if k:
                        eng.wait_ge(step, n)
                        eng.tensor_tensor(acc, acc, prod[:, k % 2, :, :, :], ALU.add).then_inc(step, 1)
                        n += 1

            Hv = H[:, :, :].rearrange("p (b t) f -> p b t f", b=B)

            @block.gpsimd
            def _(pool):
                pool.wait_ge(rows_in, 96)
                pool.wait_ge(wdt_in, 64)
                taps(pool, g_step, prod_g, Hv[:, :, DVE_T:NT, :], DVE_T, NT)

            @block.vector
            def _(dve):
                for i in range(3):
                    dve.memset(rows[i][:, :, :, :], 0.0).then_inc(zeroed, 1)
                dve.wait_ge(small_in, 64)
                dve.tensor_scalar(bn[:, 5:6], bn[:, 4:5], 1e-5, None, ALU.add).then_inc(bn_ready, 1)
                dve.wait_ge(bn_ready, 2)
                dve.reciprocal(bn[:, 5:6], bn[:, 6:7]).then_inc(bn_ready, 1)
                dve.wait_ge(bn_ready, 3)
                dve.tensor_tensor(bn[:, 6:7], bn[:, 5:6], bn[:, 1:2], ALU.mult)
                dve.tensor_tensor(bn[:, 7:8], bn[:, 0:1], bn[:, 3:4], ALU.subtract).then_inc(bn_ready, 1)
                dve.wait_ge(bn_ready, 4)
                dve.scalar_tensor_tensor(out=bn[:, 7:8], in0=bn[:, 7:8], scalar=bn[:, 6:7], in1=bn[:, 2:3],
                                         op0=ALU.mult, op1=ALU.add).then_inc(bn_ready, 1)
                for n in range(CH):
                    dve.wait_ge(wd_mm, n + 1)
                    dve.tensor_scalar(wd[:, n // half, (n % half) * QB:(n % half + 1) * QB],
                                      wd_ps[n % 2][:, :], b2[:, 0:1], None, ALU.add).then_inc(wd_ready, 1)
                dve.wait_ge(rows_in, 96)
                dve.wait_ge(wdt_in, 64)
                taps(dve, v_step, prod_v, Hv[:, :, 0:DVE_T, :], 0, DVE_T)


def norm_stage(nc, name, H, XT, ident, centred, eps, gain=None, U=None, parts=None):
    turns = U is None
    G = 16
    NG = T // G
    with ExitStack() as ctx:
        sb = lambda n, s, d=F32: ctx.enter_context(nc.sbuf_tensor(name + n, s, d))
        sem = stage_semaphores(nc, ctx, name)
        xc = sb("centred", [P, 2, G, C])
        sq = sb("squares", [P, 2, G, C])
        st = sb("stats", [P, 4, 2, G])
        tr_ps = [ctx.enter_context(nc.psum_tensor(f"{name}tr_ps{i}", [C, G // 4, QB], F32)) for i in range(2)]
        v_step, sq_ready, sd_ready = sem("v_step"), sem("sq_ready"), sem("sd_ready")
        xn_ready, transposed, xt_ready = sem("xn_ready"), sem("transposed"), sem("xt_ready")
        var_ready, xc_ready = sem("var_ready"), sem("xc_ready")
        rest_ready, mid_ready, low_ready, copied = sem("rest_ready"), sem("mid_ready"), sem("low_ready"), sem("copied")
        rest = sb("rest", [C, G * P]) if parts else None
        tokens = lambda g: slice(g * G * P, (g + 1) * G * P)
        with nc.Block() as block:
            @block.vector
            def _(dve):
                n = 0
                for g in range(NG + 2 if parts else NG + 1):
                    k = g % 2
                    if g < NG:
                        x = H[:, g * G:(g + 1) * G, :]
                        if centred:
                            dve.tensor_reduce(st[:, 0, k, :], x, AX.X, ALU.add).then_inc(v_step, 1)
                            dve.wait_ge(v_step, n + 1)
                            dve.tensor_scalar(st[:, 0, k, :], st[:, 0, k, :], -1.0 / C, None,
                                              ALU.mult).then_inc(v_step, 1)
                            dve.wait_ge(v_step, n + 2)
                            n += 2
                            if g >= 2 and turns:
                                dve.wait_ge(transposed, g - 1)
                            dve.tensor_tensor(xc[:, k, :, :], x,
                                              st[:, 0, k, :].unsqueeze(2).broadcast_to([P, G, C]),
                                              ALU.add).then_inc(xc_ready, 1)
                    if 0 < g <= NG:
                        k = (g - 1) % 2
                        dve.wait_ge(sq_ready, g)
                        dve.tensor_reduce(st[:, 1, k, :], sq[:, k, :, :], AX.X, ALU.add).then_inc(v_step, 1)
                        dve.wait_ge(v_step, n + 1)
                        dve.tensor_scalar(st[:, 1, k, :], st[:, 1, k, :], 1.0 / C, eps, ALU.mult,
                                          ALU.add).then_inc(var_ready, 1)
                        dve.wait_ge(sd_ready, g)
                        dve.reciprocal(st[:, 3, k, :], st[:, 2, k, :]).then_inc(v_step, 1)
                        dve.wait_ge(v_step, n + 2)
                        n += 2
                        if centred:
                            dve.wait_ge(xc_ready, g)
                        elif g > 2:
                            dve.wait_ge(transposed, g - 2)
                        src = xc[:, k, :, :] if centred else H[:, (g - 1) * G:g * G, :]
                        dst = xc[:, k, :, :] if U is None else U[:, (g - 1) * G:g * G, :]
                        dve.tensor_tensor(dst, src,
                                          st[:, 3, k, :].unsqueeze(2).broadcast_to([P, G, C]),
                                          ALU.mult).then_inc(xn_ready, 1)
                    if parts and g >= 2:
                        mh, hl = parts
                        m = g - 2
                        dve.wait_ge(xt_ready, m + 1)
                        if m:
                            dve.wait_ge(low_ready, m)
                        dve.scalar_tensor_tensor(
                            out=rest[:, :], in0=tr_ps[m % 2][:, :, :].rearrange("c a q -> c (a q)"),
                            scalar=1.0 if gain is None else gain, in1=hl[0:C, tokens(m)],
                            op0=ALU.mult, op1=ALU.subtract).then_inc(rest_ready, 1)
                        dve.wait_ge(mid_ready, m + 1)
                        dve.tensor_tensor(hl[C:2 * C, tokens(m)], rest[:, :], mh[0:C, tokens(m)],
                                          ALU.subtract).then_inc(low_ready, 1)

            @block.scalar
            def _(act):
                def copy_out(g):
                    act.wait_ge(transposed, g + 1)
                    out = parts[1][0:C, tokens(g)] if parts else XT[:, tokens(g)]
                    src = tr_ps[g % 2][:, :, :].rearrange("c a q -> c (a q)")
                    if gain is None:
                        act.activation(out, src, ACT.Copy).then_inc(xt_ready, 1)
                    else:
                        act.activation(out, src, ACT.Copy, scale=gain).then_inc(xt_ready, 1)
                    if parts:
                        act.wait_ge(rest_ready, g + 1)
                        act.activation(parts[0][0:C, tokens(g)], rest[:, :], ACT.Copy).then_inc(mid_ready, 1)
                for g in range(NG + 1):
                    if g < NG:
                        if centred:
                            act.wait_ge(xc_ready, g + 1)
                        if g >= 2:
                            act.wait_ge(var_ready, g - 1)
                        src = xc[:, g % 2, :, :] if centred else H[:, g * G:(g + 1) * G, :]
                        act.activation(sq[:, g % 2, :, :], src, ACT.Square).then_inc(sq_ready, 1)
                        act.wait_ge(var_ready, g + 1)
                        act.activation(st[:, 2, g % 2, :], st[:, 1, g % 2, :], ACT.Sqrt).then_inc(sd_ready, 1)
                    if g > 0 and turns:
                        copy_out(g - 1)

            @block.tensor
            def _(pe):
                for g in range(NG if turns else 0):
                    pe.wait_ge(xn_ready, g + 1)
                    if g >= 2:
                        pe.wait_ge(rest_ready if parts else xt_ready, g - 1)
                    for i in range(G):
                        mm = pe.transpose(tr_ps[g % 2][:, i // 4, (i % 4) * P:(i % 4 + 1) * P],
                                          xc[:, g % 2, i, :], ident[:, :])
                    mm.then_inc(transposed, 1)

            if parts:
                @block.gpsimd
                def _(pool):
                    for g in range(NG):
                        pool.wait_ge(xt_ready, g + 1)
                        pool.tensor_copy(parts[0][C:2 * C, tokens(g)], parts[1][0:C, tokens(g)]).then_inc(copied, 1)



M_ROW = 96


class AttentionShape:

    def __init__(self, causal, heads):
        self.causal, self.heads = causal, heads
        self.rows = heads * SUB
        self.m_rows = 3 if causal else 1
        self.halves = 2 if causal else 1
        self.sum_rows = 32 if causal else C + 1
        self.sums_all = heads * self.sum_rows
        self.max_tiles = [self._max_tiles(q) for q in range(NQ)]
        self.units = [self._units(q) for q in range(NQ)]
        first = lambda lists: np.concatenate([[0], np.cumsum([len(x) for x in lists])]).tolist()
        self.max_first, self.unit_first = first(self.max_tiles), first(self.units)
        self.max_all, self.unit_all = self.max_first[-1], self.unit_first[-1]
        self.steps = [s for q in range(-1, NQ) for s in self._phase(q)]
        self.steps += [("f", NQ - 1, s) for s in range(SUB)]

    def _max_tiles(self, q):
        out = []
        for h in range(self.heads):
            for s in range(SUB):
                for c in range(self.chunks(q)):
                    diagonal = self.causal and c == q
                    out.append((h, s, c, (s + 1) * P if diagonal else QB, diagonal))
        return out

    def _units(self, q):
        if not self.causal:
            return [(((0, 2 * u), (0, 2 * u + 1)), 0, False) for u in range(NT // 2)]
        return [(((2 * g, k), (2 * g + 1, k)), max(0, k - SUB * q) * P, k >= SUB * q)
                for k in range(SUB * (q + 1)) for g in range(NKV)]

    def chunks(self, q):
        return q + 1 if self.causal else NQ

    def kv(self, h):
        return h // 2 if self.causal else 0

    def _phase(self, q):
        tiles = len(self.max_tiles[q + 1]) if q + 1 < NQ else 0
        if q < 0:
            return [("m", 0, i) for i in range(tiles)] + [("n", 0, 0)]
        units = len(self.units[q])
        steps, m = [], 0
        for u in range(units):
            steps.append(("u", q, u))
            while m < tiles and m * (units - 1) < tiles * (u + 1):
                steps.append(("m", q + 1, m))
                m += 1
            if q > 0 and 1 <= u <= SUB:
                steps.append(("f", q - 1, u - 1))
            if u == units - 1 and tiles:
                steps.append(("n", q + 1, 0))
            if u >= 1:
                steps.append(("p", q, u - 1))
        return steps + [("p", q, units - 1), ("o", q, 0)]


def attention_core(nc, ctx, name, sh, H, ident, identb, QT, KT, V, mask, fin_rhs):
    sb = lambda n, s, d=F32: ctx.enter_context(nc.sbuf_tensor(name + n, s, d))
    ps = lambda n, s, d=F32: ctx.enter_context(nc.psum_tensor(name + n, s, d))
    sem = stage_semaphores(nc, ctx, name + "core_")
    dt = QT.dtype
    heads, rows, halves, mr = sh.heads, sh.rows, sh.halves, sh.m_rows
    turn = ident if dt == F32 else identb
    per = rows // halves
    NP = 3
    k_exp = M_ROW + mr
    exp_ps = [ps(f"exp_ps{i}", [P, 2, QB]) for i in range(2)]
    max_ps = [ps(f"max_ps{i}", [P, QB]) for i in range(2)]
    o_ps = ps("o_ps", [P, QB])
    fin_ps = ps("fin_ps", [P, QB])
    probs = sb("probs", [P, NP, 2, QB])
    mx = sb("mx", [P, rows, NQ])
    nm = sb("nm", [P, 3, rows])
    nm_p = sb("nm_parts", [P, rows, mr], dt)
    sums = sb("sums", [P, QB])
    rec = sb("rec", [P, heads])
    scaled = sb("scaled", [P, heads, C])
    headsum = sb("headsum", [P, C])
    max_mm, max_read = sem("max_mm"), sem("max_read")
    exp_mm, exp_done, pv_mm = sem("exp_mm"), sem("exp_done"), sem("pv_mm")
    nm_ready, nm_turned, nm_rows = sem("nm_ready"), sem("nm_turned"), sem("nm_rows")
    o_copied, fin_mm, fin_read, v_step = sem("o_copied"), sem("fin_mm"), sem("fin_read"), sem("v_step")
    v_image = NQ * ((5 if mr > 1 else 0) + SUB * (3 if heads > 1 else 1))
    turned = fin_ps[0:mr, :] if dt == F32 else fin_ps[0:mr, :].bitcast(BF16)

    def tensor(pe, im):
        for step, q, i in sh.steps:
            if step == "m":
                h, s, c, keys, diagonal = sh.max_tiles[q][i]
                n = sh.max_first[q] + i
                q0 = q * QB + s * P
                if n >= 2:
                    pe.wait_ge(max_read, im * sh.max_all + n - 1)
                mm = pe.matmul(max_ps[n % 2][:, 0:keys], QT[0:M_ROW, h, q0:q0 + P],
                               KT[0:M_ROW, sh.kv(h), c * QB:c * QB + keys], start=True, stop=not diagonal)
                if diagonal:
                    mm = pe.matmul(max_ps[n % 2][:, keys - P:keys], identb[:, :], mask[:, 0, :],
                                   start=False, stop=True)
                mm.then_inc(max_mm, 1)
            elif step == "u":
                pair, c0, diagonal = sh.units[q][i]
                n = sh.unit_first[q] + i
                if i == 0:
                    pe.wait_ge(nm_rows, (im * NQ + q + 1) * halves)
                if n >= 2:
                    pe.wait_ge(exp_done, im * sh.unit_all + n - 1)
                for j, (h, k) in enumerate(pair):
                    mm = pe.matmul(exp_ps[n % 2][:, j, c0:QB], KT[0:k_exp, sh.kv(h), k * P:(k + 1) * P],
                                   QT[0:k_exp, h, q * QB + c0:(q + 1) * QB], start=True, stop=not diagonal)
                    if diagonal:
                        mm = pe.matmul(exp_ps[n % 2][:, j, c0:c0 + P], identb[:, :], mask[:, 1, :],
                                       start=False, stop=True)
                mm.then_inc(exp_mm, 1)
            elif step == "p":
                pair, c0, _ = sh.units[q][i]
                n = sh.unit_first[q] + i
                pe.wait_ge(exp_done, im * sh.unit_all + n + 1)
                if i == 0 and q > 0:
                    pe.wait_ge(o_copied, im * NQ + q)
                for j, (h, k) in enumerate(pair):
                    last = i >= len(sh.units[q]) - (NKV if sh.causal else 1) and (sh.causal or j == 1)
                    mm = pe.matmul(o_ps[32 * h:32 * h + sh.sum_rows, c0:QB], V[:, k, sh.kv(h), :],
                                   probs[:, n % NP, j, c0:QB], start=(k == 0), stop=last)
                mm.then_inc(pv_mm, 1)
            elif step == "n":
                pe.wait_ge(nm_ready, im * NQ + q + 1)
                if q > 1:
                    pe.wait_ge(fin_read, (im * NQ + q - 1) * SUB)
                for r in range(halves):
                    if r:
                        pe.wait_ge(nm_rows, (im * NQ + q) * halves + r)
                    for k in range(per):
                        mm = pe.transpose(turned[:, k * P:(k + 1) * P], nm_p[:, r * per + k, :], turn[:, :])
                    mm.then_inc(nm_turned, 1)
            elif step == "f":
                if i == 0:
                    pe.wait_ge(o_copied, im * NQ + q + 1)
                if i or q:
                    pe.wait_ge(fin_read, (im * NQ + q) * SUB + i)
                pe.matmul(fin_ps[:, 0:heads * (C + 1)], sums[0:sh.sums_all, i * P:(i + 1) * P], fin_rhs,
                          start=True, stop=True).then_inc(fin_mm, 1)

    def scalar(act, im):
        for step, q, i in sh.steps:
            if step == "u":
                c0 = sh.units[q][i][1]
                n = sh.unit_first[q] + i
                act.wait_ge(exp_mm, im * sh.unit_all + n + 1)
                if n >= NP:
                    act.wait_ge(pv_mm, im * sh.unit_all + n - NP + 1)
                act.activation(probs[:, n % NP, :, c0:QB], exp_ps[n % 2][:, :, c0:QB],
                               ACT.Exp).then_inc(exp_done, 1)
            elif step == "o":
                act.wait_ge(pv_mm, im * sh.unit_all + sh.unit_first[q + 1])
                if q:
                    act.wait_ge(fin_mm, (im * NQ + q) * SUB)
                act.activation(sums[0:sh.sums_all, :], o_ps[0:sh.sums_all, :], ACT.Copy).then_inc(o_copied, 1)

    def vector(dve, im):
        own = 0

        def own_step(ins):
            nonlocal own
            ins.then_inc(v_step, 1)
            own += 1
            dve.wait_ge(v_step, im * v_image + own)

        for step, q, i in sh.steps:
            if step == "m":
                h, s, c, keys, _ = sh.max_tiles[q][i]
                n = sh.max_first[q] + i
                dve.wait_ge(max_mm, im * sh.max_all + n + 1)
                dve.tensor_reduce(mx[:, h * SUB + s, c:c + 1], max_ps[n % 2][:, 0:keys], AX.X,
                                  ALU.max).then_inc(max_read, 1)
            elif step == "n":
                dve.wait_ge(max_read, im * sh.max_all + sh.max_first[q + 1])
                tiles = mx[:, :, 0:sh.chunks(q)]
                if mr == 1:
                    dve.tensor_reduce(nm_p[:, :, 0], tiles, AX.X, ALU.max, negate=True).then_inc(nm_ready, 1)
                else:
                    own_step(dve.tensor_reduce(nm[:, 0, :], tiles, AX.X, ALU.max, negate=True))
                    own_step(dve.tensor_copy(nm_p[:, :, 0], nm[:, 0, :]))
                    own_step(dve.tensor_tensor(nm[:, 1, :], nm[:, 0, :], nm_p[:, :, 0], ALU.subtract))
                    own_step(dve.tensor_copy(nm_p[:, :, 1], nm[:, 1, :]))
                    own_step(dve.tensor_tensor(nm[:, 2, :], nm[:, 1, :], nm_p[:, :, 1], ALU.subtract))
                    dve.tensor_copy(nm_p[:, :, 2], nm[:, 2, :]).then_inc(nm_ready, 1)
                for r in range(halves):
                    dve.wait_ge(nm_turned, (im * NQ + q) * halves + r + 1)
                    hs = slice(r * heads // halves, (r + 1) * heads // halves)
                    dve.tensor_copy(QT[M_ROW:M_ROW + mr, hs, q * QB:(q + 1) * QB],
                                    turned[:, 0:per * P].rearrange("m (h t) -> m h t", t=QB)
                                    ).then_inc(nm_rows, 1)
            elif step == "f":
                dve.wait_ge(fin_mm, (im * NQ + q) * SUB + i + 1)
                fin = fin_ps[:, 0:heads * (C + 1)].rearrange("p (h c) -> p h c", h=heads)
                h_tile = H[:, bass.ds(im * NT + (q * SUB + i), 1), :]
                own_step(dve.reciprocal(rec[:, :], fin[:, :, C]))
                if heads == 1:
                    dve.scalar_tensor_tensor(out=h_tile, in0=fin[:, :, 0:C], scalar=rec[:, 0:1], in1=h_tile,
                                             op0=ALU.mult, op1=ALU.add).then_inc(fin_read, 1)
                else:
                    dve.tensor_tensor(scaled[:, :, :], fin[:, :, 0:C],
                                      rec[:, :].unsqueeze(2).broadcast_to([P, heads, C]),
                                      ALU.mult).then_inc(fin_read, 1)
                    dve.wait_ge(fin_read, (im * NQ + q) * SUB + i + 1)
                    own_step(dve.tensor_reduce(headsum[:, :], scaled[:, :, :].rearrange("p h c -> p c h"),
                                               AX.X, ALU.add))
                    own_step(dve.tensor_tensor(h_tile, h_tile, headsum[:, :].unsqueeze(1), ALU.add))
        assert own == v_image

    return tensor, scalar, vector, exp_ps, max_ps


def attention0_stage(nc, t, H, XT, ident, identb):
    sh = AttentionShape(causal=False, heads=1)
    with ExitStack() as ctx:
        sb = lambda n, s, d=F32: ctx.enter_context(nc.sbuf_tensor("at0_" + n, s, d))
        sem = stage_semaphores(nc, ctx, "at0_")
        QT, KT = sb("QT", [P, 1, N]), sb("KT", [P, 1, N])
        V = sb("V", [P, NT, 1, C + 1])
        xb = sb("x_image", [C, N])
        w = sb("wqkv", [C, 3 * C])
        bias = sb("bias", [C, 2])
        beta = sb("beta", [P, 1])
        bv = sb("bias_v", [P, C])
        tensor, scalar, vector, exp_ps, max_ps = attention_core(
            nc, ctx, "at0_", sh, H, ident, identb, QT, KT, V, None, ident[0:C + 1, 0:C + 1])
        w_in, x_in, zeroed, table_in = sem("w_in"), sem("x_in"), sem("zeroed"), sem("table_in")
        qk_mm, k_ready, q_ready, v_mm, v_ready = (sem("qk_mm"), sem("k_ready"), sem("q_ready"),
                                                  sem("v_mm"), sem("v_ready"))
        beta_ready = sem("beta_ready")
        VG = NT // 8
        with nc.Block() as block:
            @block.sync
            def _(sp):
                for im in range(B):
                    if im:
                        sp.wait_ge(v_mm, im * VG)
                    sp.dma_start(xb[:, :], XT[:, im * N:(im + 1) * N]).then_inc(x_in, 16)
                    if im == 0:
                        sp.dma_start(w[:, :], t["at0_w"]).then_inc(w_in, 16)
                        sp.dma_start(bias[:, :], t["at0_b"]).then_inc(w_in, 16)
                        sp.dma_start(beta[C:C + 4, :], t["at0_beta"]).then_inc(w_in, 16)
                        sp.dma_start(bv[:, :], t["at0_bv"].broadcast_to([P, C])).then_inc(w_in, 16)
                        sp.wait_ge(zeroed, 2)
                        sp.dma_start(QT[C:C + 4, 0, :], t["at0_table"]).then_inc(table_in, 16)
                        sp.dma_start(KT[C:C + 4, 0, :], t["at0_table"]).then_inc(table_in, 16)

            @block.gpsimd
            def _(pool):
                pool.memset(QT[C:M_ROW, 0, :], 0.0).then_inc(zeroed, 1)
                pool.wait_ge(zeroed, 1)
                pool.memset(KT[C:M_ROW, 0, :], 0.0).then_inc(zeroed, 1)
                pool.wait_ge(zeroed, 2)
                pool.memset(KT[M_ROW:M_ROW + 1, 0, :], 1.0).then_inc(zeroed, 1)
                pool.wait_ge(zeroed, 3)
                pool.memset(V[:, :, :, C:C + 1], 1.0).then_inc(zeroed, 1)

            @block.tensor
            def _(pe):
                pe.wait_ge(w_in, 64)
                pe.wait_ge(zeroed, 4)
                pe.wait_ge(beta_ready, 1)
                with pe.Fori(0, B) as im:
                    pe.wait_ge(x_in, im * 16 + 16)
                    for c in range(NQ):
                        if c >= 2:
                            pe.wait_ge(k_ready, im * NQ + c - 1)
                            pe.wait_ge(q_ready, im * NQ + c - 1)
                        x = xb[:, c * QB:(c + 1) * QB]
                        pe.matmul(exp_ps[c % 2][:, 0, :], w[:, 0:2 * C], x, start=True,
                                  stop=True).then_inc(qk_mm, 1)
                    for g in range(VG):
                        if g >= 2:
                            pe.wait_ge(v_ready, im * VG + g - 1)
                        for k in range(8):
                            j = g * 8 + k
                            mm = pe.matmul(max_ps[g % 2][:, k * C:(k + 1) * C], xb[:, j * P:(j + 1) * P],
                                           w[:, 2 * C:3 * C], start=True, stop=True)
                        mm.then_inc(v_mm, 1)
                    pe.wait_ge(k_ready, im * NQ + NQ)
                    pe.wait_ge(q_ready, im * NQ + NQ)
                    pe.wait_ge(v_ready, im * VG + VG)
                    tensor(pe, im)

            @block.scalar
            def _(act):
                act.wait_ge(w_in, 64)
                with act.Fori(0, B) as im:
                    for c in range(NQ):
                        act.wait_ge(q_ready, im * NQ + c + 1)
                        act.activation(KT[0:C, 0, c * QB:(c + 1) * QB], exp_ps[c % 2][C:2 * C, 0, :],
                                       ACT.Identity, bias=bias[:, 1:2]).then_inc(k_ready, 1)
                    scalar(act, im)

            @block.vector
            def _(dve):
                dve.wait_ge(table_in, 32)
                dve.wait_ge(w_in, 64)
                dve.tensor_scalar(QT[C:C + 4, 0, :], QT[C:C + 4, 0, :], beta[C:C + 4, 0:1], None,
                                  ALU.mult).then_inc(beta_ready, 1)
                with dve.Fori(0, B) as im:
                    for c in range(NQ):
                        dve.wait_ge(qk_mm, im * NQ + c + 1)
                        dve.tensor_scalar(QT[0:C, 0, c * QB:(c + 1) * QB], exp_ps[c % 2][0:C, 0, :],
                                          bias[:, 0:1], C ** -0.5, ALU.add, ALU.mult).then_inc(q_ready, 1)
                    for g in range(VG):
                        dve.wait_ge(v_mm, im * VG + g + 1)
                        dve.tensor_tensor(V[:, g * 8:(g + 1) * 8, 0, 0:C],
                                          max_ps[g % 2][:, :].rearrange("p (k c) -> p k c", c=C),
                                          bv[:, :].unsqueeze(1).broadcast_to([P, 8, C]),
                                          ALU.add).then_inc(v_ready, 1)
                    vector(dve, im)




def attention1_stage(nc, t, U, XT, ident, identb):
    sh = AttentionShape(causal=True, heads=NH)
    HQK = NH + NKV
    GT = 16
    NG = NT // GT
    with ExitStack() as ctx:
        sb = lambda n, s, d=F32: ctx.enter_context(nc.sbuf_tensor("at1_" + n, s, d))
        sem = stage_semaphores(nc, ctx, "at1_")
        QT, KT = sb("QT", [P, NH, N], BF16), sb("KT", [P, NKV, N], BF16)
        V = sb("V", [P, NT, NKV, 32])
        xb = sb("x_image", [C, GT * P])
        w = sb("wqkv", [C, P])
        wo = sb("wo", [P, NH * (C + 1)])
        mask = sb("mask", [P, 2, P], BF16)
        cos, sin = sb("cos", [P, NT, HD // 2]), sb("sin", [P, NT, HD // 2])
        qk = sb("qk", [P, GT, HQK, HD])
        rot = sb("rot", [P, GT, HQK, HD])
        tmp = sb("tmp", [P, GT, HQK, HD // 2])
        part = sb("parts", [P, 3, GT, HQK, HD], BF16)
        QA, KA = sb("QA", [P, GT, NH, 6, HD], BF16), sb("KA", [P, GT, NKV, 6, HD], BF16)
        tensor, scalar, vector, exp_ps, max_ps = attention_core(
            nc, ctx, "at1_", sh, U, ident, identb, QT, KT, V, mask, wo[:, :])
        w_in, x_in, filled = sem("w_in"), sem("x_in"), sem("filled")
        qkv_mm, qk_ready, v_ready, rope = sem("qkv_mm"), sem("qk_ready"), sem("v_ready"), sem("rope")
        parts_ready, qa_ready, ka_ready = sem("parts_ready"), sem("qa_ready"), sem("ka_ready")
        turned, q_out, k_out = sem("turned"), sem("q_out"), sem("k_out")
        CG = GT // SUB
        ROPE_STEPS = 6 + 4
        loads = [(w[:, :], t["at1_w"]), (wo[:, :], t["at1_wo"]), (cos[:, :, :], t["at1_cos"]),
                 (sin[:, :, :], t["at1_sin"]), (mask[:, :, :], t["causal_mask"])]
        q_slots, k_slots = ((0, 1, 4), (2, 3), (5,)), ((0, 2, 5), (1, 3), (4,))

        def spread(copy, slots, dst, src_heads, done):
            for p, slots_of_part in enumerate(slots):
                for s in slots_of_part:
                    ins = copy(dst[:, :, :, s, :], part[:, p, :, src_heads, :])
            ins.then_inc(done, 1)

        with nc.Block() as block:
            @block.sync
            def _(sp):
                for n in range(B * NG):
                    if n:
                        sp.wait_ge(qkv_mm, n * CG)
                    sp.dma_start(xb[:, :], XT[:, n * GT * P:(n + 1) * GT * P]).then_inc(x_in, 16)
                    if n == 0:
                        for dst, src in loads:
                            sp.dma_start(dst, src).then_inc(w_in, 16)

            @block.gpsimd
            def _(pool):
                pool.memset(V[:, :, :, HD:32], 0.0).then_inc(filled, 1)
                pool.wait_ge(filled, 1)
                pool.memset(V[:, :, :, HD:HD + 1], 1.0).then_inc(filled, 1)
                pool.wait_ge(filled, 2)
                pool.memset(KT[M_ROW:M_ROW + sh.m_rows, :, :], 1.0).then_inc(filled, 1)

            @block.tensor
            def _(pe):
                pe.wait_ge(w_in, 16 * len(loads))
                pe.wait_ge(filled, 3)
                with pe.Fori(0, B) as im:
                    for g in range(NG):
                        pe.wait_ge(x_in, (im * NG + g) * 16 + 16)
                        for c in range(CG):
                            if c >= 2:
                                n = im * NG * CG + (g * CG + c - 1)
                                pe.wait_ge(qk_ready, n)
                                pe.wait_ge(v_ready, n)
                            for i in range(SUB):
                                k = c * SUB + i
                                mm = pe.matmul(max_ps[c % 2][:, i * P:(i + 1) * P], xb[:, k * P:(k + 1) * P],
                                               w[:, :], start=True, stop=True)
                            mm.then_inc(qkv_mm, 1)
                        pe.wait_ge(qa_ready, im * NG + g + 1)
                        pe.wait_ge(ka_ready, im * NG + g + 1)
                        for c in range(CG):
                            n = im * NG * CG + (g * CG + c)
                            if c:
                                pe.wait_ge(q_out, n)
                            dst = exp_ps[0][:, :, :].rearrange("p a q -> p (a q)").bitcast(BF16)
                            for h in range(NH):
                                for i in range(SUB):
                                    mm = pe.transpose(dst[0:M_ROW, (h * SUB + i) * P:(h * SUB + i + 1) * P],
                                                      QA[:, c * SUB + i, h, :, :].rearrange("p s d -> p (s d)"),
                                                      identb[:, :])
                            mm.then_inc(turned, 1)
                            if c:
                                pe.wait_ge(k_out, n)
                            dst = exp_ps[1][:, 0, :].bitcast(BF16)
                            for h in range(NKV):
                                for i in range(SUB):
                                    mm = pe.transpose(dst[0:M_ROW, (h * SUB + i) * P:(h * SUB + i + 1) * P],
                                                      KA[:, c * SUB + i, h, :, :].rearrange("p s d -> p (s d)"),
                                                      identb[:, :])
                            mm.then_inc(turned, 1)
                    pe.wait_ge(q_out, im * NG * CG + NG * CG)
                    pe.wait_ge(k_out, im * NG * CG + NG * CG)
                    pe.wait_ge(v_ready, im * NG * CG + NG * CG)
                    tensor(pe, im)

            @block.scalar
            def _(act):
                with act.Fori(0, B) as im:
                    for g in range(NG):
                        for c in range(CG):
                            act.wait_ge(qkv_mm, im * NG * CG + (g * CG + c + 1))
                            src = max_ps[c % 2][:, :].rearrange("p (i h d) -> p i h d", i=SUB, d=HD)
                            tiles = slice(c * SUB, (c + 1) * SUB)
                            if c == 0 and g:
                                act.wait_ge(parts_ready, im * NG + g)
                            act.activation(qk[:, tiles, 0:NH, :], src[:, :, 0:NH, :], ACT.Copy, scale=HD ** -0.5)
                            act.activation(qk[:, tiles, NH:HQK, :], src[:, :, NH:HQK, :],
                                           ACT.Copy).then_inc(qk_ready, 1)
                            act.activation(V[:, g * GT + c * SUB:g * GT + (c + 1) * SUB, :, 0:HD],
                                           src[:, :, HQK:HQK + NKV, :], ACT.Copy).then_inc(v_ready, 1)
                        act.wait_ge(parts_ready, im * NG + g + 1)
                        if g:
                            act.wait_ge(turned, (im * NG + g) * 2 * CG)
                        spread(lambda o, i: act.activation(o, i, ACT.Copy), q_slots, QA, slice(0, NH), qa_ready)
                        for c in range(CG):
                            n = im * NG * CG + (g * CG + c)
                            act.wait_ge(turned, n * 2 + 1)
                            q0 = (g * CG + c) * QB
                            act.activation(QT[0:M_ROW, :, q0:q0 + QB],
                                           exp_ps[0][0:M_ROW, :, :].rearrange("p a q -> p (a q)").bitcast(BF16)
                                           .rearrange("p (h q) -> p h q", h=NH), ACT.Copy).then_inc(q_out, 1)
                    scalar(act, im)

            @block.vector
            def _(dve):
                dve.wait_ge(w_in, 16 * len(loads))
                half = HD // 2
                with dve.Fori(0, B) as im:
                    for g in range(NG):
                        dve.wait_ge(qk_ready, im * NG * CG + (g + 1) * CG)
                        tiles = slice(g * GT, (g + 1) * GT)
                        table = lambda x: x[:, tiles, :].unsqueeze(2).broadcast_to([P, GT, HQK, half])
                        lo, hi = qk[:, :, :, 0:half], qk[:, :, :, half:HD]
                        rlo, rhi = rot[:, :, :, 0:half], rot[:, :, :, half:HD]
                        own = 0

                        def step(ins):
                            nonlocal own
                            ins.then_inc(rope, 1)
                            own += 1
                            dve.wait_ge(rope, (im * NG + g) * ROPE_STEPS + own)

                        step(dve.tensor_tensor(rlo, lo, table(cos), ALU.mult))
                        step(dve.tensor_tensor(tmp[:, :, :, :], hi, table(sin), ALU.mult))
                        step(dve.tensor_tensor(rlo, rlo, tmp[:, :, :, :], ALU.subtract))
                        step(dve.tensor_tensor(rhi, hi, table(cos), ALU.mult))
                        step(dve.tensor_tensor(tmp[:, :, :, :], lo, table(sin), ALU.mult))
                        step(dve.tensor_tensor(rhi, rhi, tmp[:, :, :, :], ALU.add))
                        if g:
                            dve.wait_ge(qa_ready, im * NG + g)
                            dve.wait_ge(ka_ready, im * NG + g)
                        r = rot[:, :, :, :]
                        step(dve.tensor_copy(part[:, 0, :, :, :], r))
                        step(dve.tensor_tensor(r, r, part[:, 0, :, :, :], ALU.subtract))
                        step(dve.tensor_copy(part[:, 1, :, :, :], r))
                        step(dve.tensor_tensor(r, r, part[:, 1, :, :, :], ALU.subtract))
                        dve.tensor_copy(part[:, 2, :, :, :], r).then_inc(parts_ready, 1)
                        dve.wait_ge(parts_ready, im * NG + g + 1)
                        if g:
                            dve.wait_ge(turned, (im * NG + g) * 2 * CG)
                        spread(dve.tensor_copy, k_slots, KA, slice(NH, HQK), ka_ready)
                        for c in range(CG):
                            n = im * NG * CG + (g * CG + c)
                            dve.wait_ge(turned, n * 2 + 2)
                            q0 = (g * CG + c) * QB
                            dve.tensor_copy(KT[0:M_ROW, :, q0:q0 + QB],
                                            exp_ps[1][0:M_ROW, 0, :].bitcast(BF16)
                                            .rearrange("p (h q) -> p h q", h=NKV)).then_inc(k_out, 1)
                    vector(dve, im)


def split_weights_stage(nc, name, sets):
    with ExitStack() as ctx:
        sem = stage_semaphores(nc, ctx, name)
        most = max(src.shape[1] for src, _ in sets)
        src_sb = ctx.enter_context(nc.sbuf_tensor(name + "w_whole", [C, len(sets), most], F32))
        rest = ctx.enter_context(nc.sbuf_tensor(name + "w_rest", [C, len(sets), most], F32))
        loaded = [sem(f"w_loaded{n}") for n in range(len(sets))]
        high, left, middle, low, copied = sem("w_high"), sem("w_left"), sem("w_middle"), sem("w_low"), sem("w_copied")
        with nc.Block() as block:
            @block.sync
            def _(sp):
                for n, (src, _) in enumerate(sets):
                    sp.dma_start(src_sb[:, n, 0:src.shape[1]], src).then_inc(loaded[n], 16)

            @block.scalar
            def _(act):
                for n, (src, (hh, mm, lh)) in enumerate(sets):
                    k = src.shape[1]
                    act.wait_ge(loaded[n], 16)
                    act.activation(hh[0:C, 0:k], src_sb[:, n, 0:k], ACT.Copy).then_inc(high, 1)
                    act.wait_ge(left, n + 1)
                    act.activation(mm[0:C, 0:k], rest[:, n, 0:k], ACT.Copy).then_inc(middle, 1)

            @block.vector
            def _(dve):
                for n, (src, (hh, mm, lh)) in enumerate(sets):
                    k = src.shape[1]
                    dve.wait_ge(high, n + 1)
                    dve.tensor_tensor(rest[:, n, 0:k], src_sb[:, n, 0:k], hh[0:C, 0:k],
                                      ALU.subtract).then_inc(left, 1)
                    dve.wait_ge(middle, n + 1)
                    dve.tensor_tensor(lh[0:C, 0:k], rest[:, n, 0:k], mm[0:C, 0:k],
                                      ALU.subtract).then_inc(low, 1)

            @block.gpsimd
            def _(pool):
                done = 0
                for n, (src, (hh, mm, lh)) in enumerate(sets):
                    k = src.shape[1]
                    pool.wait_ge(high, n + 1)
                    pool.tensor_copy(hh[C:2 * C, 0:k], hh[0:C, 0:k]).then_inc(copied, 1)
                    pool.wait_ge(copied, done + 1)
                    pool.tensor_copy(lh[C:2 * C, 0:k], hh[0:C, 0:k]).then_inc(copied, 1)
                    pool.wait_ge(copied, done + 2)
                    pool.wait_ge(middle, n + 1)
                    pool.tensor_copy(mm[C:2 * C, 0:k], mm[0:C, 0:k]).then_inc(copied, 1)
                    pool.wait_ge(copied, done + 3)
                    done += 3


def moe_stage(nc, name, t, H, parts, ident, width, shared, gated, denom_eps):
    E = NE + shared
    NB = T * P // QB
    HT = 2 * E
    UP, HB = (2, 6) if gated else (3, 6)
    if gated:
        HB = 4
    with ExitStack() as ctx:
        sb = lambda n, s, d=F32: ctx.enter_context(nc.sbuf_tensor(name + n, s, d))
        ps = lambda n, s, d=F32: ctx.enter_context(nc.psum_tensor(name + n, s, d))
        sem = stage_semaphores(nc, ctx, name)
        meets = (0, 0, 1)
        wr = [sb(f"router{i}", [P, NE], BF16) for i in range(3)]
        w1 = [sb(f"w1_{i}", [P, HT * width], BF16) for i in range(3)]
        w3 = [sb(f"w3_{i}", [P, HT * width], BF16) for i in range(3)] if gated else None
        w2 = sb("w2", [width, HT, C])
        b1 = sb("b1", [width, HT])
        b2 = sb("b2", [E, C])
        rank = sb("rank", [P, NE])
        gate = sb("gate", [P, T, E])
        g = {n: sb("g_" + n, [P, T, NE]) for n in ("p", "eq", "oh", "p2")}
        col = sb("cols", [P, 4, T])
        gate_t = sb("gate_t", [E, T * P]) if shared else None
        gate_b = sb("gate_b", [E, 2, QB]) if shared else None
        act_out = sb("act_out", [width, 2, QB]) if gated else None
        hid = sb("hidden", [width, HB, QB])
        weighted = sb("weighted", [P, NE, C])
        mixed = sb("mixed", [P, 2, C])
        if gated:
            up = [ps(f"up{i}", [width, 2, QB]) for i in range(UP)]
        else:
            up = [ps(f"up{i}", [width, 1, QB]) for i in range(UP)]
        down = [ps(f"down{i}", [P, NE, C]) for i in range(SUB)]
        sh_ps = ps("shared_ps", [P, SUB, C]) if shared else None
        w_in, logits_mm, gate_step, exp_ready = sem("w_in"), sem("logits_mm"), sem("gate_step"), sem("exp_ready")
        gate_turned, gate_out, gate_b_ready = sem("gate_turned"), sem("gate_out"), sem("gate_b_ready")
        up_mm, act_done, hid_ready = sem("up_mm"), sem("act_done"), sem("hid_ready")
        down_mm, down_done, down_read = sem("down_mm"), sem("down_done"), sem("down_read")
        sh_done, sh_read, v_step = sem("sh_done"), sem("sh_read"), sem("v_step")
        loads = [(w2[:, :, :], "w2"), (rank[:, :], None)]
        loads += [] if gated else [(b1[:, :], "b1"), (b2[:, :], "b2")]
        split_weights_stage(nc, name, [(t[name + "router"], wr), (t[name + "w1"], w1)]
                            + ([(t[name + "w3"], w3)] if gated else []))
        gate_steps = 22
        TURNS = T // SUB

        with nc.Block() as block:
            @block.sync
            def _(sp):
                for dst, src in loads:
                    sp.dma_start(dst, t[name + src] if src else t["rank"].broadcast_to([P, NE])).then_inc(w_in, 16)
                if shared:
                    sp.wait_ge(gate_out, TURNS)
                    with sp.Fori(0, NB) as nb:
                        sp.wait_ge(sh_done, nb + 1)
                        sp.dma_start(gate_b[:, 0, :], gate_t[:, bass.ds(nb * QB, QB)]).then_inc(gate_b_ready, 16)

            @block.tensor
            def _(pe):
                pe.wait_ge(w_in, 16 * len(loads))
                for j in range(T):
                    for i in range(3):
                        mm = pe.matmul(down[0][:, :, :].rearrange("p e c -> p (e c)")[:, j * NE:(j + 1) * NE],
                                       parts[meets[i]][:, j * P:(j + 1) * P], wr[i][:, :],
                                       start=(i == 0), stop=(i == 2))
                mm.then_inc(logits_mm, 1)
                pe.wait_ge(gate_step, gate_steps)
                if shared:
                    for n in range(TURNS):
                        if n >= 2:
                            pe.wait_ge(gate_out, n - 1)
                        for i in range(SUB):
                            mm = pe.transpose(up[n % 2][0:E, 0, i * P:(i + 1) * P],
                                              gate[:, n * SUB + i, :], ident[:, :])
                        mm.then_inc(gate_turned, 1)
                    pe.wait_ge(gate_out, TURNS)
                with pe.Fori(0, NB) as nb:
                    def down_products(e):
                        for f in range(2):
                            pe.wait_ge(hid_ready, nb * HT + 2 * e + f + 1)
                        if e == 0:
                            pe.wait_ge(down_read, nb * SUB + SUB)
                        if e == NE:
                            pe.wait_ge(gate_b_ready, nb * 16 + 16)
                            pe.wait_ge(sh_read, nb + 1)
                        for s in range(SUB):
                            for f in range(2):
                                k = 2 * e + f
                                out = sh_ps[:, s, :] if e == NE else down[s][:, e, :]
                                mm = pe.matmul(out, hid[:, k % HB, s * P:(s + 1) * P], w2[:, k, :],
                                               start=(f == 0), stop=(f == 1 and e < NE))
                            if e == NE:
                                mm = pe.matmul(out, gate_b[:, 0, s * P:(s + 1) * P], b2[:, :],
                                               start=False, stop=True)
                                if s == SUB - 1:
                                    mm.then_inc(sh_done, 1)
                            elif e == NE - 1:
                                mm.then_inc(down_done, 1)
                            elif s == SUB - 1:
                                mm.then_inc(down_mm, 1)

                    for e in range(E + 1):
                        if e < E:
                            for f in range(2):
                                k = 2 * e + f
                                if k >= UP:
                                    pe.wait_ge(hid_ready, nb * HT + k - UP + 1)
                                for a, w in enumerate([w1, w3] if gated else [w1]):
                                    for i in range(3):
                                        mm = pe.matmul(up[k % UP][:, a, :], w[i][:, k * width:(k + 1) * width],
                                                       parts[meets[i]][:, bass.ds(nb * QB, QB)],
                                                       start=(i == 0), stop=(i == 2))
                                mm.then_inc(up_mm, 1)
                        if e >= 1:
                            down_products(e - 1)

            def hidden_free(eng, nb, k):
                e = (k - HB) // 2
                if k >= HB:
                    eng.wait_ge(down_mm, nb * (NE - 1) + e + 1)

            @block.scalar
            def _(act):
                act.wait_ge(gate_step, 2)
                act.activation(g["p"][:, :, :], g["p"][:, :, :], ACT.Exp).then_inc(exp_ready, 1)
                if shared:
                    for n in range(TURNS):
                        act.wait_ge(gate_turned, n + 1)
                        act.activation(gate_t[:, n * QB:(n + 1) * QB], up[n % 2][0:E, 0, :],
                                       ACT.Copy).then_inc(gate_out, 1)
                with act.Fori(0, NB) as nb:
                    for k in range(HT):
                        act.wait_ge(up_mm, nb * HT + k + 1)
                        if gated:
                            if k >= 2:
                                act.wait_ge(hid_ready, nb * HT + k - 1)
                            act.activation(act_out[:, k % 2, :], up[k % UP][:, 0, :], ACT.Silu).then_inc(act_done, 1)
                        else:
                            hidden_free(act, nb, k)
                            act.activation(hid[:, k % HB, :], up[k % UP][:, 0, :], ACT.Gelu,
                                           bias=b1[:, k:k + 1]).then_inc(hid_ready, 1)

            @block.vector
            def _(dve):
                own = 0

                def step(ins):
                    nonlocal own
                    ins.then_inc(gate_step, 1)
                    own += 1
                    dve.wait_ge(gate_step, own)

                wide = lambda a: a.unsqueeze(2).broadcast_to([P, T, NE])
                p, eq, oh, p2 = (g[n][:, :, :] for n in ("p", "eq", "oh", "p2"))
                c = [col[:, i, :] for i in range(4)]
                ranks = rank[:, :].unsqueeze(1).broadcast_to([P, T, NE])
                dve.wait_ge(logits_mm, 1)
                logits = down[0][:, :, :].rearrange("p e c -> p (e c)").rearrange("p (t e) -> p t e", e=NE)
                step(dve.tensor_reduce(c[0], logits, AX.X, ALU.max))
                step(dve.tensor_tensor(p, logits, wide(c[0]), ALU.subtract))
                dve.wait_ge(exp_ready, 1)
                step(dve.tensor_reduce(c[0], p, AX.X, ALU.add))
                step(dve.reciprocal(c[1], c[0]))
                step(dve.tensor_tensor(p, p, wide(c[1]), ALU.mult))

                def first_max(src, largest):
                    step(dve.tensor_reduce(c[largest], src, AX.X, ALU.max))
                    step(dve.tensor_tensor(eq, src, wide(c[largest]), ALU.is_equal))
                    step(dve.tensor_tensor(eq, eq, ranks, ALU.mult))
                    step(dve.tensor_reduce(c[3], eq, AX.X, ALU.max))

                first_max(p, 0)
                step(dve.tensor_tensor(oh, eq, wide(c[3]), ALU.is_equal))
                step(dve.scalar_tensor_tensor(out=p2, in0=oh, scalar=-2.0, in1=p, op0=ALU.mult, op1=ALU.add))
                first_max(p2, 1)
                step(dve.tensor_tensor(eq, eq, wide(c[3]), ALU.is_equal))
                step(dve.tensor_tensor(oh, oh, eq, ALU.add))
                step(dve.tensor_tensor(c[2], c[0], c[1], ALU.add))
                if denom_eps:
                    step(dve.tensor_scalar(c[2], c[2], denom_eps, None, ALU.add))
                step(dve.reciprocal(c[3], c[2]))
                step(dve.tensor_tensor(p, p, wide(c[3]), ALU.mult))
                if shared:
                    step(dve.memset(gate[:, :, NE:E], 1.0))
                step(dve.tensor_tensor(gate[:, :, 0:NE], p, oh, ALU.mult))
                assert own == gate_steps, own

                def weigh(nb, s):
                    n = nb * SUB + s
                    tile = bass.ds(n, 1)
                    dve.wait_ge(down_done, n + 1)
                    dve.tensor_tensor(weighted[:, :, :], down[s][:, :, :],
                                      gate[:, tile, 0:NE].rearrange("p t e -> p (t e)").unsqueeze(2)
                                      .broadcast_to([P, NE, C]), ALU.mult).then_inc(down_read, 1)
                    dve.wait_ge(down_read, n + SUB + 1)
                    dve.tensor_reduce(mixed[:, 0, :], weighted[:, :, :].rearrange("p e c -> p c e"), AX.X,
                                      ALU.add).then_inc(v_step, 1)
                    k = 2 + shared
                    v_block = SUB * k - shared
                    dve.wait_ge(v_step, nb * v_block + s * k + 1)
                    if shared:
                        dve.wait_ge(sh_done, nb + 2)
                        ins = dve.tensor_tensor(mixed[:, 1, :], mixed[:, 0, :], sh_ps[:, s, :], ALU.add)
                        ins.then_inc(sh_read if s == SUB - 1 else v_step, 1)
                        if s == SUB - 1:
                            dve.wait_ge(sh_read, nb + 2)
                        else:
                            dve.wait_ge(v_step, nb * v_block + s * k + 2)
                    dve.tensor_tensor(H[:, tile, :], H[:, tile, :], mixed[:, shared:shared + 1, :],
                                      ALU.add).then_inc(v_step, 1)

                dve.sem_inc(down_read, SUB)
                if shared:
                    dve.sem_inc(sh_done, 1)
                    dve.sem_inc(sh_read, 1)
                with dve.Fori(0, NB) as nb:
                    if gated:
                        for k in range(HT):
                            dve.wait_ge(act_done, nb * HT + k + 1)
                            hidden_free(dve, nb, k)
                            dve.tensor_tensor(hid[:, k % HB, :], act_out[:, k % 2, :], up[k % UP][:, 1, :],
                                              ALU.mult).then_inc(hid_ready, 1)
                    for s in range(SUB):
                        weigh(nb, s)


def linear_attention_stage(nc, t, H, XT):
    NBL = 2 * NQ
    with ExitStack() as ctx:
        sb = lambda n, s, d=F32: ctx.enter_context(nc.sbuf_tensor("lin_" + n, s, d))
        ps = lambda n, s, d=F32: ctx.enter_context(nc.psum_tensor("lin_" + n, s, d))
        sem = stage_semaphores(nc, ctx, "lin_")
        w = sb("w", [C, 3 * C])
        b_qk = sb("b_qk", [C, 2])
        b_kv = sb("b_kv", [P, 2 * C])
        decay = sb("decay", [P, P])
        q_decay = sb("q_decay", [C, P])
        k_decay = sb("k_decay", [P, 1])
        q_t, k_t, qd_t = (sb(n, [C, 2, QB]) for n in ("q_t", "k_t", "qd_t"))
        kv = sb("kv", [P, 2, SUB, 2 * C])
        kd = sb("kd", [P, 2, SUB, C])
        pr = sb("probs", [P, 2, SUB, P])
        state = sb("state", [C, B, NT + 1, C])
        qk_ps, kv_ps = ps("qk_ps", [C, 2, QB]), ps("kv_ps", [P, SUB, 2 * C])
        sc_ps, st_ps, out_ps = ps("sc_ps", [P, SUB, P]), ps("st_ps", [C, SUB, C]), ps("out_ps", [P, SUB, C])
        w_in, proj, q_ready, k_ready, kv_ready, kd_ready, qd_ready = (
            sem(n) for n in ("w_in", "proj", "q_ready", "k_ready", "kv_ready", "kd_ready", "qd_ready"))
        scored, pr_ready, st_mm, st_ready, out_mm, out_read, zeroed = (
            sem(n) for n in ("scored", "pr_ready", "st_mm", "st_ready", "out_mm", "out_read", "zeroed"))
        loads = [(w[:, :], t["lin_w"]), (b_qk[:, :], t["lin_b_qk"]), (b_kv[:, :], t["lin_b_kv"].broadcast_to([P, 2 * C])),
                 (decay[:, :], t["lin_decay"]), (q_decay[:, :], t["lin_q_decay"].broadcast_to([C, P])),
                 (k_decay[:, :], t["lin_k_decay"])]
        first = lambda n: (n % B) * N + (n // B) * QB

        with nc.Block() as block:
            @block.sync
            def _(sp):
                for dst, src in loads:
                    sp.dma_start(dst, src).then_inc(w_in, 16)

            @block.tensor
            def _(pe):
                pe.wait_ge(w_in, 16 * len(loads))
                for n in range(NBL + 2):
                    if n < NBL:
                        if n:
                            pe.wait_ge(q_ready, n)
                            pe.wait_ge(k_ready, n)
                            pe.wait_ge(kv_ready, n)
                        x = XT[:, first(n):first(n) + QB]
                        pe.matmul(qk_ps[:, 0, :], w[:, 0:C], x, start=True, stop=True)
                        pe.matmul(qk_ps[:, 1, :], w[:, C:2 * C], x, start=True, stop=True)
                        for i in range(SUB):
                            mm = pe.matmul(kv_ps[:, i, :], x[:, i * P:(i + 1) * P], w[:, C:3 * C],
                                           start=True, stop=True)
                        mm.then_inc(proj, 1)
                    if 1 <= n <= NBL:
                        m = n - 1
                        pe.wait_ge(q_ready, m + 1)
                        pe.wait_ge(k_ready, m + 1)
                        if m:
                            pe.wait_ge(pr_ready, m)
                            pe.wait_ge(st_ready, m)
                        for i in range(SUB):
                            mm = pe.matmul(sc_ps[:, i, :], k_t[:, m % 2, i * P:(i + 1) * P],
                                           q_t[:, m % 2, i * P:(i + 1) * P], start=True, stop=True)
                        mm.then_inc(scored, 1)
                        pe.wait_ge(kd_ready, m + 1)
                        for i in range(SUB):
                            mm = pe.matmul(st_ps[:, i, :], kd[:, m % 2, i, :], kv[:, m % 2, i, C:2 * C],
                                           start=True, stop=True)
                        mm.then_inc(st_mm, 1)
                    if n >= 2:
                        m = n - 2
                        pe.wait_ge(pr_ready, m + 1)
                        pe.wait_ge(st_ready, m + 1)
                        pe.wait_ge(qd_ready, m + 1)
                        if m:
                            pe.wait_ge(out_read, m)
                        for i in range(SUB):
                            pe.matmul(out_ps[:, i, :], pr[:, m % 2, i, :], kv[:, m % 2, i, C:2 * C],
                                      start=True, stop=False)
                            mm = pe.matmul(out_ps[:, i, :], qd_t[:, m % 2, i * P:(i + 1) * P],
                                           state[:, m % B, (m // B) * SUB + i, :], start=False, stop=True)
                        mm.then_inc(out_mm, 1)

            @block.scalar
            def _(act):
                act.wait_ge(w_in, 16 * len(loads))
                for n in range(NBL):
                    act.wait_ge(proj, n + 1)
                    if n >= 2:
                        act.wait_ge(scored, n - 1)
                    act.activation(k_t[:, n % 2, :], qk_ps[:, 1, :], ACT.Identity,
                                   bias=b_qk[:, 1:2]).then_inc(k_ready, 1)
                    act.wait_ge(kv_ready, n + 1)
                    if n >= 2:
                        act.wait_ge(st_mm, n - 1)
                    act.activation(kd[:, n % 2, :, :], kv[:, n % 2, :, 0:C], ACT.Copy,
                                   scale=k_decay[:, 0:1]).then_inc(kd_ready, 1)

            @block.vector
            def _(dve):
                dve.memset(state[:, :, 0, :], 0.0).then_inc(zeroed, 1)
                dve.wait_ge(zeroed, 1)
                dve.wait_ge(w_in, 16 * len(loads))
                for n in range(NBL + 2):
                    if n < NBL:
                        dve.wait_ge(proj, n + 1)
                        if n >= 2:
                            dve.wait_ge(out_mm, n - 1)
                        dve.tensor_scalar(q_t[:, n % 2, :], qk_ps[:, 0, :], b_qk[:, 0:1], C ** -0.5, ALU.add,
                                          ALU.mult).then_inc(q_ready, 1)
                        dve.tensor_tensor(kv[:, n % 2, :, :], kv_ps[:, :, :],
                                          b_kv[:, :].unsqueeze(1).broadcast_to([P, SUB, 2 * C]),
                                          ALU.add).then_inc(kv_ready, 1)
                        dve.wait_ge(q_ready, n + 1)
                        dve.tensor_tensor(qd_t[:, n % 2, :].rearrange("c (i q) -> c i q", i=SUB),
                                          q_t[:, n % 2, :].rearrange("c (i q) -> c i q", i=SUB),
                                          q_decay[:, :].unsqueeze(1).broadcast_to([C, SUB, P]),
                                          ALU.mult).then_inc(qd_ready, 1)
                    if 1 <= n <= NBL:
                        m = n - 1
                        dve.wait_ge(scored, m + 1)
                        dve.tensor_tensor(pr[:, m % 2, :, :], sc_ps[:, :, :],
                                          decay[:, :].unsqueeze(1).broadcast_to([P, SUB, P]),
                                          ALU.mult).then_inc(pr_ready, 1)
                        dve.wait_ge(st_mm, m + 1)
                        for i in range(SUB):
                            c = (m // B) * SUB + i
                            ins = dve.scalar_tensor_tensor(out=state[:, m % B, c + 1, :], in0=state[:, m % B, c, :],
                                                           scalar=float(ALPHA ** P), in1=st_ps[:, i, :],
                                                           op0=ALU.mult, op1=ALU.add)
                            if i < SUB - 1:
                                ins.then_inc(zeroed, 1)
                                dve.wait_ge(zeroed, m * (SUB - 1) + i + 2)
                        ins.then_inc(st_ready, 1)
                    if n >= 2:
                        m = n - 2
                        dve.wait_ge(out_mm, m + 1)
                        tile = first(m) // P
                        dve.tensor_tensor(H[:, tile:tile + SUB, :], H[:, tile:tile + SUB, :], out_ps[:, :, :],
                                          ALU.add).then_inc(out_read, 1)


def tower(nc, t, out, stages=99, only=None):
    with ExitStack() as ctx:
        sb = lambda n, s, d=F32: ctx.enter_context(nc.sbuf_tensor(n, s, d))
        H = sb("H", [P, T, C])
        ident = sb("ident", [P, P])
        identb = sb("identb", [P, P], BF16)
        in_sem = ctx.enter_context(nc.semaphore("ident_in"))
        cast_sem = ctx.enter_context(nc.semaphore("ident_cast"))
        out_sem = ctx.enter_context(nc.semaphore("out_written"))
        with nc.Block() as block:
            @block.sync
            def _(sp):
                sp.dma_start(ident[:, :], t["ident"]).then_inc(in_sem, 16)
                if only is not None:
                    sp.dma_start(H[:, :, :].rearrange("p t f -> p (t f)"), t["h_in"]).then_inc(out_sem, 16)
                    sp.wait_ge(out_sem, 16)
            @block.vector
            def _(dve):
                dve.wait_ge(in_sem, 16)
                dve.tensor_copy(identb[:, :], ident[:, :]).then_inc(cast_sem, 1)
                dve.wait_ge(cast_sem, 1)
        def run(n):
            return stages >= n and (only is None or only + 2 == n)
        if only is None:
            involution_stage(nc, t, H)
        if run(2):
            with ExitStack() as c2:
                XT = c2.enter_context(nc.sbuf_tensor("XT", [C, T * P], F32))
                norm_stage(nc, "ln1_", H, XT, ident, True, 1e-5)
                attention0_stage(nc, t, H, XT, ident, identb)
        if run(3):
            with ExitStack() as c2:
                XT = [c2.enter_context(nc.sbuf_tensor(f"XT2_{i}", [P, T * P], BF16)) for i in range(2)]
                norm_stage(nc, "ln2_", H, None, ident, True, 1e-5, parts=XT)
                moe_stage(nc, "moe0_", t, H, XT, ident, F0 // 2, 1, False, 0.0)
        if run(4):
            with ExitStack() as c2:
                XT = c2.enter_context(nc.sbuf_tensor("XT3", [C, T * P], F32))
                norm_stage(nc, "ln3_", H, XT, ident, True, 1e-5)
                linear_attention_stage(nc, t, H, XT)
        if run(5):
            final_stages(nc, t, H, ident, identb, out)
        else:
            with nc.Block() as block:
                @block.sync
                def _(sp):
                    sp.dma_start(out, H[:, :, :].rearrange("p t f -> p (t f)")).then_inc(in_sem, 16)
                    sp.wait_ge(in_sem, 32)


def final_stages(nc, t, H, ident, identb, out):
    flat = lambda x: x[:, :, :].rearrange("p t f -> p (t f)")
    with ExitStack() as ctx:
        U = ctx.enter_context(nc.sbuf_tensor("U", [P, T, C], F32))
        gains = ctx.enter_context(nc.sbuf_tensor("gains", [C, 2], F32))
        gains_in, h_out, h_in, summed, u_out = (
            ctx.enter_context(nc.semaphore(n)) for n in ("gains_in", "h_out", "h_in", "summed", "u_out"))
        norm_stage(nc, "ln4_", H, None, ident, True, 1e-5, U=U)
        with nc.Block() as block:
            @block.sync
            def _(sp):
                sp.dma_start(t["h_dram"], flat(H)).then_inc(h_out, 16)
                sp.dma_start(gains[:, :], t["gains"]).then_inc(gains_in, 16)
                sp.wait_ge(h_out, 16)
                sp.wait_ge(gains_in, 16)
        with ExitStack() as c2:
            XT = c2.enter_context(nc.sbuf_tensor("XT4", [C, T * P], F32))
            norm_stage(nc, "rms1_", U, XT, ident, False, 1e-6, gain=gains[:, 0:1])
            attention1_stage(nc, t, U, XT, ident, identb)
        with ExitStack() as c2:
            XT = [c2.enter_context(nc.sbuf_tensor(f"XT5_{i}", [P, T * P], BF16)) for i in range(2)]
            norm_stage(nc, "rms2_", U, None, ident, False, 1e-6, gain=gains[:, 1:2], parts=XT)
            moe_stage(nc, "moe1_", t, U, XT, ident, F1 // 2, 0, True, 1e-9)
        with nc.Block() as block:
            @block.sync
            def _(sp):
                sp.dma_start(flat(H), t["h_dram"]).then_inc(h_in, 16)
                sp.wait_ge(summed, 1)
                sp.dma_start(out, flat(U)).then_inc(u_out, 16)
                sp.wait_ge(u_out, 16)

            @block.vector
            def _(dve):
                dve.wait_ge(h_in, 16)
                dve.tensor_tensor(flat(U), flat(U), flat(H), ALU.add).then_inc(summed, 1)


def bias_table():
    n = np.arange(N, dtype=np.float64)
    return np.stack([f(2 * np.pi * n / period) for period in (24.0, 720.0) for f in (np.cos, np.sin)]
                    ).astype(np.float32)


def decay_tables():
    n = np.arange(P, dtype=np.float64)
    between = n[None, :] - n[:, None]
    return {"lin_decay": np.where(between >= 0, ALPHA ** np.maximum(between, 0), 0.0).astype(np.float32),
            "lin_q_decay": (ALPHA ** (n + 1)).astype(np.float32)[None],
            "lin_k_decay": (ALPHA ** (P - 1 - n)).astype(np.float32)[:, None]}


def rotary_tables():
    inv = 1.0 / 10000.0 ** (np.arange(0, HD, 2, dtype=np.float32) / HD)
    angle = np.outer(np.arange(N, dtype=np.float32), inv).reshape(NT, P, HD // 2).transpose(1, 0, 2)
    return {"at1_cos": np.cos(angle), "at1_sin": np.sin(angle)}


def causal_masks():
    n = np.arange(P)
    after = (n[None, :] > n[:, None]) * np.float32(NEG)
    return np.stack([after, after.T], 1).astype(mybir.dt.np(BF16))


def output_rows(wo):
    a = np.zeros((NH, 32, NH, C + 1), np.float32)
    for h in range(NH):
        a[h, :HD, h, :C] = wo[:, h * HD:(h + 1) * HD].T
        a[h, HD, h, C] = 1
    return a.reshape(P, NH * (C + 1))


def layouts(i):
    f = lambda n: np.asarray(i[n])
    x = f("x")
    a = {
        "x_rows": x.reshape(B, NT, 2, S, S).transpose(2, 3, 0, 1, 4),
        "x_chan": x.reshape(B, C, N).transpose(1, 0, 2).reshape(C, B * N),
        "conv1T": f("L0_tok_conv1_w").T,
        "conv2T": f("L0_tok_conv2_w").T,
        "bn": np.stack([f("L0_tok_conv1_b"), f("L0_tok_bn_gamma"), f("L0_tok_bn_beta"),
                        f("L0_tok_bn_mean"), f("L0_tok_bn_var")], 1),
        "conv2_b": f("L0_tok_conv2_b")[:, None],
        "ident": np.eye(P, dtype=np.float32),
        "at0_w": np.concatenate([f("L0_attn_Wq").T, f("L0_attn_Wk").T, f("L0_attn_Wv").T], 1),
        "at0_b": np.stack([f("L0_attn_bq"), f("L0_attn_bk")], 1),
        "at0_bv": f("L0_attn_bv")[None],
        "at0_beta": np.repeat(f("L0_attn_beta"), 2)[:, None],
        "at0_table": bias_table(),
        "rank": np.arange(NE, 0, -1, dtype=np.float32)[None],
        "moe0_router": f("L0_ffn_Wr"),
        "moe0_w1": np.concatenate([f("L0_ffn_W1p"), f("L0_ffn_W1s")[None]]).transpose(1, 0, 2)
                     .reshape(C, -1),
        "moe0_w2": np.concatenate([f("L0_ffn_W2p"), f("L0_ffn_W2s")[None]])
                     .reshape(2 * NE + 2, F0 // 2, C).transpose(1, 0, 2),
        "moe0_b1": np.concatenate([f("L0_ffn_b1p"), f("L0_ffn_b1s")[None]]).reshape(2 * NE + 2, F0 // 2).T,
        "moe0_b2": np.concatenate([f("L0_ffn_b2p"), f("L0_ffn_b2s")[None]]),
        "lin_w": f("L1_attn_Wqkv"),
        "lin_b_qk": f("L1_attn_bqkv")[:2 * C].reshape(2, C).T,
        "lin_b_kv": f("L1_attn_bqkv")[None, C:],
        **decay_tables(),
        "gains": np.stack([f("L1_ffn_ln1_w"), f("L1_ffn_ln2_w")], 1),
        "at1_w": np.concatenate([f("L1_ffn_wq"), f("L1_ffn_wk"), f("L1_ffn_wv")]).T,
        "at1_wo": output_rows(f("L1_ffn_wo")),
        **rotary_tables(),
        "causal_mask": causal_masks(),
        "moe1_router": f("L1_ffn_router_w").T,
        "moe1_w1": f("L1_ffn_w1").transpose(2, 0, 1).reshape(C, -1),
        "moe1_w3": f("L1_ffn_w3").transpose(2, 0, 1).reshape(C, -1),
        "moe1_w2": f("L1_ffn_w2").transpose(0, 2, 1).reshape(2 * NE, F1 // 2, C).transpose(1, 0, 2),
    }
    a["x_rows"] = a["x_rows"].reshape(P, B, NT, S)
    return {k: np.ascontiguousarray(v) for k, v in a.items()}


def kernel(**inputs):
    import concourse.bacc as _bacc
    from concourse.bass_utils import run_bass_kernel_spmd as _run

    nc = _bacc.Bacc("TRN2", target_bir_lowering=False, num_devices=1)
    arrays = layouts(inputs)
    t = {n: nc.dram_tensor(n + "_dram", a.shape, mybir.dt.from_np(a.dtype), kind="ExternalInput").ap()
         for n, a in arrays.items()}
    t["h_dram"] = nc.dram_tensor("h_scratch", (P, T * C), F32, kind="Internal").ap()
    t["wd_dram"] = nc.dram_tensor("wd_scratch", (TAPS, B * N), F32, kind="Internal").ap()
    out = nc.dram_tensor("out_0_dram", (P, T * C), F32, kind="ExternalOutput").ap()
    tower(nc, t, out)
    r = _run(nc, [{n + "_dram": a for n, a in arrays.items()}], core_ids=[0])
    got = r.results[0]["out_0_dram"]
    return got.reshape(P, B, NT, C).transpose(1, 2, 0, 3).reshape(B, N, C)
```

```python
from contextlib import ExitStack

import numpy as np

import concourse.bass as bass
from concourse import mybir

ALU = mybir.AluOpType
ACT = mybir.ActivationFunctionType
F32 = mybir.dt.float32
BF16 = mybir.dt.bfloat16
AX = mybir.AxisListType

P = 128
B = 2
C = 64
S = 64
N = C * S
NT = N // P
T = B * NT
QB = 512
NQ = N // QB
SUB = QB // P
CR = 16
TAPS = 9
NE = 8
F0 = 256
F1 = 170
NH, NKV, HD = 4, 2, 16
ALPHA = float(np.float32(0.99))
NEG = -1e30


def stage_semaphores(nc, ctx, prefix):
    taken = []

    def zero():
        nc.clear_and_free_semaphores(taken)
        nc.all_engine_barrier()

    ctx.callback(zero)

    def sem(name):
        taken.append(nc.alloc_semaphore(prefix + name))
        return taken[-1]

    return sem


def involution_stage(nc, t, H):
    POOL_T = 10
    DVE_T = NT - POOL_T
    CH = B * N // QB
    with ExitStack() as ctx:
        sb = lambda n, s, d=F32: ctx.enter_context(nc.sbuf_tensor(n, s, d))
        ps = lambda n, s, d=F32: ctx.enter_context(nc.psum_tensor(n, s, d))
        sem = stage_semaphores(nc, ctx, "")
        rows = [sb(f"x_rows{i}", [P, B, NT, S + 2]) for i in range(3)]
        xc = sb("x_chan", [C, B * N // 2])
        w1 = sb("conv1", [C, CR])
        w2 = sb("conv2", [CR, TAPS])
        bn = sb("bn", [CR, 8])
        b2 = sb("conv2_bias", [TAPS, 1])
        y = sb("bottleneck", [CR, 2, QB])
        wd = sb("tap_weights", [TAPS, B, N])
        wdt = sb("tap_weights_tok", [P, B, TAPS, S])
        prod_v = sb("prod_v", [P, 2, B, DVE_T, S])
        prod_g = sb("prod_g", [P, 2, B, POOL_T, S])
        y_ps = [ps(f"y_ps{i}", [CR, QB]) for i in range(2)]
        wd_ps = [ps(f"wd_ps{i}", [TAPS, QB]) for i in range(2)]

        zeroed = sem("zeroed")
        rows_in = sem("rows_in")
        small_in = sem("small_in")
        xc_in = [sem("xc_in0"), sem("xc_in1")]
        bn_ready = sem("bn_ready")
        y_mm, y_ready, wd_mm, wd_ready = sem("y_mm"), sem("y_ready"), sem("wd_mm"), sem("wd_ready")
        wd_out, wdt_in = sem("wd_out"), sem("wdt_in")
        v_step, g_step = sem("inv_v_step"), sem("inv_g_step")
        half = CH // 2

        with nc.Block() as block:
            @block.sync
            def _(sp):
                sp.dma_start(w1[:, :], t["conv1T"]).then_inc(small_in, 16)
                sp.dma_start(w2[:, :], t["conv2T"]).then_inc(small_in, 16)
                sp.dma_start(bn[:, 0:5], t["bn"]).then_inc(small_in, 16)
                sp.dma_start(b2[:, :], t["conv2_b"]).then_inc(small_in, 16)
                sp.dma_start(xc[:, :], t["x_chan"][:, 0:N]).then_inc(xc_in[0], 16)
                sp.wait_ge(zeroed, 3)
                for i in range(3):
                    for half_p in range(2):
                        lo, hi = max(0, 1 - i), min(S, S + 1 - i)
                        src = t["x_rows"][half_p * S + lo + i - 1:half_p * S + hi + i - 1]
                        sp.dma_start(rows[i][half_p * S + lo:half_p * S + hi, :, :, 1:S + 1],
                                     src).then_inc(rows_in, 16)
                sp.wait_ge(y_mm, half)
                sp.dma_start(xc[:, :], t["x_chan"][:, N:2 * N]).then_inc(xc_in[1], 16)
                sp.wait_ge(wd_ready, CH)
                sp.dma_start(t["wd_dram"], wd[:, :, :].rearrange("k b n -> k (b n)")).then_inc(wd_out, 16)
                sp.wait_ge(wd_out, 16)
                for half_p in range(2):
                    for b in range(B):
                        sp.dma_start(wdt[half_p * S:(half_p + 1) * S, b, :, :],
                                     t["wd_dram"].rearrange("k (b h w) -> b h k w", b=B, h=S)[b])\
                          .then_inc(wdt_in, 16)

            @block.tensor
            def _(pe):
                pe.wait_ge(small_in, 64)
                for im in range(B):
                    pe.wait_ge(xc_in[im], 16)
                    for c in range(half):
                        n = im * half + c
                        if n >= 2:
                            pe.wait_ge(y_ready, n - 1)
                        pe.matmul(y_ps[n % 2][:, :], w1[:, :], xc[:, c * QB:(c + 1) * QB],
                                  start=True, stop=True).then_inc(y_mm, 1)
                        if n >= 2:
                            pe.wait_ge(wd_ready, n - 1)
                        pe.wait_ge(y_ready, n + 1)
                        pe.matmul(wd_ps[n % 2][:, :], w2[:, :], y[:, n % 2, :],
                                  start=True, stop=True).then_inc(wd_mm, 1)

            @block.scalar
            def _(act):
                act.wait_ge(bn_ready, 1)
                act.activation(bn[:, 6:7], bn[:, 5:6], ACT.Sqrt).then_inc(bn_ready, 1)
                act.wait_ge(bn_ready, 5)
                for n in range(CH):
                    act.wait_ge(y_mm, n + 1)
                    if n >= 2:
                        act.wait_ge(wd_mm, n - 1)
                    act.activation(y[:, n % 2, :], y_ps[n % 2][:, :], ACT.Relu, bias=bn[:, 7:8],
                                   scale=bn[:, 6:7]).then_inc(y_ready, 1)

            def taps(eng, step, prod, acc, t0, t1):
                n = 0
                for k in range(TAPS):
                    x = rows[k // 3][:, :, t0:t1, k % 3:k % 3 + S]
                    w = wdt[:, :, k:k + 1, :].broadcast_to([P, B, t1 - t0, S])
                    if k >= 3:
                        eng.wait_ge(step, n - 2)
                    eng.tensor_tensor(acc if k == 0 else prod[:, k % 2, :, :, :], x, w,
                                      ALU.mult).then_inc(step, 1)
                    n += 1
                    if k:
                        eng.wait_ge(step, n)
                        eng.tensor_tensor(acc, acc, prod[:, k % 2, :, :, :], ALU.add).then_inc(step, 1)
                        n += 1

            Hv = H[:, :, :].rearrange("p (b t) f -> p b t f", b=B)

            @block.gpsimd
            def _(pool):
                pool.wait_ge(rows_in, 96)
                pool.wait_ge(wdt_in, 64)
                taps(pool, g_step, prod_g, Hv[:, :, DVE_T:NT, :], DVE_T, NT)

            @block.vector
            def _(dve):
                for i in range(3):
                    dve.memset(rows[i][:, :, :, :], 0.0).then_inc(zeroed, 1)
                dve.wait_ge(small_in, 64)
                dve.tensor_scalar(bn[:, 5:6], bn[:, 4:5], 1e-5, None, ALU.add).then_inc(bn_ready, 1)
                dve.wait_ge(bn_ready, 2)
                dve.reciprocal(bn[:, 5:6], bn[:, 6:7]).then_inc(bn_ready, 1)
                dve.wait_ge(bn_ready, 3)
                dve.tensor_tensor(bn[:, 6:7], bn[:, 5:6], bn[:, 1:2], ALU.mult)
                dve.tensor_tensor(bn[:, 7:8], bn[:, 0:1], bn[:, 3:4], ALU.subtract).then_inc(bn_ready, 1)
                dve.wait_ge(bn_ready, 4)
                dve.scalar_tensor_tensor(out=bn[:, 7:8], in0=bn[:, 7:8], scalar=bn[:, 6:7], in1=bn[:, 2:3],
                                         op0=ALU.mult, op1=ALU.add).then_inc(bn_ready, 1)
                for n in range(CH):
                    dve.wait_ge(wd_mm, n + 1)
                    dve.tensor_scalar(wd[:, n // half, (n % half) * QB:(n % half + 1) * QB],
                                      wd_ps[n % 2][:, :], b2[:, 0:1], None, ALU.add).then_inc(wd_ready, 1)
                dve.wait_ge(rows_in, 96)
                dve.wait_ge(wdt_in, 64)
                taps(dve, v_step, prod_v, Hv[:, :, 0:DVE_T, :], 0, DVE_T)


def norm_stage(nc, name, H, XT, ident, centred, eps, gain=None, U=None, parts=None):
    turns = U is None
    G = 16
    NG = T // G
    with ExitStack() as ctx:
        sb = lambda n, s, d=F32: ctx.enter_context(nc.sbuf_tensor(name + n, s, d))
        sem = stage_semaphores(nc, ctx, name)
        xc = sb("centred", [P, 2, G, C])
        sq = sb("squares", [P, 2, G, C])
        st = sb("stats", [P, 4, 2, G])
        tr_ps = [ctx.enter_context(nc.psum_tensor(f"{name}tr_ps{i}", [C, G // 4, QB], F32)) for i in range(2)]
        v_step, sq_ready, sd_ready = sem("v_step"), sem("sq_ready"), sem("sd_ready")
        xn_ready, transposed, xt_ready = sem("xn_ready"), sem("transposed"), sem("xt_ready")
        var_ready, xc_ready = sem("var_ready"), sem("xc_ready")
        rest_ready, mid_ready, low_ready, copied = sem("rest_ready"), sem("mid_ready"), sem("low_ready"), sem("copied")
        rest = sb("rest", [C, G * P]) if parts else None
        tokens = lambda g: slice(g * G * P, (g + 1) * G * P)
        with nc.Block() as block:
            @block.vector
            def _(dve):
                n = 0
                for g in range(NG + 2 if parts else NG + 1):
                    k = g % 2
                    if g < NG:
                        x = H[:, g * G:(g + 1) * G, :]
                        if centred:
                            dve.tensor_reduce(st[:, 0, k, :], x, AX.X, ALU.add).then_inc(v_step, 1)
                            dve.wait_ge(v_step, n + 1)
                            dve.tensor_scalar(st[:, 0, k, :], st[:, 0, k, :], -1.0 / C, None,
                                              ALU.mult).then_inc(v_step, 1)
                            dve.wait_ge(v_step, n + 2)
                            n += 2
                            if g >= 2 and turns:
                                dve.wait_ge(transposed, g - 1)
                            dve.tensor_tensor(xc[:, k, :, :], x,
                                              st[:, 0, k, :].unsqueeze(2).broadcast_to([P, G, C]),
                                              ALU.add).then_inc(xc_ready, 1)
                    if 0 < g <= NG:
                        k = (g - 1) % 2
                        dve.wait_ge(sq_ready, g)
                        dve.tensor_reduce(st[:, 1, k, :], sq[:, k, :, :], AX.X, ALU.add).then_inc(v_step, 1)
                        dve.wait_ge(v_step, n + 1)
                        dve.tensor_scalar(st[:, 1, k, :], st[:, 1, k, :], 1.0 / C, eps, ALU.mult,
                                          ALU.add).then_inc(var_ready, 1)
                        dve.wait_ge(sd_ready, g)
                        dve.reciprocal(st[:, 3, k, :], st[:, 2, k, :]).then_inc(v_step, 1)
                        dve.wait_ge(v_step, n + 2)
                        n += 2
                        if centred:
                            dve.wait_ge(xc_ready, g)
                        elif g > 2:
                            dve.wait_ge(transposed, g - 2)
                        src = xc[:, k, :, :] if centred else H[:, (g - 1) * G:g * G, :]
                        dst = xc[:, k, :, :] if U is None else U[:, (g - 1) * G:g * G, :]
                        dve.tensor_tensor(dst, src,
                                          st[:, 3, k, :].unsqueeze(2).broadcast_to([P, G, C]),
                                          ALU.mult).then_inc(xn_ready, 1)
                    if parts and g >= 2:
                        mh, hl = parts
                        m = g - 2
                        dve.wait_ge(xt_ready, m + 1)
                        if m:
                            dve.wait_ge(low_ready, m)
                        dve.scalar_tensor_tensor(
                            out=rest[:, :], in0=tr_ps[m % 2][:, :, :].rearrange("c a q -> c (a q)"),
                            scalar=1.0 if gain is None else gain, in1=hl[0:C, tokens(m)],
                            op0=ALU.mult, op1=ALU.subtract).then_inc(rest_ready, 1)
                        dve.wait_ge(mid_ready, m + 1)
                        dve.tensor_tensor(hl[C:2 * C, tokens(m)], rest[:, :], mh[0:C, tokens(m)],
                                          ALU.subtract).then_inc(low_ready, 1)

            @block.scalar
            def _(act):
                def copy_out(g):
                    act.wait_ge(transposed, g + 1)
                    out = parts[1][0:C, tokens(g)] if parts else XT[:, tokens(g)]
                    src = tr_ps[g % 2][:, :, :].rearrange("c a q -> c (a q)")
                    if gain is None:
                        act.activation(out, src, ACT.Copy).then_inc(xt_ready, 1)
                    else:
                        act.activation(out, src, ACT.Copy, scale=gain).then_inc(xt_ready, 1)
                    if parts:
                        act.wait_ge(rest_ready, g + 1)
                        act.activation(parts[0][0:C, tokens(g)], rest[:, :], ACT.Copy).then_inc(mid_ready, 1)
                for g in range(NG + 1):
                    if g < NG:
                        if centred:
                            act.wait_ge(xc_ready, g + 1)
                        if g >= 2:
                            act.wait_ge(var_ready, g - 1)
                        src = xc[:, g % 2, :, :] if centred else H[:, g * G:(g + 1) * G, :]
                        act.activation(sq[:, g % 2, :, :], src, ACT.Square).then_inc(sq_ready, 1)
                        act.wait_ge(var_ready, g + 1)
                        act.activation(st[:, 2, g % 2, :], st[:, 1, g % 2, :], ACT.Sqrt).then_inc(sd_ready, 1)
                    if g > 0 and turns:
                        copy_out(g - 1)

            @block.tensor
            def _(pe):
                for g in range(NG if turns else 0):
                    pe.wait_ge(xn_ready, g + 1)
                    if g >= 2:
                        pe.wait_ge(rest_ready if parts else xt_ready, g - 1)
                    for i in range(G):
                        mm = pe.transpose(tr_ps[g % 2][:, i // 4, (i % 4) * P:(i % 4 + 1) * P],
                                          xc[:, g % 2, i, :], ident[:, :])
                    mm.then_inc(transposed, 1)

            if parts:
                @block.gpsimd
                def _(pool):
                    for g in range(NG):
                        pool.wait_ge(xt_ready, g + 1)
                        pool.tensor_copy(parts[0][C:2 * C, tokens(g)], parts[1][0:C, tokens(g)]).then_inc(copied, 1)



M_ROW = 96


class AttentionShape:

    def __init__(self, causal, heads):
        self.causal, self.heads = causal, heads
        self.rows = heads * SUB
        self.m_rows = 3 if causal else 1
        self.halves = 2 if causal else 1
        self.sum_rows = 32 if causal else C + 1
        self.sums_all = heads * self.sum_rows
        self.pv_units = NKV if causal else 1
        self.probs_bufs = 4 if causal else 3
        self.order = list(reversed(range(NQ))) if causal else list(range(NQ))
        self.max_tiles = [self._max_tiles(q) for q in self.order]
        self.units = [self._units(q) for q in self.order]
        first = lambda lists: np.concatenate([[0], np.cumsum([len(x) for x in lists])]).tolist()
        self.max_first, self.unit_first = first(self.max_tiles), first(self.units)
        self.pv_first = [n // self.pv_units for n in self.unit_first]
        self.max_all, self.unit_all, self.pv_all = self.max_first[-1], self.unit_first[-1], self.pv_first[-1]
        self.steps = self._schedule()

    def _max_tiles(self, q):
        out = []
        for h in range(self.heads):
            for s in range(SUB):
                for c in range(self.chunks(q)):
                    diagonal = self.causal and c == q
                    out.append((h, s, c, (s + 1) * P if diagonal else QB, diagonal))
        return out

    def _units(self, q):
        if not self.causal:
            return [(((0, 2 * u), (0, 2 * u + 1)), 0, False) for u in range(NT // 2)]
        return [(((2 * g, k), (2 * g + 1, k)), max(0, k - SUB * q) * P, k >= SUB * q)
                for k in range(SUB * (q + 1)) for g in range(NKV)]

    def chunks(self, q):
        return q + 1 if self.causal else NQ

    def kv(self, h):
        return h // 2 if self.causal else 0

    def _schedule(self):
        step_us, col = 0.15, 1 / 2400.
        max_cost = 1
        exp_cost = 1 if self.causal else 4
        place = [j for j in range(NQ) for _ in self.units[j]]
        steps, t, dve, act = [], 0.0, 0.0, 0.0
        m = u = p = o = f = closed = n = 0
        max_done, exp_done, rows_done, fin_free, sums_done, o_free = [], [], {}, 0.0, {}, 0.0
        chain_done = {}
        while f < NQ * SUB:
            ready = []
            j = next((k for k in range(NQ) if m < self.max_first[k + 1]), NQ)
            if j < NQ and (m + 1 < self.max_first[j + 1] or n >= j * self.halves):
                ready.append((max_done[m - 2] if m >= 2 else 0.0, 0, "m"))
            if n < closed * self.halves:
                ready.append((max(fin_free, chain_done[n // self.halves]), 1, "n"))
            if f < o * SUB:
                ready.append((max(fin_free, sums_done[f // SUB]), 2, "f"))
            if p < self.pv_all and (p + 1) * self.pv_units <= u:
                k = place[p * self.pv_units]
                if k <= o:
                    ready.append((max(exp_done[(p + 1) * self.pv_units - 1],
                                      o_free if p == self.pv_first[k] else 0.0), 4, "p"))
            if u < self.unit_all and u < self.probs_bufs + p * self.pv_units and place[u] in rows_done:
                ready.append((max(exp_done[u - 2] if u >= 2 else 0.0, rows_done[place[u]]), 3, "u"))
            if o < NQ and p == self.pv_first[o + 1] and f >= o * SUB:
                ready.append((0.0, -1, "o"))
            at, _, kind = min((max(at, t), order, kind) for at, order, kind in ready)
            t = at
            if kind == "m":
                keys = self.max_tiles[j][m - self.max_first[j]][3]
                steps.append(("m", j, m - self.max_first[j]))
                t += keys * col * max_cost
                dve = max(dve, t + step_us) + keys / 960. + 0.06
                max_done.append(dve + step_us)
                m += 1
                if m == self.max_first[j + 1]:
                    steps.append(("c", j, 0))
                    dve += 0.2 * (6 if self.m_rows > 1 else 1)
                    chain_done[j] = dve + step_us
                    closed += 1
            elif kind == "n":
                j, r = divmod(n, self.halves)
                steps.append(("n", j, r))
                t += 0.055 * self.rows / self.halves
                dve = max(dve, t + step_us) + 0.6
                fin_free = dve + step_us
                if r == self.halves - 1:
                    rows_done[j] = dve + step_us
                n += 1
            elif kind == "u":
                j = place[u]
                c = 2 * (QB - self.units[j][u - self.unit_first[j]][1])
                steps.append(("u", j, u - self.unit_first[j]))
                t += c * col * exp_cost
                act = max(act, t + step_us) + c / 1200. + 0.05
                exp_done.append(act + step_us)
                u += 1
            elif kind == "p":
                j = place[p * self.pv_units]
                c = QB - self.units[j][p * self.pv_units - self.unit_first[j]][1]
                steps.append(("p", j, p - self.pv_first[j]))
                t += c * col * (4 if self.causal else 8)
                p += 1
            elif kind == "o":
                steps.append(("o", o, 0))
                act = max(act, t + step_us) + 0.5
                sums_done[o] = o_free = act + step_us
                o += 1
            else:
                steps.append(("f",) + divmod(f, SUB))
                t += (C + 1) * self.heads * 4 * col
                dve = max(dve, t + step_us) + 0.6
                fin_free = dve + step_us
                f += 1
        return steps


def attention_core(nc, ctx, name, sh, H, ident, identb, QT, KT, V, mask, fin_rhs):
    sb = lambda n, s, d=F32: ctx.enter_context(nc.sbuf_tensor(name + n, s, d))
    ps = lambda n, s, d=F32: ctx.enter_context(nc.psum_tensor(name + n, s, d))
    sem = stage_semaphores(nc, ctx, name + "core_")
    dt = QT.dtype
    heads, rows, halves, mr = sh.heads, sh.rows, sh.halves, sh.m_rows
    turn = ident if dt == F32 else identb
    per = rows // halves
    NP, PU = sh.probs_bufs, sh.pv_units
    k_exp = M_ROW + mr
    exp_ps = [ps(f"exp_ps{i}", [P, 2, QB]) for i in range(2)]
    max_ps = [ps(f"max_ps{i}", [P, QB]) for i in range(2)]
    o_ps = ps("o_ps", [P, QB])
    fin_ps = ps("fin_ps", [P, QB])
    probs = sb("probs", [P, NP, 2, QB])
    mx = sb("mx", [P, rows, NQ])
    nm = sb("nm", [P, 3, rows])
    nm_p = sb("nm_parts", [P, rows, mr], dt)
    sums = sb("sums", [P, QB])
    rec = sb("rec", [P, heads])
    scaled = sb("scaled", [P, 2, heads, C]) if heads > 1 else None
    max_mm, max_read = sem("max_mm"), sem("max_read")
    exp_mm, exp_done, pv_mm = sem("exp_mm"), sem("exp_done"), sem("pv_mm")
    nm_ready, nm_turned, nm_rows = sem("nm_ready"), sem("nm_turned"), sem("nm_rows")
    o_copied, fin_mm, fin_read, v_step = sem("o_copied"), sem("fin_mm"), sem("fin_read"), sem("v_step")
    head_step = sem("head_step")
    v_image = NQ * ((5 if mr > 1 else 0) + SUB)
    f_all, n_all = NQ * SUB, NQ * halves
    turned = fin_ps[0:mr, :] if dt == F32 else fin_ps[0:mr, :].bitcast(BF16)

    def tensor(pe, im):
        turned_before = read_before = 0
        for step, j, i in sh.steps:
            q = sh.order[j]
            if step == "m":
                h, s, c, keys, diagonal = sh.max_tiles[j][i]
                n = sh.max_first[j] + i
                q0 = q * QB + s * P
                if n >= 2:
                    pe.wait_ge(max_read, im * sh.max_all + n - 1)
                mm = pe.matmul(max_ps[n % 2][:, 0:keys], QT[0:M_ROW, h, q0:q0 + P],
                               KT[0:M_ROW, sh.kv(h), c * QB:c * QB + keys], start=True, stop=not diagonal)
                if diagonal:
                    mm = pe.matmul(max_ps[n % 2][:, keys - P:keys], identb[:, :], mask[:, 0, :],
                                   start=False, stop=True)
                mm.then_inc(max_mm, 1)
            elif step == "u":
                pair, c0, diagonal = sh.units[j][i]
                n = sh.unit_first[j] + i
                if i == 0:
                    pe.wait_ge(nm_rows, im * n_all + (j + 1) * halves)
                if n >= 2:
                    pe.wait_ge(exp_done, im * sh.unit_all + n - 1)
                for a, (h, k) in enumerate(pair):
                    mm = pe.matmul(exp_ps[n % 2][:, a, c0:QB], KT[0:k_exp, sh.kv(h), k * P:(k + 1) * P],
                                   QT[0:k_exp, h, q * QB + c0:(q + 1) * QB], start=True, stop=not diagonal)
                    if diagonal:
                        mm = pe.matmul(exp_ps[n % 2][:, a, c0:c0 + P], identb[:, :], mask[:, 1, :],
                                       start=False, stop=True)
                mm.then_inc(exp_mm, 1)
            elif step == "p":
                pe.wait_ge(exp_done, im * sh.unit_all + sh.unit_first[j] + (i + 1) * PU)
                if i == 0 and j > 0:
                    pe.wait_ge(o_copied, im * NQ + j)
                for u in range(i * PU, (i + 1) * PU):
                    pair, c0, _ = sh.units[j][u]
                    n = sh.unit_first[j] + u
                    for a, (h, k) in enumerate(pair):
                        last = u >= len(sh.units[j]) - PU and (sh.causal or a == 1)
                        mm = pe.matmul(o_ps[32 * h:32 * h + sh.sum_rows, c0:QB], V[:, k, sh.kv(h), :],
                                       probs[:, n % NP, a, c0:QB], start=(k == 0), stop=last)
                mm.then_inc(pv_mm, 1)
            elif step == "n":
                pe.wait_ge(nm_ready, im * NQ + j + 1)
                if turned_before:
                    pe.wait_ge(nm_rows, im * n_all + turned_before)
                if read_before:
                    pe.wait_ge(fin_read, im * f_all + read_before)
                for k in range(per):
                    mm = pe.transpose(turned[:, k * P:(k + 1) * P], nm_p[:, i * per + k, :], turn[:, :])
                mm.then_inc(nm_turned, 1)
                turned_before += 1
            elif step == "f":
                if i == 0:
                    pe.wait_ge(o_copied, im * NQ + j + 1)
                pe.wait_ge(nm_rows, im * n_all + turned_before)
                if read_before:
                    pe.wait_ge(fin_read, im * f_all + read_before)
                pe.matmul(fin_ps[:, 0:heads * (C + 1)], sums[0:sh.sums_all, i * P:(i + 1) * P], fin_rhs,
                          start=True, stop=True).then_inc(fin_mm, 1)
                read_before += 1

    def scalar(act, im):
        for step, j, i in sh.steps:
            if step == "u":
                c0 = sh.units[j][i][1]
                n = sh.unit_first[j] + i
                act.wait_ge(exp_mm, im * sh.unit_all + n + 1)
                if n >= NP:
                    act.wait_ge(pv_mm, im * sh.pv_all + (n - NP) // PU + 1)
                act.activation(probs[:, n % NP, :, c0:QB], exp_ps[n % 2][:, :, c0:QB],
                               ACT.Exp).then_inc(exp_done, 1)
            elif step == "o":
                act.wait_ge(pv_mm, im * sh.pv_all + sh.pv_first[j + 1])
                if j:
                    act.wait_ge(fin_mm, im * f_all + j * SUB)
                act.activation(sums[0:sh.sums_all, :], o_ps[0:sh.sums_all, :], ACT.Copy).then_inc(o_copied, 1)

    def vector(dve, im):
        own = 0

        def own_step(ins):
            nonlocal own
            ins.then_inc(v_step, 1)
            own += 1
            dve.wait_ge(v_step, im * v_image + own)

        for step, j, i in sh.steps:
            q = sh.order[j]
            if step == "m":
                h, s, c, keys, _ = sh.max_tiles[j][i]
                n = sh.max_first[j] + i
                dve.wait_ge(max_mm, im * sh.max_all + n + 1)
                dve.tensor_reduce(mx[:, h * SUB + s, c:c + 1], max_ps[n % 2][:, 0:keys], AX.X,
                                  ALU.max).then_inc(max_read, 1)
            elif step == "c":
                dve.wait_ge(max_read, im * sh.max_all + sh.max_first[j + 1])
                tiles = mx[:, :, 0:sh.chunks(q)]
                if mr == 1:
                    dve.tensor_reduce(nm_p[:, :, 0], tiles, AX.X, ALU.max, negate=True).then_inc(nm_ready, 1)
                    dve.wait_ge(nm_ready, im * NQ + j + 1)
                else:
                    own_step(dve.tensor_reduce(nm[:, 0, :], tiles, AX.X, ALU.max, negate=True))
                    own_step(dve.tensor_copy(nm_p[:, :, 0], nm[:, 0, :]))
                    own_step(dve.tensor_tensor(nm[:, 1, :], nm[:, 0, :], nm_p[:, :, 0], ALU.subtract))
                    own_step(dve.tensor_copy(nm_p[:, :, 1], nm[:, 1, :]))
                    own_step(dve.tensor_tensor(nm[:, 2, :], nm[:, 1, :], nm_p[:, :, 1], ALU.subtract))
                    dve.tensor_copy(nm_p[:, :, 2], nm[:, 2, :]).then_inc(nm_ready, 1)
            elif step == "n":
                dve.wait_ge(nm_turned, im * n_all + j * halves + i + 1)
                hs = slice(i * heads // halves, (i + 1) * heads // halves)
                dve.tensor_copy(QT[M_ROW:M_ROW + mr, hs, q * QB:(q + 1) * QB],
                                turned[:, 0:per * P].rearrange("m (h t) -> m h t", t=QB)
                                ).then_inc(nm_rows, 1)
            elif step == "f":
                n = j * SUB + i
                dve.wait_ge(fin_mm, im * f_all + n + 1)
                fin = fin_ps[:, 0:heads * (C + 1)].rearrange("p (h c) -> p h c", h=heads)
                own_step(dve.reciprocal(rec[:, :], fin[:, :, C]))
                if heads == 1:
                    h_tile = H[:, bass.ds(im * NT + (q * SUB + i), 1), :]
                    dve.scalar_tensor_tensor(out=h_tile, in0=fin[:, :, 0:C], scalar=rec[:, 0:1], in1=h_tile,
                                             op0=ALU.mult, op1=ALU.add).then_inc(fin_read, 1)
                else:
                    dve.wait_ge(head_step, (im * f_all + n + 1) * 3)
                    dve.tensor_tensor(scaled[:, n % 2, :, :], fin[:, :, 0:C],
                                      rec[:, :].unsqueeze(2).broadcast_to([P, heads, C]),
                                      ALU.mult).then_inc(fin_read, 1)

    def heads_onto_h(pool, im):
        for step, j, i in sh.steps:
            if step != "f":
                continue
            n = j * SUB + i
            tile = scaled[:, n % 2, :, :]
            h_tile = H[:, bass.ds(im * NT + (sh.order[j] * SUB + i), 1), :]
            count = lambda k: (im * f_all + n + 2) * 3 + k
            pool.wait_ge(fin_read, im * f_all + n + 1)
            pool.tensor_tensor(tile[:, 0:2, :], tile[:, 0:2, :], tile[:, 2:4, :], ALU.add).then_inc(head_step, 1)
            pool.wait_ge(head_step, count(1))
            pool.tensor_tensor(tile[:, 0, :], tile[:, 0, :], tile[:, 1, :], ALU.add).then_inc(head_step, 1)
            pool.wait_ge(head_step, count(2))
            pool.tensor_tensor(h_tile, h_tile, tile[:, 0:1, :], ALU.add).then_inc(head_step, 1)
            pool.wait_ge(head_step, count(3))

    return tensor, scalar, vector, heads_onto_h, head_step, exp_ps, max_ps


def attention0_stage(nc, t, H, XT, ident, identb):
    sh = AttentionShape(causal=False, heads=1)
    with ExitStack() as ctx:
        sb = lambda n, s, d=F32: ctx.enter_context(nc.sbuf_tensor("at0_" + n, s, d))
        sem = stage_semaphores(nc, ctx, "at0_")
        QT, KT = sb("QT", [P, 1, N]), sb("KT", [P, 1, N])
        V = sb("V", [P, NT, 1, C + 1])
        xb = sb("x_image", [C, N])
        w = sb("wqkv", [C, 3 * C])
        bias = sb("bias", [C, 2])
        beta = sb("beta", [P, 1])
        bv = sb("bias_v", [P, C])
        tensor, scalar, vector, _, _, exp_ps, max_ps = attention_core(
            nc, ctx, "at0_", sh, H, ident, identb, QT, KT, V, None, ident[0:C + 1, 0:C + 1])
        w_in, x_in, zeroed, table_in = sem("w_in"), sem("x_in"), sem("zeroed"), sem("table_in")
        qk_mm, k_ready, q_ready, v_mm, v_ready = (sem("qk_mm"), sem("k_ready"), sem("q_ready"),
                                                  sem("v_mm"), sem("v_ready"))
        beta_ready = sem("beta_ready")
        VG = NT // 8
        with nc.Block() as block:
            @block.sync
            def _(sp):
                for im in range(B):
                    if im:
                        sp.wait_ge(v_mm, im * VG)
                    sp.dma_start(xb[:, :], XT[:, im * N:(im + 1) * N]).then_inc(x_in, 16)
                    if im == 0:
                        sp.dma_start(w[:, :], t["at0_w"]).then_inc(w_in, 16)
                        sp.dma_start(bias[:, :], t["at0_b"]).then_inc(w_in, 16)
                        sp.dma_start(beta[C:C + 4, :], t["at0_beta"]).then_inc(w_in, 16)
                        sp.dma_start(bv[:, :], t["at0_bv"].broadcast_to([P, C])).then_inc(w_in, 16)
                        sp.wait_ge(zeroed, 2)
                        sp.dma_start(QT[C:C + 4, 0, :], t["at0_table"]).then_inc(table_in, 16)
                        sp.dma_start(KT[C:C + 4, 0, :], t["at0_table"]).then_inc(table_in, 16)

            @block.gpsimd
            def _(pool):
                pool.memset(QT[C:M_ROW, 0, :], 0.0).then_inc(zeroed, 1)
                pool.wait_ge(zeroed, 1)
                pool.memset(KT[C:M_ROW, 0, :], 0.0).then_inc(zeroed, 1)
                pool.wait_ge(zeroed, 2)
                pool.memset(KT[M_ROW:M_ROW + 1, 0, :], 1.0).then_inc(zeroed, 1)
                pool.wait_ge(zeroed, 3)
                pool.memset(V[:, :, :, C:C + 1], 1.0).then_inc(zeroed, 1)

            @block.tensor
            def _(pe):
                pe.wait_ge(w_in, 64)
                pe.wait_ge(zeroed, 4)
                pe.wait_ge(beta_ready, 1)
                with pe.Fori(0, B) as im:
                    pe.wait_ge(x_in, im * 16 + 16)
                    for c in range(NQ):
                        if c >= 2:
                            pe.wait_ge(k_ready, im * NQ + c - 1)
                            pe.wait_ge(q_ready, im * NQ + c - 1)
                        x = xb[:, c * QB:(c + 1) * QB]
                        pe.matmul(exp_ps[c % 2][:, 0, :], w[:, 0:2 * C], x, start=True,
                                  stop=True).then_inc(qk_mm, 1)
                    for g in range(VG):
                        if g >= 2:
                            pe.wait_ge(v_ready, im * VG + g - 1)
                        for k in range(8):
                            j = g * 8 + k
                            mm = pe.matmul(max_ps[g % 2][:, k * C:(k + 1) * C], xb[:, j * P:(j + 1) * P],
                                           w[:, 2 * C:3 * C], start=True, stop=True)
                        mm.then_inc(v_mm, 1)
                    pe.wait_ge(k_ready, im * NQ + NQ)
                    pe.wait_ge(q_ready, im * NQ + NQ)
                    pe.wait_ge(v_ready, im * VG + VG)
                    tensor(pe, im)

            @block.scalar
            def _(act):
                act.wait_ge(w_in, 64)
                with act.Fori(0, B) as im:
                    for c in range(NQ):
                        act.wait_ge(q_ready, im * NQ + c + 1)
                        act.activation(KT[0:C, 0, c * QB:(c + 1) * QB], exp_ps[c % 2][C:2 * C, 0, :],
                                       ACT.Identity, bias=bias[:, 1:2]).then_inc(k_ready, 1)
                    scalar(act, im)

            @block.vector
            def _(dve):
                dve.wait_ge(table_in, 32)
                dve.wait_ge(w_in, 64)
                dve.tensor_scalar(QT[C:C + 4, 0, :], QT[C:C + 4, 0, :], beta[C:C + 4, 0:1], None,
                                  ALU.mult).then_inc(beta_ready, 1)
                with dve.Fori(0, B) as im:
                    for c in range(NQ):
                        dve.wait_ge(qk_mm, im * NQ + c + 1)
                        dve.tensor_scalar(QT[0:C, 0, c * QB:(c + 1) * QB], exp_ps[c % 2][0:C, 0, :],
                                          bias[:, 0:1], C ** -0.5, ALU.add, ALU.mult).then_inc(q_ready, 1)
                    for g in range(VG):
                        dve.wait_ge(v_mm, im * VG + g + 1)
                        dve.tensor_tensor(V[:, g * 8:(g + 1) * 8, 0, 0:C],
                                          max_ps[g % 2][:, :].rearrange("p (k c) -> p k c", c=C),
                                          bv[:, :].unsqueeze(1).broadcast_to([P, 8, C]),
                                          ALU.add).then_inc(v_ready, 1)
                    vector(dve, im)




def attention1_stage(nc, t, U, XT, ident, identb):
    sh = AttentionShape(causal=True, heads=NH)
    HQK = NH + NKV
    GT = 16
    NG = NT // GT
    with ExitStack() as ctx:
        sb = lambda n, s, d=F32: ctx.enter_context(nc.sbuf_tensor("at1_" + n, s, d))
        sem = stage_semaphores(nc, ctx, "at1_")
        QT, KT = sb("QT", [P, NH, N], BF16), sb("KT", [P, NKV, N], BF16)
        V = sb("V", [P, NT, NKV, 32])
        xb = sb("x_image", [C, GT * P])
        w = sb("wqkv", [C, P])
        wo = sb("wo", [P, NH * (C + 1)])
        mask = sb("mask", [P, 2, P], BF16)
        cos, sin = sb("cos", [P, NT, HD // 2]), sb("sin", [P, NT, HD // 2])
        qk = sb("qk", [P, GT, HQK, HD])
        rot = sb("rot", [P, GT, HQK, HD])
        tmp = sb("tmp", [P, GT, HQK, HD // 2])
        part = sb("parts", [P, 3, GT, HQK, HD], BF16)
        QA, KA = sb("QA", [P, GT, NH, 6, HD], BF16), sb("KA", [P, GT, NKV, 6, HD], BF16)
        tensor, scalar, vector, heads_onto_h, head_step, exp_ps, max_ps = attention_core(
            nc, ctx, "at1_", sh, U, ident, identb, QT, KT, V, mask, wo[:, :])
        w_in, x_in, filled = sem("w_in"), sem("x_in"), sem("filled")
        qkv_mm, qk_ready, v_ready, rope = sem("qkv_mm"), sem("qk_ready"), sem("v_ready"), sem("rope")
        parts_ready, qa_ready, ka_ready = sem("parts_ready"), sem("qa_ready"), sem("ka_ready")
        turned, q_out, k_out = sem("turned"), sem("q_out"), sem("k_out")
        CG = GT // SUB
        ROPE_STEPS = 6 + 4
        loads = [(w[:, :], t["at1_w"]), (wo[:, :], t["at1_wo"]), (cos[:, :, :], t["at1_cos"]),
                 (sin[:, :, :], t["at1_sin"]), (mask[:, :, :], t["causal_mask"])]
        q_slots, k_slots = ((0, 1, 4), (2, 3), (5,)), ((0, 2, 5), (1, 3), (4,))

        def spread(copy, slots, dst, src_heads, done):
            for p, slots_of_part in enumerate(slots):
                for s in slots_of_part:
                    ins = copy(dst[:, :, :, s, :], part[:, p, :, src_heads, :])
            ins.then_inc(done, 1)

        with nc.Block() as block:
            @block.sync
            def _(sp):
                for n in range(B * NG):
                    if n:
                        sp.wait_ge(qkv_mm, n * CG)
                    sp.dma_start(xb[:, :], XT[:, n * GT * P:(n + 1) * GT * P]).then_inc(x_in, 16)
                    if n == 0:
                        for dst, src in loads:
                            sp.dma_start(dst, src).then_inc(w_in, 16)

            @block.gpsimd
            def _(pool):
                pool.memset(V[:, :, :, HD:32], 0.0).then_inc(filled, 1)
                pool.wait_ge(filled, 1)
                pool.memset(V[:, :, :, HD:HD + 1], 1.0).then_inc(filled, 1)
                pool.wait_ge(filled, 2)
                pool.memset(KT[M_ROW:M_ROW + sh.m_rows, :, :], 1.0).then_inc(filled, 1)
                pool.wait_ge(filled, 3)
                with pool.Fori(0, B) as im:
                    heads_onto_h(pool, im)

            @block.tensor
            def _(pe):
                pe.wait_ge(w_in, 16 * len(loads))
                pe.wait_ge(filled, 3)
                with pe.Fori(0, B) as im:
                    for g in range(NG):
                        pe.wait_ge(x_in, (im * NG + g) * 16 + 16)
                        for c in range(CG):
                            if c >= 2:
                                n = im * NG * CG + (g * CG + c - 1)
                                pe.wait_ge(qk_ready, n)
                                pe.wait_ge(v_ready, n)
                            for i in range(SUB):
                                k = c * SUB + i
                                mm = pe.matmul(max_ps[c % 2][:, i * P:(i + 1) * P], xb[:, k * P:(k + 1) * P],
                                               w[:, :], start=True, stop=True)
                            mm.then_inc(qkv_mm, 1)
                        pe.wait_ge(qa_ready, im * NG + g + 1)
                        pe.wait_ge(ka_ready, im * NG + g + 1)
                        for c in range(CG):
                            n = im * NG * CG + (g * CG + c)
                            if c:
                                pe.wait_ge(q_out, n)
                            dst = exp_ps[0][:, :, :].rearrange("p a q -> p (a q)").bitcast(BF16)
                            for h in range(NH):
                                for i in range(SUB):
                                    mm = pe.transpose(dst[0:M_ROW, (h * SUB + i) * P:(h * SUB + i + 1) * P],
                                                      QA[:, c * SUB + i, h, :, :].rearrange("p s d -> p (s d)"),
                                                      identb[:, :])
                            mm.then_inc(turned, 1)
                            if c:
                                pe.wait_ge(k_out, n)
                            dst = exp_ps[1][:, 0, :].bitcast(BF16)
                            for h in range(NKV):
                                for i in range(SUB):
                                    mm = pe.transpose(dst[0:M_ROW, (h * SUB + i) * P:(h * SUB + i + 1) * P],
                                                      KA[:, c * SUB + i, h, :, :].rearrange("p s d -> p (s d)"),
                                                      identb[:, :])
                            mm.then_inc(turned, 1)
                    pe.wait_ge(q_out, im * NG * CG + NG * CG)
                    pe.wait_ge(k_out, im * NG * CG + NG * CG)
                    pe.wait_ge(v_ready, im * NG * CG + NG * CG)
                    tensor(pe, im)

            @block.scalar
            def _(act):
                with act.Fori(0, B) as im:
                    for g in range(NG):
                        for c in range(CG):
                            act.wait_ge(qkv_mm, im * NG * CG + (g * CG + c + 1))
                            src = max_ps[c % 2][:, :].rearrange("p (i h d) -> p i h d", i=SUB, d=HD)
                            tiles = slice(c * SUB, (c + 1) * SUB)
                            if c == 0 and g:
                                act.wait_ge(parts_ready, im * NG + g)
                            act.activation(qk[:, tiles, 0:NH, :], src[:, :, 0:NH, :], ACT.Copy, scale=HD ** -0.5)
                            act.activation(qk[:, tiles, NH:HQK, :], src[:, :, NH:HQK, :],
                                           ACT.Copy).then_inc(qk_ready, 1)
                            act.activation(V[:, g * GT + c * SUB:g * GT + (c + 1) * SUB, :, 0:HD],
                                           src[:, :, HQK:HQK + NKV, :], ACT.Copy).then_inc(v_ready, 1)
                        act.wait_ge(parts_ready, im * NG + g + 1)
                        if g:
                            act.wait_ge(turned, (im * NG + g) * 2 * CG)
                        spread(lambda o, i: act.activation(o, i, ACT.Copy), q_slots, QA, slice(0, NH), qa_ready)
                        for c in range(CG):
                            n = im * NG * CG + (g * CG + c)
                            act.wait_ge(turned, n * 2 + 1)
                            q0 = (g * CG + c) * QB
                            act.activation(QT[0:M_ROW, :, q0:q0 + QB],
                                           exp_ps[0][0:M_ROW, :, :].rearrange("p a q -> p (a q)").bitcast(BF16)
                                           .rearrange("p (h q) -> p h q", h=NH), ACT.Copy).then_inc(q_out, 1)
                    scalar(act, im)

            @block.vector
            def _(dve):
                dve.wait_ge(w_in, 16 * len(loads))
                half = HD // 2
                dve.sem_inc(head_step, 6)
                with dve.Fori(0, B) as im:
                    for g in range(NG):
                        dve.wait_ge(qk_ready, im * NG * CG + (g + 1) * CG)
                        tiles = slice(g * GT, (g + 1) * GT)
                        table = lambda x: x[:, tiles, :].unsqueeze(2).broadcast_to([P, GT, HQK, half])
                        lo, hi = qk[:, :, :, 0:half], qk[:, :, :, half:HD]
                        rlo, rhi = rot[:, :, :, 0:half], rot[:, :, :, half:HD]
                        own = 0

                        def step(ins):
                            nonlocal own
                            ins.then_inc(rope, 1)
                            own += 1
                            dve.wait_ge(rope, (im * NG + g) * ROPE_STEPS + own)

                        step(dve.tensor_tensor(rlo, lo, table(cos), ALU.mult))
                        step(dve.tensor_tensor(tmp[:, :, :, :], hi, table(sin), ALU.mult))
                        step(dve.tensor_tensor(rlo, rlo, tmp[:, :, :, :], ALU.subtract))
                        step(dve.tensor_tensor(rhi, hi, table(cos), ALU.mult))
                        step(dve.tensor_tensor(tmp[:, :, :, :], lo, table(sin), ALU.mult))
                        step(dve.tensor_tensor(rhi, rhi, tmp[:, :, :, :], ALU.add))
                        if g:
                            dve.wait_ge(qa_ready, im * NG + g)
                            dve.wait_ge(ka_ready, im * NG + g)
                        r = rot[:, :, :, :]
                        step(dve.tensor_copy(part[:, 0, :, :, :], r))
                        step(dve.tensor_tensor(r, r, part[:, 0, :, :, :], ALU.subtract))
                        step(dve.tensor_copy(part[:, 1, :, :, :], r))
                        step(dve.tensor_tensor(r, r, part[:, 1, :, :, :], ALU.subtract))
                        dve.tensor_copy(part[:, 2, :, :, :], r).then_inc(parts_ready, 1)
                        dve.wait_ge(parts_ready, im * NG + g + 1)
                        if g:
                            dve.wait_ge(turned, (im * NG + g) * 2 * CG)
                        spread(dve.tensor_copy, k_slots, KA, slice(NH, HQK), ka_ready)
                        for c in range(CG):
                            n = im * NG * CG + (g * CG + c)
                            dve.wait_ge(turned, n * 2 + 2)
                            q0 = (g * CG + c) * QB
                            dve.tensor_copy(KT[0:M_ROW, :, q0:q0 + QB],
                                            exp_ps[1][0:M_ROW, 0, :].bitcast(BF16)
                                            .rearrange("p (h q) -> p h q", h=NKV)).then_inc(k_out, 1)
                    vector(dve, im)


def split_weights_stage(nc, name, sets):
    with ExitStack() as ctx:
        sem = stage_semaphores(nc, ctx, name)
        most = max(src.shape[1] for src, _ in sets)
        whole = ctx.enter_context(nc.sbuf_tensor(name + "w_whole", [2 * C, len(sets), most], F32))
        rest = ctx.enter_context(nc.sbuf_tensor(name + "w_rest", [2 * C, len(sets), most], F32))
        loaded = [sem(f"w_loaded{n}") for n in range(len(sets))]
        high, left, middle, low = sem("w_high"), sem("w_left"), sem("w_middle"), sem("w_low")
        upper, lower = slice(0, C), slice(C, 2 * C)
        with nc.Block() as block:
            @block.sync
            def _(sp):
                for n, (src, _) in enumerate(sets):
                    for rows in (upper, lower):
                        sp.dma_start(whole[rows, n, 0:src.shape[1]], src).then_inc(loaded[n], 16)

            @block.scalar
            def _(act):
                for n, (src, (hh, mm, lh)) in enumerate(sets):
                    k = src.shape[1]
                    act.wait_ge(loaded[n], 32)
                    act.activation(hh[:, 0:k], whole[:, n, 0:k], ACT.Copy).then_inc(high, 1)
                for n, (src, (hh, mm, lh)) in enumerate(sets):
                    k = src.shape[1]
                    act.wait_ge(left, n + 1)
                    act.activation(mm[:, 0:k], rest[:, n, 0:k], ACT.Copy).then_inc(middle, 1)
                act.wait_ge(middle, len(sets))

            @block.vector
            def _(dve):
                for n, (src, (hh, mm, lh)) in enumerate(sets):
                    k = src.shape[1]
                    dve.wait_ge(high, n + 1)
                    dve.tensor_tensor(rest[:, n, 0:k], whole[:, n, 0:k], hh[:, 0:k],
                                      ALU.subtract).then_inc(left, 1)
                    dve.tensor_copy(lh[lower, 0:k], hh[lower, 0:k]).then_inc(low, 1)
                for n, (src, (hh, mm, lh)) in enumerate(sets):
                    k = src.shape[1]
                    dve.wait_ge(middle, n + 1)
                    dve.tensor_tensor(lh[upper, 0:k], rest[upper, n, 0:k], mm[upper, 0:k],
                                      ALU.subtract).then_inc(low, 1)
                dve.wait_ge(low, 2 * len(sets))


def hidden_plan(experts, size):
    plan, blocks = [], 0
    for k in range(-(-experts * size // P)):
        touched = range(k * P // size, min(experts, -(-(k + 1) * P // size)))
        plan.append([(e, blocks + i, e * size >= k * P, (e + 1) * size <= (k + 1) * P)
                     for i, e in enumerate(touched)])
        blocks += len(touched)
    return plan, blocks


def moe_stage(nc, name, t, H, parts, ident, size, shared, gated, denom_eps):
    E = NE + shared
    NB = T * P // QB
    plan, w2_blocks = hidden_plan(E, size)
    HT = len(plan)
    UP, HB, LAG = (2, 4, 2) if gated else (3, 6, 3)
    last_mix = 4 + shared
    with ExitStack() as ctx:
        sb = lambda n, s, d=F32: ctx.enter_context(nc.sbuf_tensor(name + n, s, d))
        ps = lambda n, s, d=F32: ctx.enter_context(nc.psum_tensor(name + n, s, d))
        sem = stage_semaphores(nc, ctx, name)
        meets = (0, 0, 1)
        wr = [sb(f"router{i}", [P, NE], BF16) for i in range(3)]
        w1 = [sb(f"w1_{i}", [P, HT * P], BF16) for i in range(3)]
        w3 = [sb(f"w3_{i}", [P, HT * P], BF16) for i in range(3)] if gated else None
        w2 = sb("w2", [P, w2_blocks, C])
        b1 = None if gated else sb("b1", [P, HT])
        b2 = None if gated else sb("b2", [E, C])
        rank = sb("rank", [P, NE])
        gate = sb("gate", [P, T, E])
        g = {n: sb("g_" + n, [P, T, NE]) for n in ("p", "eq", "oh", "p2")}
        col = sb("cols", [P, 4, T])
        gate_t = sb("gate_t", [E, T * P]) if shared else None
        gate_b = sb("gate_b", [E, QB]) if shared else None
        shared_out = sb("shared_out", [P, SUB, C]) if shared else None
        act_out = sb("act_out", [P, 2, QB]) if gated else None
        hid = sb("hidden", [P, HB, QB])
        weighted = sb("weighted", [P, SUB, NE, C])
        up = [ps(f"up{i}", [P, 2 if gated else 1, QB]) for i in range(UP)]
        down = [ps(f"down{i}", [P, NE, C]) for i in range(SUB)]
        sh_ps = ps("shared_ps", [P, SUB, C]) if shared else None
        rank_in, w_in, logits_mm = sem("rank_in"), sem("w_in"), sem("logits_mm")
        gate_step, exp_ready = sem("gate_step"), sem("exp_ready")
        gate_turned, gate_out, gate_b_ready = sem("gate_turned"), sem("gate_out"), sem("gate_b_ready")
        up_mm, act_done, hid_ready = sem("up_mm"), sem("act_done"), sem("hid_ready")
        down_mm, down_done, down_read = sem("down_mm"), sem("down_done"), sem("down_read")
        sh_done, sh_read, mix_step = sem("sh_done"), sem("sh_read"), sem("mix_step")
        loads = [(w2[:, :, :], "w2")]
        loads += [] if gated else [(b1[:, :], "b1"), (b2[:, :], "b2")]
        split_weights_stage(nc, name, [(t[name + "router"], wr), (t[name + "w1"], w1)]
                            + ([(t[name + "w3"], w3)] if gated else []))
        gate_steps = 22
        TURNS = T // SUB

        with nc.Block() as block:
            @block.sync
            def _(sp):
                sp.dma_start(rank[:, :], t["rank"].broadcast_to([P, NE])).then_inc(rank_in, 16)
                for dst, src in loads:
                    sp.dma_start(dst, t[name + src]).then_inc(w_in, 16)
                if shared:
                    sp.wait_ge(gate_out, TURNS)
                    with sp.Fori(0, NB) as nb:
                        sp.wait_ge(sh_done, nb + 1)
                        sp.dma_start(gate_b[:, :], gate_t[:, bass.ds(nb * QB, QB)]).then_inc(gate_b_ready, 16)

            @block.tensor
            def _(pe):
                for j in range(T):
                    for i in range(3):
                        mm = pe.matmul(down[0][:, :, :].rearrange("p e c -> p (e c)")[:, j * NE:(j + 1) * NE],
                                       parts[meets[i]][:, j * P:(j + 1) * P], wr[i][:, :],
                                       start=(i == 0), stop=(i == 2))
                mm.then_inc(logits_mm, 1)
                pe.wait_ge(w_in, 16 * len(loads))
                if shared:
                    pe.wait_ge(gate_step, gate_steps)
                    for n in range(TURNS):
                        if n >= 2:
                            pe.wait_ge(gate_out, n - 1)
                        for i in range(SUB):
                            mm = pe.transpose(up[n % 2][0:E, 0, i * P:(i + 1) * P],
                                              gate[:, n * SUB + i, :], ident[:, :])
                        mm.then_inc(gate_turned, 1)
                    pe.wait_ge(gate_out, TURNS)
                with pe.Fori(0, NB) as nb:
                    def up_products(k):
                        if k >= UP:
                            pe.wait_ge(hid_ready, nb * HT + k - UP + 1)
                        for a, w in enumerate([w1, w3] if gated else [w1]):
                            for i in range(3):
                                mm = pe.matmul(up[k % UP][:, a, :], w[i][:, k * P:(k + 1) * P],
                                               parts[meets[i]][:, bass.ds(nb * QB, QB)],
                                               start=(i == 0), stop=(i == 2))
                        mm.then_inc(up_mm, 1)

                    def down_products(tiles):
                        pe.wait_ge(hid_ready, nb * HT + tiles[-1] + 1)
                        if shared and tiles[0] == 0:
                            pe.wait_ge(sh_read, nb + 1)
                            pe.wait_ge(gate_b_ready, nb * 16 + 16)
                        for s in range(SUB):
                            for k in tiles:
                                for e, block_no, opens, closes in plan[k]:
                                    if opens and e == shared:
                                        pe.wait_ge(down_read, nb * SUB + s + 1)
                                    is_shared = e < shared
                                    out = sh_ps[:, s, :] if is_shared else down[s][:, e - shared, :]
                                    mm = pe.matmul(out, hid[:, k % HB, s * P:(s + 1) * P], w2[:, block_no, :],
                                                   start=opens, stop=closes and not is_shared)
                                    if is_shared and closes:
                                        mm = pe.matmul(out, gate_b[:, s * P:(s + 1) * P], b2[:, :],
                                                       start=False, stop=True)
                            if is_shared and s == SUB - 1:
                                mm.then_inc(sh_done, 1)
                            elif tiles[-1] == HT - 1:
                                mm.then_inc(down_done, 1)
                            elif s == SUB - 1:
                                mm.then_inc(down_mm, len(tiles))

                    for k in range(HT + LAG):
                        if k < HT:
                            up_products(k)
                        if shared and k - LAG < 2:
                            if k - LAG == 1:
                                down_products([0, 1])
                        elif k >= LAG:
                            down_products([k - LAG])

            def hidden_free(eng, nb, k):
                if shared and HB <= k < HB + 2:
                    eng.wait_ge(sh_done, nb + 2)
                elif k >= HB:
                    eng.wait_ge(down_mm, nb * (HT - 1 - 2 * shared) + k - HB + 1 - 2 * shared)

            @block.scalar
            def _(act):
                act.wait_ge(gate_step, 2)
                act.activation(g["p"][:, :, :], g["p"][:, :, :], ACT.Exp).then_inc(exp_ready, 1)
                if shared:
                    for n in range(TURNS):
                        act.wait_ge(gate_turned, n + 1)
                        act.activation(gate_t[:, n * QB:(n + 1) * QB], up[n % 2][0:E, 0, :],
                                       ACT.Copy).then_inc(gate_out, 1)
                with act.Fori(0, NB) as nb:
                    for k in range(HT):
                        act.wait_ge(up_mm, nb * HT + k + 1)
                        if gated:
                            if k >= 2:
                                act.wait_ge(hid_ready, nb * HT + k - 1)
                            act.activation(act_out[:, k % 2, :], up[k % UP][:, 0, :], ACT.Silu).then_inc(act_done, 1)
                        else:
                            hidden_free(act, nb, k)
                            act.activation(hid[:, k % HB, :], up[k % UP][:, 0, :], ACT.Gelu,
                                           bias=b1[:, k:k + 1]).then_inc(hid_ready, 1)

            @block.gpsimd
            def _(pool):
                with pool.Fori(0, NB) as nb:
                    w = lambda i, n: weighted[:, :, i:i + n, :]
                    blk = bass.ds(nb * SUB, SUB)
                    pool.wait_ge(down_read, nb * SUB + 2 * SUB)
                    pool.tensor_tensor(w(0, 4), w(0, 4), w(4, 4), ALU.add).then_inc(mix_step, 1)
                    pool.wait_ge(mix_step, nb * last_mix + 2)
                    pool.tensor_tensor(w(0, 2), w(0, 2), w(2, 2), ALU.add).then_inc(mix_step, 1)
                    pool.wait_ge(mix_step, nb * last_mix + 3)
                    pool.tensor_tensor(weighted[:, :, 0, :], weighted[:, :, 0, :], weighted[:, :, 1, :],
                                       ALU.add).then_inc(mix_step, 1)
                    pool.wait_ge(mix_step, nb * last_mix + 4)
                    if shared:
                        pool.wait_ge(sh_read, nb + 2)
                        pool.tensor_tensor(weighted[:, :, 0, :], weighted[:, :, 0, :], shared_out[:, :, :],
                                           ALU.add).then_inc(mix_step, 1)
                        pool.wait_ge(mix_step, nb * last_mix + 5)
                    pool.tensor_tensor(H[:, blk, :], H[:, blk, :], weighted[:, :, 0, :],
                                       ALU.add).then_inc(mix_step, 1)

            @block.vector
            def _(dve):
                own = 0

                def step(ins):
                    nonlocal own
                    ins.then_inc(gate_step, 1)
                    own += 1
                    dve.wait_ge(gate_step, own)

                wide = lambda a: a.unsqueeze(2).broadcast_to([P, T, NE])
                p, eq, oh, p2 = (g[n][:, :, :] for n in ("p", "eq", "oh", "p2"))
                c = [col[:, i, :] for i in range(4)]
                ranks = rank[:, :].unsqueeze(1).broadcast_to([P, T, NE])
                dve.wait_ge(logits_mm, 1)
                logits = down[0][:, :, :].rearrange("p e c -> p (e c)").rearrange("p (t e) -> p t e", e=NE)
                step(dve.tensor_reduce(c[0], logits, AX.X, ALU.max))
                step(dve.tensor_tensor(p, logits, wide(c[0]), ALU.subtract))
                dve.wait_ge(exp_ready, 1)
                step(dve.tensor_reduce(c[0], p, AX.X, ALU.add))
                step(dve.reciprocal(c[1], c[0]))
                step(dve.tensor_tensor(p, p, wide(c[1]), ALU.mult))

                def first_max(src, largest):
                    step(dve.tensor_reduce(c[largest], src, AX.X, ALU.max))
                    step(dve.tensor_tensor(eq, src, wide(c[largest]), ALU.is_equal))
                    step(dve.tensor_tensor(eq, eq, ranks, ALU.mult))
                    step(dve.tensor_reduce(c[3], eq, AX.X, ALU.max))

                dve.wait_ge(rank_in, 16)
                first_max(p, 0)
                step(dve.tensor_tensor(oh, eq, wide(c[3]), ALU.is_equal))
                step(dve.scalar_tensor_tensor(out=p2, in0=oh, scalar=-2.0, in1=p, op0=ALU.mult, op1=ALU.add))
                first_max(p2, 1)
                step(dve.tensor_tensor(eq, eq, wide(c[3]), ALU.is_equal))
                step(dve.tensor_tensor(oh, oh, eq, ALU.add))
                step(dve.tensor_tensor(c[2], c[0], c[1], ALU.add))
                if denom_eps:
                    step(dve.tensor_scalar(c[2], c[2], denom_eps, None, ALU.add))
                step(dve.reciprocal(c[3], c[2]))
                step(dve.tensor_tensor(p, p, wide(c[3]), ALU.mult))
                if shared:
                    step(dve.memset(gate[:, :, NE:E], 1.0))
                step(dve.tensor_tensor(gate[:, :, 0:NE], p, oh, ALU.mult))
                assert own == gate_steps, own

                dve.sem_inc(down_read, SUB)
                dve.sem_inc(mix_step, 1)
                if shared:
                    dve.sem_inc(sh_done, 1)
                    dve.sem_inc(sh_read, 1)
                with dve.Fori(0, NB) as nb:
                    if gated:
                        for k in range(HT):
                            dve.wait_ge(act_done, nb * HT + k + 1)
                            hidden_free(dve, nb, k)
                            dve.tensor_tensor(hid[:, k % HB, :], act_out[:, k % 2, :], up[k % UP][:, 1, :],
                                              ALU.mult).then_inc(hid_ready, 1)
                    dve.wait_ge(mix_step, nb * last_mix + 1)
                    if shared:
                        dve.wait_ge(sh_done, nb + 2)
                        dve.tensor_copy(shared_out[:, :, :], sh_ps[:, :, :]).then_inc(sh_read, 1)
                    for s in range(SUB):
                        dve.wait_ge(down_done, nb * SUB + s + 1)
                        dve.tensor_tensor(weighted[:, s, :, :], down[s][:, :, :],
                                          gate[:, bass.ds(nb * SUB + s, 1), 0:NE]
                                          .rearrange("p t e -> p (t e)").unsqueeze(2)
                                          .broadcast_to([P, NE, C]), ALU.mult).then_inc(down_read, 1)


def linear_attention_stage(nc, t, H, XT):
    NBL = 2 * NQ
    with ExitStack() as ctx:
        sb = lambda n, s, d=F32: ctx.enter_context(nc.sbuf_tensor("lin_" + n, s, d))
        ps = lambda n, s, d=F32: ctx.enter_context(nc.psum_tensor("lin_" + n, s, d))
        sem = stage_semaphores(nc, ctx, "lin_")
        w = sb("w", [C, 3 * C])
        b_qk = sb("b_qk", [C, 2])
        b_kv = sb("b_kv", [P, 2 * C])
        decay = sb("decay", [P, P])
        q_decay = sb("q_decay", [C, P])
        k_decay = sb("k_decay", [P, 1])
        q_t, k_t, qd_t = (sb(n, [C, 2, QB]) for n in ("q_t", "k_t", "qd_t"))
        kv = sb("kv", [P, 2, SUB, 2 * C])
        kd = sb("kd", [P, 2, SUB, C])
        pr = sb("probs", [P, 2, SUB, P])
        state = sb("state", [C, B, NT + 1, C])
        qk_ps, kv_ps = ps("qk_ps", [C, 2, QB]), ps("kv_ps", [P, SUB, 2 * C])
        sc_ps, st_ps, out_ps = ps("sc_ps", [P, SUB, P]), ps("st_ps", [C, SUB, C]), ps("out_ps", [P, SUB, C])
        w_in, proj, q_ready, k_ready, kv_ready, kd_ready, qd_ready = (
            sem(n) for n in ("w_in", "proj", "q_ready", "k_ready", "kv_ready", "kd_ready", "qd_ready"))
        scored, pr_ready, st_mm, st_ready, out_mm, out_read, zeroed = (
            sem(n) for n in ("scored", "pr_ready", "st_mm", "st_ready", "out_mm", "out_read", "zeroed"))
        loads = [(w[:, :], t["lin_w"]), (b_qk[:, :], t["lin_b_qk"]), (b_kv[:, :], t["lin_b_kv"].broadcast_to([P, 2 * C])),
                 (decay[:, :], t["lin_decay"]), (q_decay[:, :], t["lin_q_decay"].broadcast_to([C, P])),
                 (k_decay[:, :], t["lin_k_decay"])]
        first = lambda n: (n % B) * N + (n // B) * QB

        with nc.Block() as block:
            @block.sync
            def _(sp):
                for dst, src in loads:
                    sp.dma_start(dst, src).then_inc(w_in, 16)

            @block.tensor
            def _(pe):
                pe.wait_ge(w_in, 16 * len(loads))
                for n in range(NBL + 2):
                    if n < NBL:
                        if n:
                            pe.wait_ge(q_ready, n)
                            pe.wait_ge(k_ready, n)
                            pe.wait_ge(kv_ready, n)
                        x = XT[:, first(n):first(n) + QB]
                        pe.matmul(qk_ps[:, 0, :], w[:, 0:C], x, start=True, stop=True)
                        pe.matmul(qk_ps[:, 1, :], w[:, C:2 * C], x, start=True, stop=True)
                        for i in range(SUB):
                            mm = pe.matmul(kv_ps[:, i, :], x[:, i * P:(i + 1) * P], w[:, C:3 * C],
                                           start=True, stop=True)
                        mm.then_inc(proj, 1)
                    if 1 <= n <= NBL:
                        m = n - 1
                        pe.wait_ge(q_ready, m + 1)
                        pe.wait_ge(k_ready, m + 1)
                        if m:
                            pe.wait_ge(pr_ready, m)
                            pe.wait_ge(st_ready, m)
                        for i in range(SUB):
                            mm = pe.matmul(sc_ps[:, i, :], k_t[:, m % 2, i * P:(i + 1) * P],
                                           q_t[:, m % 2, i * P:(i + 1) * P], start=True, stop=True)
                        mm.then_inc(scored, 1)
                        pe.wait_ge(kd_ready, m + 1)
                        for i in range(SUB):
                            mm = pe.matmul(st_ps[:, i, :], kd[:, m % 2, i, :], kv[:, m % 2, i, C:2 * C],
                                           start=True, stop=True)
                        mm.then_inc(st_mm, 1)
                    if n >= 2:
                        m = n - 2
                        pe.wait_ge(pr_ready, m + 1)
                        pe.wait_ge(st_ready, m + 1)
                        pe.wait_ge(qd_ready, m + 1)
                        if m:
                            pe.wait_ge(out_read, m)
                        for i in range(SUB):
                            pe.matmul(out_ps[:, i, :], pr[:, m % 2, i, :], kv[:, m % 2, i, C:2 * C],
                                      start=True, stop=False)
                            mm = pe.matmul(out_ps[:, i, :], qd_t[:, m % 2, i * P:(i + 1) * P],
                                           state[:, m % B, (m // B) * SUB + i, :], start=False, stop=True)
                        mm.then_inc(out_mm, 1)

            @block.scalar
            def _(act):
                act.wait_ge(w_in, 16 * len(loads))
                for n in range(NBL):
                    act.wait_ge(proj, n + 1)
                    if n >= 2:
                        act.wait_ge(scored, n - 1)
                    act.activation(k_t[:, n % 2, :], qk_ps[:, 1, :], ACT.Identity,
                                   bias=b_qk[:, 1:2]).then_inc(k_ready, 1)
                    act.wait_ge(kv_ready, n + 1)
                    if n >= 2:
                        act.wait_ge(st_mm, n - 1)
                    act.activation(kd[:, n % 2, :, :], kv[:, n % 2, :, 0:C], ACT.Copy,
                                   scale=k_decay[:, 0:1]).then_inc(kd_ready, 1)

            @block.vector
            def _(dve):
                dve.memset(state[:, :, 0, :], 0.0).then_inc(zeroed, 1)
                dve.wait_ge(zeroed, 1)
                dve.wait_ge(w_in, 16 * len(loads))
                for n in range(NBL + 2):
                    if n < NBL:
                        dve.wait_ge(proj, n + 1)
                        if n >= 2:
                            dve.wait_ge(out_mm, n - 1)
                        dve.tensor_scalar(q_t[:, n % 2, :], qk_ps[:, 0, :], b_qk[:, 0:1], C ** -0.5, ALU.add,
                                          ALU.mult).then_inc(q_ready, 1)
                        dve.tensor_tensor(kv[:, n % 2, :, :], kv_ps[:, :, :],
                                          b_kv[:, :].unsqueeze(1).broadcast_to([P, SUB, 2 * C]),
                                          ALU.add).then_inc(kv_ready, 1)
                        dve.wait_ge(q_ready, n + 1)
                        dve.tensor_tensor(qd_t[:, n % 2, :].rearrange("c (i q) -> c i q", i=SUB),
                                          q_t[:, n % 2, :].rearrange("c (i q) -> c i q", i=SUB),
                                          q_decay[:, :].unsqueeze(1).broadcast_to([C, SUB, P]),
                                          ALU.mult).then_inc(qd_ready, 1)
                    if 1 <= n <= NBL:
                        m = n - 1
                        dve.wait_ge(scored, m + 1)
                        dve.tensor_tensor(pr[:, m % 2, :, :], sc_ps[:, :, :],
                                          decay[:, :].unsqueeze(1).broadcast_to([P, SUB, P]),
                                          ALU.mult).then_inc(pr_ready, 1)
                        dve.wait_ge(st_mm, m + 1)
                        for i in range(SUB):
                            c = (m // B) * SUB + i
                            ins = dve.scalar_tensor_tensor(out=state[:, m % B, c + 1, :], in0=state[:, m % B, c, :],
                                                           scalar=float(ALPHA ** P), in1=st_ps[:, i, :],
                                                           op0=ALU.mult, op1=ALU.add)
                            if i < SUB - 1:
                                ins.then_inc(zeroed, 1)
                                dve.wait_ge(zeroed, m * (SUB - 1) + i + 2)
                        ins.then_inc(st_ready, 1)
                    if n >= 2:
                        m = n - 2
                        dve.wait_ge(out_mm, m + 1)
                        tile = first(m) // P
                        dve.tensor_tensor(H[:, tile:tile + SUB, :], H[:, tile:tile + SUB, :], out_ps[:, :, :],
                                          ALU.add).then_inc(out_read, 1)


def tower(nc, t, out, stages=99, only=None):
    with ExitStack() as ctx:
        sb = lambda n, s, d=F32: ctx.enter_context(nc.sbuf_tensor(n, s, d))
        H = sb("H", [P, T, C])
        ident = sb("ident", [P, P])
        identb = sb("identb", [P, P], BF16)
        in_sem = ctx.enter_context(nc.semaphore("ident_in"))
        cast_sem = ctx.enter_context(nc.semaphore("ident_cast"))
        out_sem = ctx.enter_context(nc.semaphore("out_written"))
        with nc.Block() as block:
            @block.sync
            def _(sp):
                sp.dma_start(ident[:, :], t["ident"]).then_inc(in_sem, 16)
                if only is not None:
                    sp.dma_start(H[:, :, :].rearrange("p t f -> p (t f)"), t["h_in"]).then_inc(out_sem, 16)
                    sp.wait_ge(out_sem, 16)
            @block.vector
            def _(dve):
                dve.wait_ge(in_sem, 16)
                dve.tensor_copy(identb[:, :], ident[:, :]).then_inc(cast_sem, 1)
                dve.wait_ge(cast_sem, 1)
        def run(n):
            return stages >= n and (only is None or only + 2 == n)
        if only is None:
            involution_stage(nc, t, H)
        if run(2):
            with ExitStack() as c2:
                XT = c2.enter_context(nc.sbuf_tensor("XT", [C, T * P], F32))
                norm_stage(nc, "ln1_", H, XT, ident, True, 1e-5)
                attention0_stage(nc, t, H, XT, ident, identb)
        if run(3):
            with ExitStack() as c2:
                XT = [c2.enter_context(nc.sbuf_tensor(f"XT2_{i}", [P, T * P], BF16)) for i in range(2)]
                norm_stage(nc, "ln2_", H, None, ident, True, 1e-5, parts=XT)
                moe_stage(nc, "moe0_", t, H, XT, ident, F0, 1, False, 0.0)
        if run(4):
            with ExitStack() as c2:
                XT = c2.enter_context(nc.sbuf_tensor("XT3", [C, T * P], F32))
                norm_stage(nc, "ln3_", H, XT, ident, True, 1e-5)
                linear_attention_stage(nc, t, H, XT)
        if run(5):
            final_stages(nc, t, H, ident, identb, out)
        else:
            with nc.Block() as block:
                @block.sync
                def _(sp):
                    sp.dma_start(out, H[:, :, :].rearrange("p t f -> p (t f)")).then_inc(in_sem, 16)
                    sp.wait_ge(in_sem, 32)


def final_stages(nc, t, H, ident, identb, out):
    flat = lambda x: x[:, :, :].rearrange("p t f -> p (t f)")
    with ExitStack() as ctx:
        U = ctx.enter_context(nc.sbuf_tensor("U", [P, T, C], F32))
        gains = ctx.enter_context(nc.sbuf_tensor("gains", [C, 2], F32))
        gains_in, h_out, h_in, summed, u_out = (
            ctx.enter_context(nc.semaphore(n)) for n in ("gains_in", "h_out", "h_in", "summed", "u_out"))
        norm_stage(nc, "ln4_", H, None, ident, True, 1e-5, U=U)
        with nc.Block() as block:
            @block.sync
            def _(sp):
                sp.dma_start(t["h_dram"], flat(H)).then_inc(h_out, 16)
                sp.dma_start(gains[:, :], t["gains"]).then_inc(gains_in, 16)
                sp.wait_ge(h_out, 16)
                sp.wait_ge(gains_in, 16)
        with ExitStack() as c2:
            XT = c2.enter_context(nc.sbuf_tensor("XT4", [C, T * P], F32))
            norm_stage(nc, "rms1_", U, XT, ident, False, 1e-6, gain=gains[:, 0:1])
            attention1_stage(nc, t, U, XT, ident, identb)
        with ExitStack() as c2:
            XT = [c2.enter_context(nc.sbuf_tensor(f"XT5_{i}", [P, T * P], BF16)) for i in range(2)]
            norm_stage(nc, "rms2_", U, None, ident, False, 1e-6, gain=gains[:, 1:2], parts=XT)
            moe_stage(nc, "moe1_", t, U, XT, ident, F1, 0, True, 1e-9)
        with nc.Block() as block:
            @block.sync
            def _(sp):
                sp.dma_start(flat(H), t["h_dram"]).then_inc(h_in, 16)
                sp.wait_ge(summed, 1)
                sp.dma_start(out, flat(U)).then_inc(u_out, 16)
                sp.wait_ge(u_out, 16)

            @block.vector
            def _(dve):
                dve.wait_ge(h_in, 16)
                dve.tensor_tensor(flat(U), flat(U), flat(H), ALU.add).then_inc(summed, 1)


def bias_table():
    n = np.arange(N, dtype=np.float64)
    return np.stack([f(2 * np.pi * n / period) for period in (24.0, 720.0) for f in (np.cos, np.sin)]
                    ).astype(np.float32)


def decay_tables():
    n = np.arange(P, dtype=np.float64)
    between = n[None, :] - n[:, None]
    return {"lin_decay": np.where(between >= 0, ALPHA ** np.maximum(between, 0), 0.0).astype(np.float32),
            "lin_q_decay": (ALPHA ** (n + 1)).astype(np.float32)[None],
            "lin_k_decay": (ALPHA ** (P - 1 - n)).astype(np.float32)[:, None]}


def rotary_tables():
    inv = 1.0 / 10000.0 ** (np.arange(0, HD, 2, dtype=np.float32) / HD)
    angle = np.outer(np.arange(N, dtype=np.float32), inv).reshape(NT, P, HD // 2).transpose(1, 0, 2)
    return {"at1_cos": np.cos(angle), "at1_sin": np.sin(angle)}


def causal_masks():
    n = np.arange(P)
    after = (n[None, :] > n[:, None]) * np.float32(NEG)
    return np.stack([after, after.T], 1).astype(mybir.dt.np(BF16))


def output_rows(wo):
    a = np.zeros((NH, 32, NH, C + 1), np.float32)
    for h in range(NH):
        a[h, :HD, h, :C] = wo[:, h * HD:(h + 1) * HD].T
        a[h, HD, h, C] = 1
    return a.reshape(P, NH * (C + 1))


def joined_units(w):
    w = w.reshape(C, -1)
    return np.pad(w, ((0, 0), (0, -w.shape[1] % P)))


def expert_rows(w2):
    plan, blocks = hidden_plan(*w2.shape[:2])
    a = np.zeros((blocks, P, C), np.float32)
    for k, tile in enumerate(plan):
        for e, n, _, _ in tile:
            first, last = max(e * w2.shape[1], k * P), min((e + 1) * w2.shape[1], (k + 1) * P)
            a[n, first - k * P:last - k * P] = w2[e, first - e * w2.shape[1]:last - e * w2.shape[1]]
    return a.transpose(1, 0, 2)


def layouts(i):
    f = lambda n: np.asarray(i[n])
    x = f("x")
    a = {
        "x_rows": x.reshape(B, NT, 2, S, S).transpose(2, 3, 0, 1, 4),
        "x_chan": x.reshape(B, C, N).transpose(1, 0, 2).reshape(C, B * N),
        "conv1T": f("L0_tok_conv1_w").T,
        "conv2T": f("L0_tok_conv2_w").T,
        "bn": np.stack([f("L0_tok_conv1_b"), f("L0_tok_bn_gamma"), f("L0_tok_bn_beta"),
                        f("L0_tok_bn_mean"), f("L0_tok_bn_var")], 1),
        "conv2_b": f("L0_tok_conv2_b")[:, None],
        "ident": np.eye(P, dtype=np.float32),
        "at0_w": np.concatenate([f("L0_attn_Wq").T, f("L0_attn_Wk").T, f("L0_attn_Wv").T], 1),
        "at0_b": np.stack([f("L0_attn_bq"), f("L0_attn_bk")], 1),
        "at0_bv": f("L0_attn_bv")[None],
        "at0_beta": np.repeat(f("L0_attn_beta"), 2)[:, None],
        "at0_table": bias_table(),
        "rank": np.arange(NE, 0, -1, dtype=np.float32)[None],
        "moe0_router": f("L0_ffn_Wr"),
        "moe0_w1": joined_units(np.concatenate([f("L0_ffn_W1s")[None], f("L0_ffn_W1p")]).transpose(1, 0, 2)),
        "moe0_w2": expert_rows(np.concatenate([f("L0_ffn_W2s")[None], f("L0_ffn_W2p")])),
        "moe0_b1": np.concatenate([f("L0_ffn_b1s")[None], f("L0_ffn_b1p")]).reshape(-1, P).T,
        "moe0_b2": np.concatenate([f("L0_ffn_b2p"), f("L0_ffn_b2s")[None]]),
        "lin_w": f("L1_attn_Wqkv"),
        "lin_b_qk": f("L1_attn_bqkv")[:2 * C].reshape(2, C).T,
        "lin_b_kv": f("L1_attn_bqkv")[None, C:],
        **decay_tables(),
        "gains": np.stack([f("L1_ffn_ln1_w"), f("L1_ffn_ln2_w")], 1),
        "at1_w": np.concatenate([f("L1_ffn_wq"), f("L1_ffn_wk"), f("L1_ffn_wv")]).T,
        "at1_wo": output_rows(f("L1_ffn_wo")),
        **rotary_tables(),
        "causal_mask": causal_masks(),
        "moe1_router": f("L1_ffn_router_w").T,
        "moe1_w1": joined_units(f("L1_ffn_w1").transpose(2, 0, 1)),
        "moe1_w3": joined_units(f("L1_ffn_w3").transpose(2, 0, 1)),
        "moe1_w2": expert_rows(f("L1_ffn_w2").transpose(0, 2, 1)),
    }
    a["x_rows"] = a["x_rows"].reshape(P, B, NT, S)
    return {k: np.ascontiguousarray(v) for k, v in a.items()}


def kernel(**inputs):
    import concourse.bacc as _bacc
    from concourse.bass_utils import run_bass_kernel_spmd as _run

    nc = _bacc.Bacc("TRN2", target_bir_lowering=False, num_devices=1)
    arrays = layouts(inputs)
    t = {n: nc.dram_tensor(n + "_dram", a.shape, mybir.dt.from_np(a.dtype), kind="ExternalInput").ap()
         for n, a in arrays.items()}
    t["h_dram"] = nc.dram_tensor("h_scratch", (P, T * C), F32, kind="Internal").ap()
    t["wd_dram"] = nc.dram_tensor("wd_scratch", (TAPS, B * N), F32, kind="Internal").ap()
    out = nc.dram_tensor("out_0_dram", (P, T * C), F32, kind="ExternalOutput").ap()
    tower(nc, t, out)
    r = _run(nc, [{n + "_dram": a for n, a in arrays.items()}], core_ids=[0])
    got = r.results[0]["out_0_dram"]
    return got.reshape(P, B, NT, C).transpose(1, 2, 0, 3).reshape(B, N, C)
```

```python
from contextlib import ExitStack

import numpy as np

import concourse.bass as bass
from concourse import mybir

ALU = mybir.AluOpType
ACT = mybir.ActivationFunctionType
F32 = mybir.dt.float32
BF16 = mybir.dt.bfloat16
AX = mybir.AxisListType

P = 128
B = 2
C = 64
S = 64
N = C * S
NT = N // P
T = B * NT
QB = 512
NQ = N // QB
SUB = QB // P
CR = 16
TAPS = 9
NE = 8
F0 = 256
F1 = 170
NH, NKV, HD = 4, 2, 16
ALPHA = float(np.float32(0.99))
NEG = -1e30


def stage_semaphores(nc, ctx, prefix):
    taken = []

    def zero():
        nc.clear_and_free_semaphores(taken)
        nc.all_engine_barrier()

    ctx.callback(zero)

    def sem(name):
        taken.append(nc.alloc_semaphore(prefix + name))
        return taken[-1]

    return sem


def involution_stage(nc, t, H):
    POOL_T = 10
    DVE_T = NT - POOL_T
    CH = B * N // QB
    with ExitStack() as ctx:
        sb = lambda n, s, d=F32: ctx.enter_context(nc.sbuf_tensor(n, s, d))
        ps = lambda n, s, d=F32: ctx.enter_context(nc.psum_tensor(n, s, d))
        sem = stage_semaphores(nc, ctx, "")
        rows = [sb(f"x_rows{i}", [P, B, NT, S + 2]) for i in range(3)]
        xc = sb("x_chan", [C, B * N])
        w1 = sb("conv1", [C, CR])
        w2 = sb("conv2", [CR, TAPS])
        bn = sb("bn", [CR, 8])
        b2 = sb("conv2_bias", [TAPS, 1])
        y = sb("bottleneck", [CR, 2, QB])
        wd = sb("tap_weights", [TAPS, B, N])
        wdt = sb("tap_weights_tok", [P, B, TAPS, S])
        prod_v = sb("prod_v", [P, 2, DVE_T, S])
        prod_g = sb("prod_g", [P, 2, POOL_T, S])
        y_ps = [ps(f"y_ps{i}", [CR, QB]) for i in range(2)]
        wd_ps = [ps(f"wd_ps{i}", [TAPS, QB]) for i in range(2)]

        zeroed = [sem(f"zeroed{i}") for i in range(3)]
        rows_in = [sem("rows_in0"), sem("rows_in1")]
        small_in = sem("small_in")
        xc_in = [sem("xc_in0"), sem("xc_in1")]
        bn_ready = sem("bn_ready")
        y_mm, y_ready, wd_mm, wd_ready = sem("y_mm"), sem("y_ready"), sem("wd_mm"), sem("wd_ready")
        wd_out, wdt_in = sem("wd_out"), [sem("wdt_in0"), sem("wdt_in1")]
        v_step, g_step = sem("inv_v_step"), sem("inv_g_step")
        half = CH // 2

        with nc.Block() as block:
            @block.sync
            def _(sp):
                sp.dma_start(w1[:, :], t["conv1T"]).then_inc(small_in, 16)
                sp.dma_start(w2[:, :], t["conv2T"]).then_inc(small_in, 16)
                sp.dma_start(bn[:, 0:5], t["bn"]).then_inc(small_in, 16)
                sp.dma_start(b2[:, :], t["conv2_b"]).then_inc(small_in, 16)
                sp.dma_start(xc[:, 0:N], t["x_chan"][:, 0:N]).then_inc(xc_in[0], 16)
                for im in range(B):
                    for i in (1, 0, 2):
                        if im == 0:
                            sp.wait_ge(zeroed[i], 1)
                        for half_p in range(2):
                            lo, hi = max(0, 1 - i), min(S, S + 1 - i)
                            src = t["x_rows"][half_p * S + lo + i - 1:half_p * S + hi + i - 1, im]
                            sp.dma_start(rows[i][half_p * S + lo:half_p * S + hi, im, :, 1:S + 1],
                                         src).then_inc(rows_in[im], 16)
                    if im == 0:
                        sp.dma_start(xc[:, N:2 * N], t["x_chan"][:, N:2 * N]).then_inc(xc_in[1], 16)
                for im in range(B):
                    sp.wait_ge(wd_ready, (im + 1) * half)
                    sp.dma_start(t["wd_dram"][:, im * N:(im + 1) * N], wd[:, im, :]).then_inc(wd_out, 16)
                    sp.wait_ge(wd_out, (im + 1) * 16)
                    for half_p in range(2):
                        sp.dma_start(wdt[half_p * S:(half_p + 1) * S, im, :, :],
                                     t["wd_dram"].rearrange("k (b h w) -> b h k w", b=B, h=S)[im])\
                          .then_inc(wdt_in[im], 16)

            @block.tensor
            def _(pe):
                pe.wait_ge(small_in, 64)
                for n in range(CH + 1):
                    if n < CH:
                        if n % half == 0:
                            pe.wait_ge(xc_in[n // half], 16)
                        if n >= 2:
                            pe.wait_ge(y_ready, n - 1)
                        pe.matmul(y_ps[n % 2][:, :], w1[:, :], xc[:, n * QB:(n + 1) * QB],
                                  start=True, stop=True).then_inc(y_mm, 1)
                    if n:
                        m = n - 1
                        if m >= 2:
                            pe.wait_ge(wd_ready, m - 1)
                        pe.wait_ge(y_ready, m + 1)
                        pe.matmul(wd_ps[m % 2][:, :], w2[:, :], y[:, m % 2, :],
                                  start=True, stop=True).then_inc(wd_mm, 1)

            @block.scalar
            def _(act):
                act.wait_ge(bn_ready, 1)
                act.activation(bn[:, 6:7], bn[:, 5:6], ACT.Sqrt).then_inc(bn_ready, 1)
                act.wait_ge(bn_ready, 5)
                for n in range(CH + 1):
                    if n < CH:
                        act.wait_ge(y_mm, n + 1)
                        if n >= 2:
                            act.wait_ge(wd_mm, n - 1)
                        act.activation(y[:, n % 2, :], y_ps[n % 2][:, :], ACT.Relu, bias=bn[:, 7:8],
                                       scale=bn[:, 6:7]).then_inc(y_ready, 1)
                    if n:
                        m = n - 1
                        act.wait_ge(wd_mm, m + 1)
                        act.activation(wd[:, m // half, (m % half) * QB:(m % half + 1) * QB], wd_ps[m % 2][:, :],
                                       ACT.Identity, bias=b2[:, 0:1]).then_inc(wd_ready, 1)

            Hv = H[:, :, :].rearrange("p (b t) f -> p b t f", b=B)

            def taps(eng, step, prod, t0, t1):
                n = 0
                for im in range(B):
                    eng.wait_ge(rows_in[im], 96)
                    eng.wait_ge(wdt_in[im], 32)
                    acc = Hv[:, im, t0:t1, :]
                    for i in range(TAPS):
                        k = (i + TAPS // 3) % TAPS
                        x = rows[k // 3][:, im, t0:t1, k % 3:k % 3 + S]
                        w = wdt[:, im, k:k + 1, :].broadcast_to([P, t1 - t0, S])
                        if i >= 3:
                            eng.wait_ge(step, n - 2)
                        eng.tensor_tensor(acc if i == 0 else prod[:, i % 2, :, :], x, w,
                                          ALU.mult).then_inc(step, 1)
                        n += 1
                        if i:
                            eng.wait_ge(step, n)
                            eng.tensor_tensor(acc, acc, prod[:, i % 2, :, :], ALU.add).then_inc(step, 1)
                            n += 1

            @block.gpsimd
            def _(pool):
                pool.memset(rows[2][:, :, :, :], 0.0).then_inc(zeroed[2], 1)
                taps(pool, g_step, prod_g, DVE_T, NT)

            @block.vector
            def _(dve):
                dve.memset(rows[1][:, :, :, 0:S + 2:S + 1], 0.0).then_inc(zeroed[1], 1)
                dve.memset(rows[0][:, :, :, :], 0.0).then_inc(zeroed[0], 1)
                dve.wait_ge(small_in, 64)
                dve.tensor_scalar(bn[:, 5:6], bn[:, 4:5], 1e-5, None, ALU.add).then_inc(bn_ready, 1)
                dve.wait_ge(bn_ready, 2)
                dve.reciprocal(bn[:, 5:6], bn[:, 6:7]).then_inc(bn_ready, 1)
                dve.wait_ge(bn_ready, 3)
                dve.tensor_tensor(bn[:, 6:7], bn[:, 5:6], bn[:, 1:2], ALU.mult)
                dve.tensor_tensor(bn[:, 7:8], bn[:, 0:1], bn[:, 3:4], ALU.subtract).then_inc(bn_ready, 1)
                dve.wait_ge(bn_ready, 4)
                dve.scalar_tensor_tensor(out=bn[:, 7:8], in0=bn[:, 7:8], scalar=bn[:, 6:7], in1=bn[:, 2:3],
                                         op0=ALU.mult, op1=ALU.add).then_inc(bn_ready, 1)
                taps(dve, v_step, prod_v, 0, DVE_T)


def norm_stage(nc, name, H, XT, ident, centred, eps, gain=None, U=None, parts=None):
    turns = U is None
    G = 16
    NG = T // G
    with ExitStack() as ctx:
        sb = lambda n, s, d=F32: ctx.enter_context(nc.sbuf_tensor(name + n, s, d))
        sem = stage_semaphores(nc, ctx, name)
        xc = sb("centred", [P, NG, G, C])
        sq = sb("squares", [P, 2, G, C])
        st = sb("stats", [P, 4, 2, G])
        tr_ps = [ctx.enter_context(nc.psum_tensor(f"{name}tr_ps{i}", [C, G // 4, QB], F32)) for i in range(2)]
        v_step, sq_ready, sd_ready = sem("v_step"), sem("sq_ready"), sem("sd_ready")
        xn_ready, transposed, xt_ready = sem("xn_ready"), sem("transposed"), sem("xt_ready")
        var_ready, xc_ready = sem("var_ready"), sem("xc_ready")
        rest_ready, mid_ready, low_ready, copied = sem("rest_ready"), sem("mid_ready"), sem("low_ready"), sem("copied")
        rest = sb("rest", [C, G * P]) if parts else None
        tokens = lambda g: slice(g * G * P, (g + 1) * G * P)
        with nc.Block() as block:
            @block.vector
            def _(dve):
                n = 0
                for g in range(NG + 2 if parts else NG + 1):
                    k = g % 2
                    if g < NG:
                        x = H[:, g * G:(g + 1) * G, :]
                        if centred:
                            dve.tensor_reduce(st[:, 0, k, :], x, AX.X, ALU.add).then_inc(v_step, 1)
                            dve.wait_ge(v_step, n + 1)
                            dve.tensor_scalar(st[:, 0, k, :], st[:, 0, k, :], -1.0 / C, None,
                                              ALU.mult).then_inc(v_step, 1)
                            dve.wait_ge(v_step, n + 2)
                            n += 2
                            dve.tensor_tensor(xc[:, g, :, :], x,
                                              st[:, 0, k, :].unsqueeze(2).broadcast_to([P, G, C]),
                                              ALU.add).then_inc(xc_ready, 1)
                    if 0 < g <= NG:
                        k = (g - 1) % 2
                        dve.wait_ge(sq_ready, g)
                        dve.tensor_reduce(st[:, 1, k, :], sq[:, k, :, :], AX.X, ALU.add).then_inc(v_step, 1)
                        dve.wait_ge(v_step, n + 1)
                        dve.tensor_scalar(st[:, 1, k, :], st[:, 1, k, :], 1.0 / C, eps, ALU.mult,
                                          ALU.add).then_inc(var_ready, 1)
                        dve.wait_ge(sd_ready, g)
                        dve.reciprocal(st[:, 3, k, :], st[:, 2, k, :]).then_inc(v_step, 1)
                        dve.wait_ge(v_step, n + 2)
                        n += 2
                        if centred:
                            dve.wait_ge(xc_ready, g)
                        src = xc[:, g - 1, :, :] if centred else H[:, (g - 1) * G:g * G, :]
                        dst = xc[:, g - 1, :, :] if U is None else U[:, (g - 1) * G:g * G, :]
                        dve.tensor_tensor(dst, src,
                                          st[:, 3, k, :].unsqueeze(2).broadcast_to([P, G, C]),
                                          ALU.mult).then_inc(xn_ready, 1)
                    if parts and g >= 2:
                        mh, hl = parts
                        m = g - 2
                        dve.wait_ge(xt_ready, m + 1)
                        if m:
                            dve.wait_ge(low_ready, m)
                        dve.scalar_tensor_tensor(
                            out=rest[:, :], in0=tr_ps[m % 2][:, :, :].rearrange("c a q -> c (a q)"),
                            scalar=1.0 if gain is None else gain, in1=hl[0:C, tokens(m)],
                            op0=ALU.mult, op1=ALU.subtract).then_inc(rest_ready, 1)
                        dve.wait_ge(mid_ready, m + 1)
                        dve.tensor_tensor(hl[C:2 * C, tokens(m)], rest[:, :], mh[0:C, tokens(m)],
                                          ALU.subtract).then_inc(low_ready, 1)

            @block.scalar
            def _(act):
                def copy_out(g):
                    act.wait_ge(transposed, g + 1)
                    out = parts[1][0:C, tokens(g)] if parts else XT[:, tokens(g)]
                    src = tr_ps[g % 2][:, :, :].rearrange("c a q -> c (a q)")
                    if gain is None:
                        act.activation(out, src, ACT.Copy).then_inc(xt_ready, 1)
                    else:
                        act.activation(out, src, ACT.Copy, scale=gain).then_inc(xt_ready, 1)
                    if parts:
                        act.wait_ge(rest_ready, g + 1)
                        act.activation(parts[0][0:C, tokens(g)], rest[:, :], ACT.Copy).then_inc(mid_ready, 1)
                for g in range(NG + 1):
                    if g < NG:
                        if centred:
                            act.wait_ge(xc_ready, g + 1)
                        if g >= 2:
                            act.wait_ge(var_ready, g - 1)
                        src = xc[:, g, :, :] if centred else H[:, g * G:(g + 1) * G, :]
                        act.activation(sq[:, g % 2, :, :], src, ACT.Square).then_inc(sq_ready, 1)
                        act.wait_ge(var_ready, g + 1)
                        act.activation(st[:, 2, g % 2, :], st[:, 1, g % 2, :], ACT.Sqrt).then_inc(sd_ready, 1)
                    if g > 0 and turns:
                        copy_out(g - 1)

            @block.tensor
            def _(pe):
                for g in range(NG if turns else 0):
                    pe.wait_ge(xn_ready, g + 1)
                    if g >= 2:
                        pe.wait_ge(rest_ready if parts else xt_ready, g - 1)
                    for i in range(G):
                        mm = pe.transpose(tr_ps[g % 2][:, i // 4, (i % 4) * P:(i % 4 + 1) * P],
                                          xc[:, g, i, :], ident[:, :])
                    mm.then_inc(transposed, 1)

            if parts:
                @block.gpsimd
                def _(pool):
                    for g in range(NG):
                        pool.wait_ge(xt_ready, g + 1)
                        pool.tensor_copy(parts[0][C:2 * C, tokens(g)], parts[1][0:C, tokens(g)]).then_inc(copied, 1)



M_ROW = 96


class AttentionShape:

    def __init__(self, causal, heads):
        self.causal, self.heads = causal, heads
        self.rows = heads * SUB
        self.m_rows = 3 if causal else 1
        self.halves = 2 if causal else 1
        self.sum_rows = 32 if causal else C
        self.pv_units = NKV if causal else 1
        self.probs_bufs = 4
        self.order = list(reversed(range(NQ))) if causal else list(range(NQ))
        self.max_tiles = [self._max_tiles(q) for q in self.order]
        self.units = [self._units(q) for q in self.order]
        first = lambda lists: np.concatenate([[0], np.cumsum([len(x) for x in lists])]).tolist()
        self.max_first, self.unit_first = first(self.max_tiles), first(self.units)
        self.pv_first = [n // self.pv_units for n in self.unit_first]
        self.max_all, self.unit_all, self.pv_all = self.max_first[-1], self.unit_first[-1], self.pv_first[-1]
        self.steps = self._schedule()

    def _max_tiles(self, q):
        out = []
        for h in range(self.heads):
            for s in range(SUB):
                for c in range(self.chunks(q)):
                    diagonal = self.causal and c == q
                    out.append((h, s, c, (s + 1) * P if diagonal else QB, diagonal))
        return out

    def _units(self, q):
        if not self.causal:
            return [(((0, 2 * u), (0, 2 * u + 1)), 0, False) for u in range(NT // 2)]
        return [(((2 * g, k), (2 * g + 1, k)), max(0, k - SUB * q) * P, k >= SUB * q)
                for k in range(SUB * (q + 1)) for g in range(NKV)]

    def chunks(self, q):
        return q + 1 if self.causal else NQ

    def kv(self, h):
        return h // 2 if self.causal else 0

    def _schedule(self):
        step_us, col = 0.1, 1 / 2400.
        max_cost, exp_cost = (1, 1) if self.causal else (2, 4)
        place = [j for j in range(NQ) for _ in self.units[j]]
        steps, t, dve, act = [], 0.0, 0.0, 0.0
        m = u = p = o = f = closed = n = 0
        max_done, exp_done, rows_done, fin_free, sums_done, o_free = [], [], {}, 0.0, {}, 0.0
        chain_done = {}
        while f < NQ * SUB:
            ready = []
            j = next((k for k in range(NQ) if m < self.max_first[k + 1]), NQ)
            if j < NQ and (m + 1 < self.max_first[j + 1] or n >= j * self.halves):
                ready.append((max_done[m - 2] if m >= 2 else 0.0, 0, "m"))
            if n < closed * self.halves:
                ready.append((max(fin_free, chain_done[n // self.halves]), 1, "n"))
            if f < o * SUB:
                ready.append((max(fin_free, sums_done[f // SUB]), 2, "f"))
            if p < self.pv_all and (p + 1) * self.pv_units <= u:
                k = place[p * self.pv_units]
                if k <= o:
                    ready.append((max(exp_done[(p + 1) * self.pv_units - 1],
                                      o_free if p == self.pv_first[k] else 0.0), 4, "p"))
            if u < self.unit_all and u < self.probs_bufs + p * self.pv_units and place[u] in rows_done:
                ready.append((max(exp_done[u - 2] if u >= 2 else 0.0, rows_done[place[u]]), 3, "u"))
            if o < NQ and p == self.pv_first[o + 1] and f >= o * SUB:
                ready.append((0.0, -1, "o"))
            at, _, kind = min((max(at, t), order, kind) for at, order, kind in ready)
            t = at
            if kind == "m":
                keys = self.max_tiles[j][m - self.max_first[j]][3]
                steps.append(("m", j, m - self.max_first[j]))
                t += keys * col * max_cost
                dve = max(dve, t + step_us) + keys / 960. + 0.06
                max_done.append(dve + step_us)
                m += 1
                if m == self.max_first[j + 1]:
                    steps.append(("c", j, 0))
                    dve += 0.2 * (6 if self.m_rows > 1 else 1)
                    chain_done[j] = dve + step_us
                    closed += 1
            elif kind == "n":
                j, r = divmod(n, self.halves)
                steps.append(("n", j, r))
                t += 0.055 * self.rows / self.halves
                dve = max(dve, t + step_us) + 0.6
                fin_free = dve + step_us
                if r == self.halves - 1:
                    rows_done[j] = dve + step_us
                n += 1
            elif kind == "u":
                j = place[u]
                c = 2 * (QB - self.units[j][u - self.unit_first[j]][1])
                steps.append(("u", j, u - self.unit_first[j]))
                t += c * col * exp_cost
                act = max(act, t + step_us) + c / 1200. + 0.05
                exp_done.append(act + step_us)
                u += 1
            elif kind == "p":
                j = place[p * self.pv_units]
                c = QB - self.units[j][p * self.pv_units - self.unit_first[j]][1]
                steps.append(("p", j, p - self.pv_first[j]))
                t += c * col * 4
                p += 1
            elif kind == "o":
                steps.append(("o", o, 0))
                act = max(act, t + step_us) + 0.5
                o_free = act + step_us
                sums_done[o] = o_free + (0 if self.causal else 3)
                o += 1
            else:
                steps.append(("f",) + divmod(f, SUB))
                t += (C + 1) * self.heads * 4 * col
                dve = max(dve, t + step_us) + 0.6
                fin_free = dve + step_us
                f += 1
        return steps


def attention_core(nc, ctx, name, sh, H, ident, identb, QT, KT, max_operands, V, mask, fin_rhs, ones):
    sb = lambda n, s, d=F32: ctx.enter_context(nc.sbuf_tensor(name + n, s, d))
    ps = lambda n, s, d=F32: ctx.enter_context(nc.psum_tensor(name + n, s, d))
    sem = stage_semaphores(nc, ctx, name + "core_")
    dt = QT.dtype
    heads, rows, halves, mr = sh.heads, sh.rows, sh.halves, sh.m_rows
    turn = ident if dt == F32 else identb
    per = rows // halves
    NP, PU = sh.probs_bufs, sh.pv_units
    k_exp = M_ROW + mr
    exp_ps = [ps(f"exp_ps{i}", [P, 2, QB]) for i in range(2)]
    max_ps = [ps(f"max_ps{i}", [P, QB]) for i in range(2)]
    o_ps = ps("o_ps", [P, QB])
    fin_ps = ps("fin_ps", [P, QB])
    probs = sb("probs", [P, NP, 2, QB])
    mx = sb("mx", [P, rows, NQ])
    nm = sb("nm", [P, 3, rows])
    nm_p = sb("nm_parts", [P, rows, mr], dt)
    sums = sb("sums", [P, QB])
    total = sb("total", [P, 2, 2, QB]) if heads == 1 else None
    rec = sb("rec", [P, heads])
    scaled = sb("scaled", [P, 2, heads, C]) if heads > 1 else None
    max_mm, max_read = sem("max_mm"), sem("max_read")
    exp_mm, exp_done, pv_mm = sem("exp_mm"), sem("exp_done"), sem("pv_mm")
    nm_ready, nm_turned, nm_rows = sem("nm_ready"), sem("nm_turned"), sem("nm_rows")
    o_copied, fin_mm, fin_read, v_step = sem("o_copied"), sem("fin_mm"), sem("fin_read"), sem("v_step")
    head_step, total_step = sem("head_step"), sem("total_step")
    unit_steps = len(sh.units[0]) - 1
    total_all = NQ * unit_steps
    v_image = NQ * ((5 if mr > 1 else 0) + SUB)
    f_all, n_all = NQ * SUB, NQ * halves
    turned = fin_ps[0:mr, :] if dt == F32 else fin_ps[0:mr, :].bitcast(BF16)

    def tensor(pe, im):
        turned_before = read_before = 0
        for step, j, i in sh.steps:
            q = sh.order[j]
            if step == "m":
                h, s, c, keys, diagonal = sh.max_tiles[j][i]
                n = sh.max_first[j] + i
                q0 = q * QB + s * P
                if n >= 2:
                    pe.wait_ge(max_read, im * sh.max_all + n - 1)
                for a, (qs, ks, k_rows) in enumerate(max_operands):
                    mm = pe.matmul(max_ps[n % 2][:, 0:keys], qs[0:k_rows, h, q0:q0 + P],
                                   ks[0:k_rows, sh.kv(h), c * QB:c * QB + keys], start=(a == 0),
                                   stop=a == len(max_operands) - 1 and not diagonal)
                if diagonal:
                    mm = pe.matmul(max_ps[n % 2][:, keys - P:keys], identb[:, :], mask[:, 0, :],
                                   start=False, stop=True)
                mm.then_inc(max_mm, 1)
            elif step == "u":
                pair, c0, diagonal = sh.units[j][i]
                n = sh.unit_first[j] + i
                if i == 0:
                    pe.wait_ge(nm_rows, im * n_all + (j + 1) * halves)
                if n >= 2:
                    pe.wait_ge(exp_done, im * sh.unit_all + n - 1)
                for a, (h, k) in enumerate(pair):
                    mm = pe.matmul(exp_ps[n % 2][:, a, c0:QB], KT[0:k_exp, sh.kv(h), k * P:(k + 1) * P],
                                   QT[0:k_exp, h, q * QB + c0:(q + 1) * QB], start=True, stop=not diagonal)
                    if diagonal:
                        mm = pe.matmul(exp_ps[n % 2][:, a, c0:c0 + P], identb[:, :], mask[:, 1, :],
                                       start=False, stop=True)
                mm.then_inc(exp_mm, 1)
            elif step == "p":
                pe.wait_ge(exp_done, im * sh.unit_all + sh.unit_first[j] + (i + 1) * PU)
                if i == 0 and j > 0:
                    pe.wait_ge(o_copied, im * NQ + j)
                for u in range(i * PU, (i + 1) * PU):
                    pair, c0, _ = sh.units[j][u]
                    n = sh.unit_first[j] + u
                    for a, (h, k) in enumerate(pair):
                        row = sh.sum_rows * (h if sh.causal else a)
                        mm = pe.matmul(o_ps[row:row + sh.sum_rows, c0:QB], V[:, k, sh.kv(h), :],
                                       probs[:, n % NP, a, c0:QB], start=(u < PU),
                                       stop=(u >= len(sh.units[j]) - PU))
                mm.then_inc(pv_mm, 1)
            elif step == "n":
                pe.wait_ge(nm_ready, im * NQ + j + 1)
                if turned_before:
                    pe.wait_ge(nm_rows, im * n_all + turned_before)
                if read_before:
                    pe.wait_ge(fin_read, im * f_all + read_before)
                for k in range(per):
                    mm = pe.transpose(turned[:, k * P:(k + 1) * P], nm_p[:, i * per + k, :], turn[:, :])
                mm.then_inc(nm_turned, 1)
                turned_before += 1
            elif step == "f":
                if i == 0:
                    pe.wait_ge(o_copied, im * NQ + j + 1)
                pe.wait_ge(nm_rows, im * n_all + turned_before)
                if read_before:
                    pe.wait_ge(fin_read, im * f_all + read_before)
                mm = pe.matmul(fin_ps[:, 0:fin_rhs.shape[1]], sums[:, i * P:(i + 1) * P], fin_rhs,
                               start=True, stop=True)
                if heads == 1:
                    if i == 0:
                        pe.wait_ge(total_step, im * total_all + (j + 1) * unit_steps)
                    for a in range(2):
                        mm = pe.matmul(fin_ps[:, C:C + 1], total[:, j % 2, a, i * P:(i + 1) * P], ones,
                                       start=(a == 0), stop=(a == 1))
                mm.then_inc(fin_mm, 1)
                read_before += 1

    def scalar(act, im):
        for step, j, i in sh.steps:
            if step == "u":
                c0 = sh.units[j][i][1]
                n = sh.unit_first[j] + i
                act.wait_ge(exp_mm, im * sh.unit_all + n + 1)
                if n >= NP:
                    act.wait_ge(pv_mm, im * sh.pv_all + (n - NP) // PU + 1)
                    if heads == 1:
                        block_no, unit = divmod(n - NP, unit_steps + 1)
                        act.wait_ge(total_step, im * total_all + block_no * unit_steps + max(unit, 1))
                act.activation(probs[:, n % NP, :, c0:QB], exp_ps[n % 2][:, :, c0:QB],
                               ACT.Exp).then_inc(exp_done, 1)
            elif step == "o":
                act.wait_ge(pv_mm, im * sh.pv_all + sh.pv_first[j + 1])
                if j:
                    act.wait_ge(fin_mm, im * f_all + j * SUB)
                act.activation(sums[:, :], o_ps[:, :], ACT.Copy).then_inc(o_copied, 1)

    def vector(dve, im):
        own = 0

        def own_step(ins):
            nonlocal own
            ins.then_inc(v_step, 1)
            own += 1
            dve.wait_ge(v_step, im * v_image + own)

        for step, j, i in sh.steps:
            q = sh.order[j]
            if step == "m":
                h, s, c, keys, _ = sh.max_tiles[j][i]
                n = sh.max_first[j] + i
                dve.wait_ge(max_mm, im * sh.max_all + n + 1)
                dve.tensor_reduce(mx[:, h * SUB + s, c:c + 1], max_ps[n % 2][:, 0:keys], AX.X,
                                  ALU.max).then_inc(max_read, 1)
            elif step == "c":
                dve.wait_ge(max_read, im * sh.max_all + sh.max_first[j + 1])
                tiles = mx[:, :, 0:sh.chunks(q)]
                if mr == 1:
                    dve.tensor_reduce(nm_p[:, :, 0], tiles, AX.X, ALU.max, negate=True).then_inc(nm_ready, 1)
                    dve.wait_ge(nm_ready, im * NQ + j + 1)
                else:
                    own_step(dve.tensor_reduce(nm[:, 0, :], tiles, AX.X, ALU.max, negate=True))
                    own_step(dve.tensor_copy(nm_p[:, :, 0], nm[:, 0, :]))
                    own_step(dve.tensor_tensor(nm[:, 1, :], nm[:, 0, :], nm_p[:, :, 0], ALU.subtract))
                    own_step(dve.tensor_copy(nm_p[:, :, 1], nm[:, 1, :]))
                    own_step(dve.tensor_tensor(nm[:, 2, :], nm[:, 1, :], nm_p[:, :, 1], ALU.subtract))
                    dve.tensor_copy(nm_p[:, :, 2], nm[:, 2, :]).then_inc(nm_ready, 1)
            elif step == "n":
                dve.wait_ge(nm_turned, im * n_all + j * halves + i + 1)
                hs = slice(i * heads // halves, (i + 1) * heads // halves)
                dve.tensor_copy(QT[M_ROW:M_ROW + mr, hs, q * QB:(q + 1) * QB],
                                turned[:, 0:per * P].rearrange("m (h t) -> m h t", t=QB)
                                ).then_inc(nm_rows, 1)
            elif step == "f":
                n = j * SUB + i
                dve.wait_ge(fin_mm, im * f_all + n + 1)
                fin = fin_ps[:, 0:heads * (C + 1)].rearrange("p (h c) -> p h c", h=heads)
                own_step(dve.reciprocal(rec[:, :], fin[:, :, C]))
                if heads == 1:
                    h_tile = H[:, bass.ds(im * NT + (q * SUB + i), 1), :]
                    dve.scalar_tensor_tensor(out=h_tile, in0=fin[:, :, 0:C], scalar=rec[:, 0:1], in1=h_tile,
                                             op0=ALU.mult, op1=ALU.add).then_inc(fin_read, 1)
                else:
                    dve.wait_ge(head_step, (im * f_all + n + 1) * 3)
                    dve.tensor_tensor(scaled[:, n % 2, :, :], fin[:, :, 0:C],
                                      rec[:, :].unsqueeze(2).broadcast_to([P, heads, C]),
                                      ALU.mult).then_inc(fin_read, 1)

    def heads_onto_h(pool, im):
        for step, j, i in sh.steps:
            if step != "f":
                continue
            n = j * SUB + i
            tile = scaled[:, n % 2, :, :]
            h_tile = H[:, bass.ds(im * NT + (sh.order[j] * SUB + i), 1), :]
            count = lambda k: (im * f_all + n + 2) * 3 + k
            pool.wait_ge(fin_read, im * f_all + n + 1)
            pool.tensor_tensor(tile[:, 0:2, :], tile[:, 0:2, :], tile[:, 2:4, :], ALU.add).then_inc(head_step, 1)
            pool.wait_ge(head_step, count(1))
            pool.tensor_tensor(tile[:, 0, :], tile[:, 0, :], tile[:, 1, :], ALU.add).then_inc(head_step, 1)
            pool.wait_ge(head_step, count(2))
            pool.tensor_tensor(h_tile, h_tile, tile[:, 0:1, :], ALU.add).then_inc(head_step, 1)
            pool.wait_ge(head_step, count(3))

    def sum_of_units(pool, im):
        for step, j, i in sh.steps:
            if step != "u" or i == 0:
                continue
            n = sh.unit_first[j] + i
            block_sum = total[:, j % 2, :, :]
            pool.wait_ge(exp_done, im * sh.unit_all + n + 1)
            if i == 1:
                if j >= 2:
                    pool.wait_ge(fin_mm, im * f_all + (j - 1) * SUB)
                pool.tensor_tensor(block_sum, probs[:, (n - 1) % NP, :, :], probs[:, n % NP, :, :],
                                   ALU.add).then_inc(total_step, 1)
            else:
                pool.wait_ge(total_step, im * total_all + j * unit_steps + i - 1)
                pool.tensor_tensor(block_sum, block_sum, probs[:, n % NP, :, :], ALU.add).then_inc(total_step, 1)

    return tensor, scalar, vector, sum_of_units if heads == 1 else heads_onto_h, head_step, exp_ps, max_ps


def attention0_stage(nc, t, H, XT, ident, identb):
    sh = AttentionShape(causal=False, heads=1)
    with ExitStack() as ctx:
        sb = lambda n, s, d=F32: ctx.enter_context(nc.sbuf_tensor("at0_" + n, s, d))
        sem = stage_semaphores(nc, ctx, "at0_")
        QT, KT = sb("QT", [P, 1, N]), sb("KT", [P, 1, N])
        V = sb("V", [P, NT, 1, C])
        QM = [sb(f"q_max{i}", [P, 1, N], BF16) for i in range(2)]
        KM = [sb(f"k_max{i}", [P, 1, N], BF16) for i in range(2)]
        table = sb("table", [P, N // (P // 4)])
        rest = sb("table_rest", [P, N // (P // 4)])
        high, low = (sb(n, [P, N // (P // 4)], BF16) for n in ("table_high", "table_low"))
        fin_rhs = sb("ident_twice", [P, C])
        ones = sb("ones", [P, 1])
        xb = sb("x_image", [C, N])
        w = sb("wqkv", [C, 3 * C])
        bias = sb("bias", [P, 2])
        beta = sb("beta", [P, 1])
        bv = sb("bias_v", [P, C])
        tensor, scalar, vector, sum_of_units, _, exp_ps, max_ps = attention_core(
            nc, ctx, "at0_", sh, H, ident, identb, QT, KT,
            [(QM[0], KM[0], P), (QM[1], KM[1], C + 16)], V, None, fin_rhs[:, :], ones[:, :])
        w_in, x_in, zeroed, table_in = sem("w_in"), sem("x_in"), sem("zeroed"), sem("table_in")
        qk_mm, k_ready, q_ready, v_mm, v_ready = (sem("qk_mm"), sem("k_ready"), sem("q_ready"),
                                                  sem("v_mm"), sem("v_ready"))
        table_step, q_rows_in, k_rows_in = sem("table_step"), sem("q_rows_in"), sem("k_rows_in")
        folded_out = sem("folded_out")
        scratch = [nc.dram_tensor("at0_" + n, (P, N // (P // 4)), d, kind="Internal").ap()
                   for n, d in (("bias_rows", F32), ("bias_high", BF16), ("bias_low", BF16))]
        k_high, q_high, q_split, k_split = sem("k_high"), sem("q_high"), sem("q_split"), sem("k_split")
        q_copy = sem("q_copy")
        VG = NT // 8
        with nc.Block() as block:
            @block.sync
            def _(sp):
                for im in range(B):
                    if im:
                        sp.wait_ge(v_mm, im * VG)
                    sp.dma_start(xb[:, :], XT[:, im * N:(im + 1) * N]).then_inc(x_in, 16)
                    if im == 0:
                        sp.dma_start(w[:, :], t["at0_w"]).then_inc(w_in, 16)
                        for half in (0, C):
                            sp.dma_start(bias[half:half + C, :], t["at0_b"]).then_inc(w_in, 16)
                            sp.dma_start(fin_rhs[half:half + C, :], t["ident"][0:C, 0:C]).then_inc(w_in, 16)
                        sp.dma_start(beta[:, :], t["at0_beta"]).then_inc(table_in, 16)
                        sp.dma_start(table[:, :], t["at0_table"]).then_inc(table_in, 16)
                        sp.dma_start(bv[:, :], t["at0_bv"].broadcast_to([P, C])).then_inc(w_in, 16)
                        sp.dma_start(KT[C:M_ROW + 1, 0, :], t["at0_k_rows"]).then_inc(k_rows_in, 16)
                        sp.dma_start(KM[1][C:C + 16, 0, :], t["at0_k_parts"]).then_inc(k_rows_in, 16)
                        sp.wait_ge(table_step, 4)
                        for src, dst in zip((table, high, low), scratch):
                            sp.dma_start(dst, src[:, :]).then_inc(folded_out, 16)
                        sp.wait_ge(folded_out, 16 * 3)
                        sp.wait_ge(zeroed, 1)
                        for dst, row, src in ((QT, 0, 0), (QM[1], 0, 1), (QM[1], 4, 1), (QM[1], 8, 2), (QM[1], 12, 2)):
                            sp.dma_start(dst[C + row:C + row + 4, 0, :],
                                         scratch[src].rearrange("(r c) n -> r (c n)", r=4)).then_inc(q_rows_in, 16)

            @block.gpsimd
            def _(pool):
                pool.memset(QT[C:M_ROW, 0, :], 0.0).then_inc(zeroed, 1)
                pool.wait_ge(zeroed, 1)
                pool.memset(ones[:, :], 1.0).then_inc(zeroed, 1)
                with pool.Fori(0, B) as im:
                    sum_of_units(pool, im)

            @block.tensor
            def _(pe):
                pe.wait_ge(w_in, 16 * 6)
                with pe.Fori(0, B) as im:
                    pe.wait_ge(x_in, im * 16 + 16)
                    for c in range(NQ):
                        if c >= 2:
                            pe.wait_ge(k_high, im * NQ + c - 1)
                            pe.wait_ge(q_ready, im * NQ + c - 1)
                        x = xb[:, c * QB:(c + 1) * QB]
                        pe.matmul(exp_ps[c % 2][:, 0, :], w[:, 0:2 * C], x, start=True,
                                  stop=True).then_inc(qk_mm, 1)
                        if c % 2:
                            g = c // 2
                            if g >= 2:
                                pe.wait_ge(v_ready, im * VG + g - 1)
                            for k in range(8):
                                j = g * 8 + k
                                mm = pe.matmul(max_ps[g % 2][:, k * C:(k + 1) * C], xb[:, j * P:(j + 1) * P],
                                               w[:, 2 * C:3 * C], start=True, stop=True)
                            mm.then_inc(v_mm, 1)
                    pe.wait_ge(k_ready, im * NQ + NQ)
                    pe.wait_ge(q_ready, im * NQ + NQ)
                    pe.wait_ge(k_high, im * NQ + NQ)
                    pe.wait_ge(q_copy, im * NQ + NQ)
                    pe.wait_ge(q_split, im * NQ + NQ)
                    pe.wait_ge(k_split, im * 2 * NQ + 2 * NQ)
                    pe.wait_ge(v_ready, im * VG + VG)
                    pe.wait_ge(zeroed, 2)
                    pe.wait_ge(q_rows_in, 16 * 5)
                    pe.wait_ge(k_rows_in, 16 * 2)
                    tensor(pe, im)

            @block.scalar
            def _(act):
                act.wait_ge(w_in, 16 * 6)
                with act.Fori(0, B) as im:
                    for c in range(NQ):
                        act.wait_ge(q_ready, im * NQ + c + 1)
                        cols = slice(c * QB, (c + 1) * QB)
                        keys = exp_ps[c % 2][C:2 * C, 0, :]
                        act.activation(KT[0:C, 0, cols], keys, ACT.Identity, bias=bias[C:2 * C, 1:2]).then_inc(k_ready, 1)
                        act.activation(KM[0][C:2 * C, 0, cols], keys, ACT.Identity,
                                       bias=bias[C:2 * C, 1:2]).then_inc(k_high, 1)
                        act.activation(QM[0][0:C, 0, cols], QT[0:C, 0, cols], ACT.Copy).then_inc(q_high, 1)
                        act.activation(QM[1][0:C, 0, cols], QT[0:C, 0, cols], ACT.Copy).then_inc(q_copy, 1)
                    scalar(act, im)

            def split(dve, im, c):
                cols = slice(c * QB, (c + 1) * QB)
                dve.wait_ge(k_ready, im * NQ + c + 1)
                dve.tensor_copy(KM[0][0:C, 0, cols], KT[0:C, 0, cols]).then_inc(k_split, 1)
                dve.wait_ge(q_high, im * NQ + c + 1)
                dve.tensor_tensor(QM[0][C:2 * C, 0, cols], QT[0:C, 0, cols], QM[0][0:C, 0, cols],
                                  ALU.subtract).then_inc(q_split, 1)
                dve.wait_ge(k_split, im * 2 * NQ + 2 * c + 1)
                dve.tensor_tensor(KM[1][0:C, 0, cols], KT[0:C, 0, cols], KM[0][0:C, 0, cols],
                                  ALU.subtract).then_inc(k_split, 1)

            def values_out(dve, im, g):
                dve.wait_ge(v_mm, im * VG + g + 1)
                dve.tensor_tensor(V[:, g * 8:(g + 1) * 8, 0, 0:C],
                                  max_ps[g % 2][:, :].rearrange("p (k c) -> p k c", c=C),
                                  bv[:, :].unsqueeze(1).broadcast_to([P, 8, C]),
                                  ALU.add).then_inc(v_ready, 1)

            @block.vector
            def _(dve):
                dve.wait_ge(table_in, 32)
                dve.tensor_scalar(table[:, :], table[:, :], beta[:, 0:1], None, ALU.mult).then_inc(table_step, 1)
                dve.wait_ge(table_step, 1)
                dve.tensor_copy(high[:, :], table[:, :]).then_inc(table_step, 1)
                dve.wait_ge(table_step, 2)
                dve.tensor_tensor(rest[:, :], table[:, :], high[:, :], ALU.subtract).then_inc(table_step, 1)
                dve.wait_ge(table_step, 3)
                dve.tensor_copy(low[:, :], rest[:, :]).then_inc(table_step, 1)
                dve.wait_ge(w_in, 16 * 6)
                with dve.Fori(0, B) as im:
                    for c in range(NQ):
                        cols = slice(c * QB, (c + 1) * QB)
                        dve.wait_ge(qk_mm, im * NQ + c + 1)
                        dve.tensor_scalar(QT[0:C, 0, cols], exp_ps[c % 2][0:C, 0, :],
                                          bias[0:C, 0:1], C ** -0.5, ALU.add, ALU.mult).then_inc(q_ready, 1)
                        if c:
                            split(dve, im, c - 1)
                        if c % 2 == 0 and c or c == NQ - 1:
                            values_out(dve, im, (c - 1) // 2)
                    split(dve, im, NQ - 1)
                    vector(dve, im)




def attention1_stage(nc, t, U, XT, ident, identb):
    sh = AttentionShape(causal=True, heads=NH)
    HQK = NH + NKV
    GT = 8
    NG = NT // GT
    with ExitStack() as ctx:
        sb = lambda n, s, d=F32: ctx.enter_context(nc.sbuf_tensor("at1_" + n, s, d))
        sem = stage_semaphores(nc, ctx, "at1_")
        QT, KT = sb("QT", [P, NH, N], BF16), sb("KT", [P, NKV, N], BF16)
        V = sb("V", [P, NT, NKV, 32])
        xb = sb("x_image", [C, 2, GT * P])
        w = sb("wqkv", [C, P])
        wo = sb("wo", [P, NH * (C + 1)])
        mask = sb("mask", [P, 2, P], BF16)
        cos, sin = sb("cos", [P, NT, HD // 2]), sb("sin", [P, NT, HD // 2])
        qk = sb("qk", [P, GT, HQK, HD])
        rot = sb("rot", [P, GT, HQK, HD])
        tmp = sb("tmp", [P, GT, HQK, HD // 2])
        part = sb("parts", [P, 3, GT, HQK, HD], BF16)
        QA, KA = sb("QA", [P, GT, NH, 6, HD], BF16), sb("KA", [P, GT, NKV, 6, HD], BF16)
        tensor, scalar, vector, heads_onto_h, head_step, exp_ps, max_ps = attention_core(
            nc, ctx, "at1_", sh, U, ident, identb, QT, KT, [(QT, KT, M_ROW)], V, mask, wo[:, :], None)
        w_in, x_in, filled = sem("w_in"), [sem("x_in0"), sem("x_in1")], sem("filled")
        qkv_mm, qk_ready, v_ready, rope = sem("qkv_mm"), sem("qk_ready"), sem("v_ready"), sem("rope")
        parts_ready, qa_ready, ka_ready = sem("parts_ready"), sem("qa_ready"), sem("ka_ready")
        turned, turned_out = sem("turned"), sem("turned_out")
        CG = GT // SUB
        ROPE_STEPS = 6 + 4
        TURN = [(QA, QT, slice(0, 2), lambda: exp_ps[0][:, 0, :]), (QA, QT, slice(2, 4), lambda: exp_ps[0][:, 1, :]),
                (KA, KT, slice(0, 2), lambda: exp_ps[1][:, 0, :])]
        TURNS = NG * CG * len(TURN)
        loads = [(w[:, :], t["at1_w"]), (wo[:, :], t["at1_wo"]), (cos[:, :, :], t["at1_cos"]),
                 (sin[:, :, :], t["at1_sin"]), (mask[:, :, :], t["causal_mask"])]
        q_slots, k_slots = ((0, 1, 4), (2, 3), (5,)), ((0, 2, 5), (1, 3), (4,))

        def spread(copy, slots, dst, src_heads, done):
            for p, slots_of_part in enumerate(slots):
                for s in slots_of_part:
                    ins = copy(dst[:, :, :, s, :], part[:, p, :, src_heads, :])
            ins.then_inc(done, 1)

        with nc.Block() as block:
            @block.sync
            def _(sp):
                for n in range(B * NG):
                    if n >= 2:
                        sp.wait_ge(qkv_mm, (n - 1) * CG)
                    sp.dma_start(xb[:, n % 2, :], XT[:, n * GT * P:(n + 1) * GT * P]).then_inc(x_in[n % 2], 16)
                    if n == 0:
                        for dst, src in loads:
                            sp.dma_start(dst, src).then_inc(w_in, 16)

            @block.gpsimd
            def _(pool):
                pool.memset(V[:, :, :, HD:32], 0.0).then_inc(filled, 1)
                pool.wait_ge(filled, 1)
                pool.memset(V[:, :, :, HD:HD + 1], 1.0).then_inc(filled, 1)
                pool.wait_ge(filled, 2)
                pool.memset(KT[M_ROW:M_ROW + sh.m_rows, :, :], 1.0).then_inc(filled, 1)
                pool.wait_ge(filled, 3)
                with pool.Fori(0, B) as im:
                    heads_onto_h(pool, im)

            @block.tensor
            def _(pe):
                pe.wait_ge(w_in, 16 * len(loads))
                with pe.Fori(0, B) as im:
                    def project(g):
                        pe.wait_ge(x_in[g % 2], (im * (NG // 2) + g // 2) * 16 + 16)
                        for c in range(g * CG, (g + 1) * CG):
                            if c >= 2:
                                pe.wait_ge(qk_ready, im * NG * CG + (c - 1))
                                pe.wait_ge(v_ready, im * NG * CG + (c - 1))
                            for i in range(SUB):
                                k = (c % CG) * SUB + i
                                mm = pe.matmul(max_ps[c % 2][:, i * P:(i + 1) * P],
                                               xb[:, g % 2, k * P:(k + 1) * P], w[:, :], start=True, stop=True)
                            mm.then_inc(qkv_mm, 1)

                    project(0)
                    for g in range(NG):
                        if g + 1 < NG:
                            project(g + 1)
                        pe.wait_ge(qa_ready, im * NG + g + 1)
                        pe.wait_ge(ka_ready, im * NG + g + 1)
                        for c in range(g * CG, (g + 1) * CG):
                            for part_no, (src, _, heads, bank) in enumerate(TURN):
                                n = c * len(TURN) + part_no
                                if n >= len(TURN):
                                    pe.wait_ge(turned_out, im * TURNS + n - len(TURN) + 1)
                                for h in range(2):
                                    for i in range(SUB):
                                        mm = pe.transpose(
                                            bank().bitcast(BF16)[0:M_ROW, (h * SUB + i) * P:(h * SUB + i + 1) * P],
                                            src[:, (c % CG) * SUB + i, heads.start + h, :, :]
                                            .rearrange("p s d -> p (s d)"), identb[:, :])
                                mm.then_inc(turned, 1)
                    pe.wait_ge(turned_out, im * TURNS + TURNS)
                    pe.wait_ge(v_ready, im * NG * CG + NG * CG)
                    pe.wait_ge(filled, 3)
                    tensor(pe, im)

            @block.scalar
            def _(act):
                with act.Fori(0, B) as im:
                    def projected_out(g):
                        for c in range(g * CG, (g + 1) * CG):
                            act.wait_ge(qkv_mm, im * NG * CG + (c + 1))
                            src = max_ps[c % 2][:, :].rearrange("p (i h d) -> p i h d", i=SUB, d=HD)
                            tiles = slice((c % CG) * SUB, (c % CG + 1) * SUB)
                            act.activation(qk[:, tiles, 0:NH, :], src[:, :, 0:NH, :], ACT.Copy, scale=HD ** -0.5)
                            act.activation(qk[:, tiles, NH:HQK, :], src[:, :, NH:HQK, :],
                                           ACT.Copy).then_inc(qk_ready, 1)
                            act.activation(V[:, c * SUB:(c + 1) * SUB, :, 0:HD],
                                           src[:, :, HQK:HQK + NKV, :], ACT.Copy).then_inc(v_ready, 1)

                    projected_out(0)
                    for g in range(NG):
                        act.wait_ge(parts_ready, im * NG + g + 1)
                        if g + 1 < NG:
                            projected_out(g + 1)
                        if g:
                            act.wait_ge(turned, im * TURNS + g * CG * len(TURN))
                        spread(lambda o, i: act.activation(o, i, ACT.Copy), q_slots, QA, slice(0, NH), qa_ready)
                        for c in range(g * CG, (g + 1) * CG):
                            for part_no, (_, dst, heads, bank) in enumerate(TURN):
                                act.wait_ge(turned, im * TURNS + c * len(TURN) + part_no + 1)
                                act.activation(dst[0:M_ROW, heads, c * QB:(c + 1) * QB],
                                               bank().bitcast(BF16)[0:M_ROW, :]
                                               .rearrange("p (h q) -> p h q", h=2), ACT.Copy).then_inc(turned_out, 1)
                    scalar(act, im)

            @block.vector
            def _(dve):
                dve.wait_ge(w_in, 16 * len(loads))
                half = HD // 2
                dve.sem_inc(head_step, 6)
                with dve.Fori(0, B) as im:
                    for g in range(NG):
                        dve.wait_ge(qk_ready, im * NG * CG + (g + 1) * CG)
                        tiles = slice(g * GT, (g + 1) * GT)
                        table = lambda x: x[:, tiles, :].unsqueeze(2).broadcast_to([P, GT, HQK, half])
                        lo, hi = qk[:, :, :, 0:half], qk[:, :, :, half:HD]
                        rlo, rhi = rot[:, :, :, 0:half], rot[:, :, :, half:HD]
                        own = 0

                        def step(ins):
                            nonlocal own
                            ins.then_inc(rope, 1)
                            own += 1
                            dve.wait_ge(rope, (im * NG + g) * ROPE_STEPS + own)

                        step(dve.tensor_tensor(rlo, lo, table(cos), ALU.mult))
                        step(dve.tensor_tensor(tmp[:, :, :, :], hi, table(sin), ALU.mult))
                        step(dve.tensor_tensor(rlo, rlo, tmp[:, :, :, :], ALU.subtract))
                        step(dve.tensor_tensor(rhi, hi, table(cos), ALU.mult))
                        step(dve.tensor_tensor(tmp[:, :, :, :], lo, table(sin), ALU.mult))
                        step(dve.tensor_tensor(rhi, rhi, tmp[:, :, :, :], ALU.add))
                        if g:
                            dve.wait_ge(qa_ready, im * NG + g)
                            dve.wait_ge(ka_ready, im * NG + g)
                        r = rot[:, :, :, :]
                        step(dve.tensor_copy(part[:, 0, :, :, :], r))
                        step(dve.tensor_tensor(r, r, part[:, 0, :, :, :], ALU.subtract))
                        step(dve.tensor_copy(part[:, 1, :, :, :], r))
                        step(dve.tensor_tensor(r, r, part[:, 1, :, :, :], ALU.subtract))
                        dve.tensor_copy(part[:, 2, :, :, :], r).then_inc(parts_ready, 1)
                        dve.wait_ge(parts_ready, im * NG + g + 1)
                        if g:
                            dve.wait_ge(turned, im * TURNS + g * CG * len(TURN))
                        spread(dve.tensor_copy, k_slots, KA, slice(NH, HQK), ka_ready)
                    vector(dve, im)


def split_weights_stage(nc, name, sets):
    with ExitStack() as ctx:
        sem = stage_semaphores(nc, ctx, name)
        most = max(src.shape[1] for src, _ in sets)
        whole = ctx.enter_context(nc.sbuf_tensor(name + "w_whole", [2 * C, len(sets), most], F32))
        rest = ctx.enter_context(nc.sbuf_tensor(name + "w_rest", [2 * C, len(sets), most], F32))
        loaded = [sem(f"w_loaded{n}") for n in range(len(sets))]
        high, left, middle, low = sem("w_high"), sem("w_left"), sem("w_middle"), sem("w_low")
        upper, lower = slice(0, C), slice(C, 2 * C)
        with nc.Block() as block:
            @block.sync
            def _(sp):
                for n, (src, _) in enumerate(sets):
                    for rows in (upper, lower):
                        sp.dma_start(whole[rows, n, 0:src.shape[1]], src).then_inc(loaded[n], 16)

            @block.scalar
            def _(act):
                for n, (src, (hh, mm, lh)) in enumerate(sets):
                    k = src.shape[1]
                    act.wait_ge(loaded[n], 32)
                    act.activation(hh[:, 0:k], whole[:, n, 0:k], ACT.Copy).then_inc(high, 1)
                for n, (src, (hh, mm, lh)) in enumerate(sets):
                    k = src.shape[1]
                    act.wait_ge(left, n + 1)
                    act.activation(mm[:, 0:k], rest[:, n, 0:k], ACT.Copy).then_inc(middle, 1)
                act.wait_ge(middle, len(sets))

            @block.vector
            def _(dve):
                for n, (src, (hh, mm, lh)) in enumerate(sets):
                    k = src.shape[1]
                    dve.wait_ge(high, n + 1)
                    dve.tensor_tensor(rest[:, n, 0:k], whole[:, n, 0:k], hh[:, 0:k],
                                      ALU.subtract).then_inc(left, 1)
                    dve.tensor_copy(lh[lower, 0:k], hh[lower, 0:k]).then_inc(low, 1)
                for n, (src, (hh, mm, lh)) in enumerate(sets):
                    k = src.shape[1]
                    dve.wait_ge(middle, n + 1)
                    dve.tensor_tensor(lh[upper, 0:k], rest[upper, n, 0:k], mm[upper, 0:k],
                                      ALU.subtract).then_inc(low, 1)
                dve.wait_ge(low, 2 * len(sets))


def hidden_plan(experts, size):
    plan, blocks = [], 0
    for k in range(-(-experts * size // P)):
        touched = range(k * P // size, min(experts, -(-(k + 1) * P // size)))
        plan.append([(e, blocks + i, e * size >= k * P, (e + 1) * size <= (k + 1) * P)
                     for i, e in enumerate(touched)])
        blocks += len(touched)
    return plan, blocks


def moe_stage(nc, name, t, H, parts, ident, size, shared, gated, denom_eps, residual=None, out=None):
    E = NE + shared
    NB = T * P // QB
    plan, w2_blocks = hidden_plan(E, size)
    HT = len(plan)
    straddles = any(len(tile) > 1 for tile in plan)
    first_private = next(k for k in range(HT) if plan[k][0][0] >= shared)
    UP, HB, LAG = (2, 6, 3) if gated else (3, 6, 2)
    last_mix = 4 + shared + (residual is not None)
    with ExitStack() as ctx:
        sb = lambda n, s, d=F32: ctx.enter_context(nc.sbuf_tensor(name + n, s, d))
        ps = lambda n, s, d=F32: ctx.enter_context(nc.psum_tensor(name + n, s, d))
        sem = stage_semaphores(nc, ctx, name)
        meets = (0, 0, 1)
        wr = [sb(f"router{i}", [P, NE], BF16) for i in range(3)]
        w1 = [sb(f"w1_{i}", [P, HT * P], BF16) for i in range(3)]
        w3 = [sb(f"w3_{i}", [P, HT * P], BF16) for i in range(3)] if gated else None
        w2 = sb("w2", [P, w2_blocks, C])
        b1 = None if gated else sb("b1", [P, HT])
        b2 = None if gated else sb("b2", [E, C])
        rank = sb("rank", [P, NE])
        gate = sb("gate", [P, T, E])
        g = {n: sb("g_" + n, [P, T, NE]) for n in ("p", "eq", "oh", "p2")}
        col = sb("cols", [P, 4, T])
        gate_t = sb("gate_t", [E, T * P]) if shared else None
        gate_b = sb("gate_b", [E, QB]) if shared else None
        shared_out = sb("shared_out", [P, SUB, C]) if shared else None
        act_out = sb("act_out", [P, 2, QB]) if gated else None
        hid = sb("hidden", [P, HB, QB])
        weighted = sb("weighted", [P, SUB, NE, C])
        zeros = sb("zeros", [P, QB], BF16) if straddles else None
        up = [ps(f"up{i}", [P, 2 if gated else 1, QB]) for i in range(UP)]
        down = [ps(f"down{i}", [P, NE, C]) for i in range(SUB)]
        sh_ps = ps("shared_ps", [P, SUB, C]) if shared else None
        rank_in, w_in, logits_mm = sem("rank_in"), sem("w_in"), sem("logits_mm")
        gate_step, exp_ready = sem("gate_step"), sem("exp_ready")
        gate_turned, gate_out, gate_b_ready = sem("gate_turned"), sem("gate_out"), sem("gate_b_ready")
        up_mm, act_done, hid_ready = sem("up_mm"), sem("act_done"), sem("hid_ready")
        down_mm, down_done, down_read = sem("down_mm"), sem("down_done"), sem("down_read")
        sh_done, sh_read, mix_step = sem("sh_done"), sem("sh_read"), sem("mix_step")
        out_written, zeros_ready = sem("out_written"), sem("zeros_ready")
        loads = [(w2[:, :, :], "w2")]
        loads += [] if gated else [(b1[:, :], "b1"), (b2[:, :], "b2")]
        split_weights_stage(nc, name, [(t[name + "router"], wr), (t[name + "w1"], w1)]
                            + ([(t[name + "w3"], w3)] if gated else []))
        gate_steps = 22
        TURNS = T // SUB

        with nc.Block() as block:
            @block.sync
            def _(sp):
                sp.dma_start(rank[:, :], t["rank"].broadcast_to([P, NE])).then_inc(rank_in, 16)
                for dst, src in loads:
                    sp.dma_start(dst, t[name + src]).then_inc(w_in, 16)
                if shared:
                    sp.wait_ge(gate_out, TURNS)
                    with sp.Fori(0, NB) as nb:
                        sp.wait_ge(sh_done, nb + 1)
                        sp.dma_start(gate_b[:, :], gate_t[:, bass.ds(nb * QB, QB)]).then_inc(gate_b_ready, 16)

                if out is not None:
                    with sp.Fori(0, NB) as nb:
                        sp.wait_ge(mix_step, nb * last_mix + last_mix + 1)
                        sp.dma_start(out[:, bass.ds(nb * SUB * C, SUB * C)],
                                     H[:, bass.ds(nb * SUB, SUB), :].rearrange("p t f -> p (t f)")
                                     ).then_inc(out_written, 16)
                    sp.wait_ge(out_written, 16 * NB)

            @block.tensor
            def _(pe):
                for j in range(T):
                    for i in range(3):
                        mm = pe.matmul(down[0][:, :, :].rearrange("p e c -> p (e c)")[:, j * NE:(j + 1) * NE],
                                       parts[meets[i]][:, j * P:(j + 1) * P], wr[i][:, :],
                                       start=(i == 0), stop=(i == 2))
                mm.then_inc(logits_mm, 1)
                pe.wait_ge(w_in, 16 * len(loads))
                if straddles:
                    pe.wait_ge(zeros_ready, 1)
                if shared:
                    pe.wait_ge(gate_step, gate_steps)
                    for n in range(TURNS):
                        if n >= 2:
                            pe.wait_ge(gate_out, n - 1)
                        for i in range(SUB):
                            mm = pe.transpose(up[n % 2][0:E, 0, i * P:(i + 1) * P],
                                              gate[:, n * SUB + i, :], ident[:, :])
                        mm.then_inc(gate_turned, 1)
                    pe.wait_ge(gate_out, TURNS)
                with pe.Fori(0, NB) as nb:
                    def up_products(k):
                        if k >= UP:
                            pe.wait_ge(hid_ready, nb * HT + k - UP + 1)
                        for a, w in enumerate([w1, w3] if gated else [w1]):
                            for i in range(3):
                                mm = pe.matmul(up[k % UP][:, a, :], w[i][:, k * P:(k + 1) * P],
                                               parts[meets[i]][:, bass.ds(nb * QB, QB)],
                                               start=(i == 0), stop=(i == 2))
                        mm.then_inc(up_mm, 1)

                    def down_products(tiles):
                        pe.wait_ge(hid_ready, nb * HT + tiles[-1] + 1)
                        if shared and tiles[0] == 0:
                            pe.wait_ge(sh_read, nb + 1)
                            pe.wait_ge(gate_b_ready, nb * 16 + 16)
                        for s in range(SUB):
                            for k in tiles:
                                experts = plan[k]
                                is_shared = experts[0][0] < shared
                                units = hid[:, k % HB, s * P:(s + 1) * P]
                                if is_shared:
                                    _, block_no, opens, closes = experts[0]
                                    mm = pe.matmul(sh_ps[:, s, :], units, w2[:, block_no, :],
                                                   start=opens, stop=False)
                                    if closes:
                                        mm = pe.matmul(sh_ps[:, s, :], gate_b[:, s * P:(s + 1) * P], b2[:, :],
                                                       start=False, stop=True)
                                    continue
                                if k == first_private:
                                    pe.wait_ge(down_read, nb * SUB + s + 1)
                                    if straddles:
                                        pe.matmul(down[s][:, :, :].rearrange("p e c -> p (e c)"), zeros[:, 0:P],
                                                  zeros[:, :], start=True, stop=False)
                                e0, n0, e1 = experts[0][0] - shared, experts[0][1], experts[-1][0] - shared + 1
                                mm = pe.matmul(down[s][:, e0:e1, :].rearrange("p e c -> p (e c)"), units,
                                               w2[:, n0:n0 + e1 - e0, :].rearrange("p e c -> p (e c)"),
                                               start=(k == first_private and not straddles), stop=(k == HT - 1))
                            if is_shared and s == SUB - 1:
                                mm.then_inc(sh_done, 1)
                            elif tiles[-1] == HT - 1:
                                mm.then_inc(down_done, 1)
                            elif s == SUB - 1:
                                mm.then_inc(down_mm, len(tiles))

                    for k in range(HT + LAG):
                        if k < HT:
                            up_products(k)
                        if shared and k - LAG < 2:
                            if k - LAG == 1:
                                down_products([0, 1])
                        elif k >= LAG:
                            down_products([k - LAG])

            def hidden_free(eng, nb, k):
                if shared and HB <= k < HB + 2:
                    eng.wait_ge(sh_done, nb + 2)
                elif k >= HB:
                    eng.wait_ge(down_mm, nb * (HT - 1 - 2 * shared) + k - HB + 1 - 2 * shared)

            @block.scalar
            def _(act):
                act.wait_ge(gate_step, 2)
                act.activation(g["p"][:, :, :], g["p"][:, :, :], ACT.Exp).then_inc(exp_ready, 1)
                if shared:
                    for n in range(TURNS):
                        act.wait_ge(gate_turned, n + 1)
                        act.activation(gate_t[:, n * QB:(n + 1) * QB], up[n % 2][0:E, 0, :],
                                       ACT.Copy).then_inc(gate_out, 1)
                with act.Fori(0, NB) as nb:
                    for k in range(HT):
                        act.wait_ge(up_mm, nb * HT + k + 1)
                        if gated:
                            if k >= 2:
                                act.wait_ge(hid_ready, nb * HT + k - 1)
                            act.activation(act_out[:, k % 2, :], up[k % UP][:, 0, :], ACT.Silu).then_inc(act_done, 1)
                        else:
                            hidden_free(act, nb, k)
                            act.activation(hid[:, k % HB, :], up[k % UP][:, 0, :], ACT.Gelu,
                                           bias=b1[:, k:k + 1]).then_inc(hid_ready, 1)

            @block.gpsimd
            def _(pool):
                if straddles:
                    pool.memset(zeros[:, :], 0.0).then_inc(zeros_ready, 1)
                with pool.Fori(0, NB) as nb:
                    w = lambda i, n: weighted[:, :, i:i + n, :]
                    blk = bass.ds(nb * SUB, SUB)
                    pool.wait_ge(down_read, nb * SUB + 2 * SUB)
                    pool.tensor_tensor(w(0, 4), w(0, 4), w(4, 4), ALU.add).then_inc(mix_step, 1)
                    pool.wait_ge(mix_step, nb * last_mix + 2)
                    pool.tensor_tensor(w(0, 2), w(0, 2), w(2, 2), ALU.add).then_inc(mix_step, 1)
                    pool.wait_ge(mix_step, nb * last_mix + 3)
                    pool.tensor_tensor(weighted[:, :, 0, :], weighted[:, :, 0, :], weighted[:, :, 1, :],
                                       ALU.add).then_inc(mix_step, 1)
                    pool.wait_ge(mix_step, nb * last_mix + 4)
                    if shared:
                        pool.wait_ge(sh_read, nb + 2)
                        pool.tensor_tensor(weighted[:, :, 0, :], weighted[:, :, 0, :], shared_out[:, :, :],
                                           ALU.add).then_inc(mix_step, 1)
                        pool.wait_ge(mix_step, nb * last_mix + 5)
                    pool.tensor_tensor(H[:, blk, :], H[:, blk, :], weighted[:, :, 0, :],
                                       ALU.add).then_inc(mix_step, 1)
                    if residual is not None:
                        pool.wait_ge(mix_step, nb * last_mix + last_mix)
                        pool.tensor_tensor(H[:, blk, :], H[:, blk, :], residual[:, blk, :],
                                           ALU.add).then_inc(mix_step, 1)

            @block.vector
            def _(dve):
                own = 0

                def step(ins):
                    nonlocal own
                    ins.then_inc(gate_step, 1)
                    own += 1
                    dve.wait_ge(gate_step, own)

                wide = lambda a: a.unsqueeze(2).broadcast_to([P, T, NE])
                p, eq, oh, p2 = (g[n][:, :, :] for n in ("p", "eq", "oh", "p2"))
                c = [col[:, i, :] for i in range(4)]
                ranks = rank[:, :].unsqueeze(1).broadcast_to([P, T, NE])
                dve.wait_ge(logits_mm, 1)
                logits = down[0][:, :, :].rearrange("p e c -> p (e c)").rearrange("p (t e) -> p t e", e=NE)
                step(dve.tensor_reduce(c[0], logits, AX.X, ALU.max))
                step(dve.tensor_tensor(p, logits, wide(c[0]), ALU.subtract))
                dve.wait_ge(exp_ready, 1)
                step(dve.tensor_reduce(c[0], p, AX.X, ALU.add))
                step(dve.reciprocal(c[1], c[0]))
                step(dve.tensor_tensor(p, p, wide(c[1]), ALU.mult))

                def first_max(src, largest):
                    step(dve.tensor_reduce(c[largest], src, AX.X, ALU.max))
                    step(dve.tensor_tensor(eq, src, wide(c[largest]), ALU.is_equal))
                    step(dve.tensor_tensor(eq, eq, ranks, ALU.mult))
                    step(dve.tensor_reduce(c[3], eq, AX.X, ALU.max))

                dve.wait_ge(rank_in, 16)
                first_max(p, 0)
                step(dve.tensor_tensor(oh, eq, wide(c[3]), ALU.is_equal))
                step(dve.scalar_tensor_tensor(out=p2, in0=oh, scalar=-2.0, in1=p, op0=ALU.mult, op1=ALU.add))
                first_max(p2, 1)
                step(dve.tensor_tensor(eq, eq, wide(c[3]), ALU.is_equal))
                step(dve.tensor_tensor(oh, oh, eq, ALU.add))
                step(dve.tensor_tensor(c[2], c[0], c[1], ALU.add))
                if denom_eps:
                    step(dve.tensor_scalar(c[2], c[2], denom_eps, None, ALU.add))
                step(dve.reciprocal(c[3], c[2]))
                step(dve.tensor_tensor(p, p, wide(c[3]), ALU.mult))
                if shared:
                    step(dve.memset(gate[:, :, NE:E], 1.0))
                step(dve.tensor_tensor(gate[:, :, 0:NE], p, oh, ALU.mult))
                assert own == gate_steps, own

                dve.sem_inc(down_read, SUB)
                dve.sem_inc(mix_step, 1)
                if shared:
                    dve.sem_inc(sh_done, 1)
                    dve.sem_inc(sh_read, 1)
                with dve.Fori(0, NB) as nb:
                    if gated:
                        for k in range(HT):
                            dve.wait_ge(act_done, nb * HT + k + 1)
                            hidden_free(dve, nb, k)
                            dve.tensor_tensor(hid[:, k % HB, :], act_out[:, k % 2, :], up[k % UP][:, 1, :],
                                              ALU.mult).then_inc(hid_ready, 1)
                    dve.wait_ge(mix_step, nb * last_mix + 1)
                    if shared:
                        dve.wait_ge(sh_done, nb + 2)
                        dve.tensor_copy(shared_out[:, :, :], sh_ps[:, :, :]).then_inc(sh_read, 1)
                    for s in range(SUB):
                        dve.wait_ge(down_done, nb * SUB + s + 1)
                        dve.tensor_tensor(weighted[:, s, :, :], down[s][:, :, :],
                                          gate[:, bass.ds(nb * SUB + s, 1), 0:NE]
                                          .rearrange("p t e -> p (t e)").unsqueeze(2)
                                          .broadcast_to([P, NE, C]), ALU.mult).then_inc(down_read, 1)


def linear_attention_stage(nc, t, H, XT):
    NBL = 2 * NQ
    with ExitStack() as ctx:
        sb = lambda n, s, d=F32: ctx.enter_context(nc.sbuf_tensor("lin_" + n, s, d))
        ps = lambda n, s, d=F32: ctx.enter_context(nc.psum_tensor("lin_" + n, s, d))
        sem = stage_semaphores(nc, ctx, "lin_")
        w = sb("w", [C, 3 * C])
        b_qk = sb("b_qk", [P, 1])
        b_kv = sb("b_kv", [P, 2 * C])
        decay = sb("decay", [P, P])
        q_decay = sb("q_decay", [C, P])
        k_decay = sb("k_decay", [P, 1])
        BUFS = 3
        q_t, k_t, qd_t = (sb(n, [C, BUFS, QB]) for n in ("q_t", "k_t", "qd_t"))
        kv = sb("kv", [P, BUFS, SUB, 2 * C])
        kd = sb("kd", [P, 2, SUB, C])
        pr = sb("probs", [P, 2, SUB, P])
        state = sb("state", [C, B, NT + 1, C])
        qk_ps, kv_ps = ps("qk_ps", [P, 2, QB]), ps("kv_ps", [P, 2, SUB, 2 * C])
        sc_ps, st_ps, out_ps = ps("sc_ps", [P, SUB, P]), ps("st_ps", [C, SUB, C]), ps("out_ps", [P, SUB, C])
        w_in, proj, q_ready, k_ready, kv_ready, kd_ready, qd_ready = (
            sem(n) for n in ("w_in", "proj", "q_ready", "k_ready", "kv_ready", "kd_ready", "qd_ready"))
        scored, pr_ready, st_mm, st_ready, out_mm, out_read, zeroed = (
            sem(n) for n in ("scored", "pr_ready", "st_mm", "st_ready", "out_mm", "out_read", "zeroed"))
        loads = [(w[:, :], t["lin_w"]), (b_qk[:, :], t["lin_b_qk"]), (b_kv[:, :], t["lin_b_kv"].broadcast_to([P, 2 * C])),
                 (decay[:, :], t["lin_decay"]), (q_decay[:, :], t["lin_q_decay"].broadcast_to([C, P])),
                 (k_decay[:, :], t["lin_k_decay"])]
        first = lambda n: (n % B) * N + (n // B) * QB

        with nc.Block() as block:
            @block.sync
            def _(sp):
                for dst, src in loads:
                    sp.dma_start(dst, src).then_inc(w_in, 16)

            @block.tensor
            def _(pe):
                pe.wait_ge(w_in, 16 * len(loads))
                for n in range(NBL + 2):
                    if n < NBL:
                        if n >= 2:
                            pe.wait_ge(q_ready, n - 1)
                            pe.wait_ge(k_ready, n - 1)
                            pe.wait_ge(kv_ready, n - 1)
                        x = XT[:, first(n):first(n) + QB]
                        pe.matmul(qk_ps[:, n % 2, :], w[:, 0:2 * C], x, start=True, stop=True)
                        for i in range(SUB):
                            mm = pe.matmul(kv_ps[:, n % 2, i, :], x[:, i * P:(i + 1) * P], w[:, C:3 * C],
                                           start=True, stop=True)
                        mm.then_inc(proj, 1)
                    if 1 <= n <= NBL:
                        m = n - 1
                        pe.wait_ge(q_ready, m + 1)
                        pe.wait_ge(k_ready, m + 1)
                        if m:
                            pe.wait_ge(pr_ready, m)
                            pe.wait_ge(st_ready, m)
                        for i in range(SUB):
                            mm = pe.matmul(sc_ps[:, i, :], k_t[:, m % BUFS, i * P:(i + 1) * P],
                                           q_t[:, m % BUFS, i * P:(i + 1) * P], start=True, stop=True)
                        mm.then_inc(scored, 1)
                        pe.wait_ge(kd_ready, m + 1)
                        for i in range(SUB):
                            mm = pe.matmul(st_ps[:, i, :], kd[:, m % 2, i, :], kv[:, m % BUFS, i, C:2 * C],
                                           start=True, stop=True)
                        mm.then_inc(st_mm, 1)
                    if n >= 2:
                        m = n - 2
                        pe.wait_ge(pr_ready, m + 1)
                        pe.wait_ge(st_ready, m + 1)
                        pe.wait_ge(qd_ready, m + 1)
                        if m:
                            pe.wait_ge(out_read, m)
                        for i in range(SUB):
                            pe.matmul(out_ps[:, i, :], pr[:, m % 2, i, :], kv[:, m % BUFS, i, C:2 * C],
                                      start=True, stop=False)
                            mm = pe.matmul(out_ps[:, i, :], qd_t[:, m % BUFS, i * P:(i + 1) * P],
                                           state[:, m % B, (m // B) * SUB + i, :], start=False, stop=True)
                        mm.then_inc(out_mm, 1)

            @block.scalar
            def _(act):
                act.wait_ge(w_in, 16 * len(loads))
                for n in range(NBL):
                    act.wait_ge(proj, n + 1)
                    if n >= BUFS:
                        act.wait_ge(scored, n - BUFS + 1)
                    act.wait_ge(q_ready, n + 1)
                    act.activation(k_t[:, n % BUFS, :], qk_ps[C:2 * C, n % 2, :], ACT.Identity,
                                   bias=b_qk[C:2 * C, :]).then_inc(k_ready, 1)
                    act.wait_ge(kv_ready, n + 1)
                    if n >= 2:
                        act.wait_ge(st_mm, n - 1)
                    act.activation(kd[:, n % 2, :, :], kv[:, n % BUFS, :, 0:C], ACT.Copy,
                                   scale=k_decay[:, 0:1]).then_inc(kd_ready, 1)

            @block.vector
            def _(dve):
                dve.memset(state[:, :, 0, :], 0.0).then_inc(zeroed, 1)
                dve.wait_ge(zeroed, 1)
                dve.wait_ge(w_in, 16 * len(loads))
                for n in range(NBL + 2):
                    if n < NBL:
                        dve.wait_ge(proj, n + 1)
                        if n >= BUFS:
                            dve.wait_ge(out_mm, n - BUFS + 1)
                        dve.tensor_scalar(q_t[:, n % BUFS, :], qk_ps[0:C, n % 2, :], b_qk[0:C, :], C ** -0.5, ALU.add,
                                          ALU.mult).then_inc(q_ready, 1)
                        dve.tensor_tensor(kv[:, n % BUFS, :, :], kv_ps[:, n % 2, :, :],
                                          b_kv[:, :].unsqueeze(1).broadcast_to([P, SUB, 2 * C]),
                                          ALU.add).then_inc(kv_ready, 1)
                        dve.wait_ge(q_ready, n + 1)
                        dve.tensor_tensor(qd_t[:, n % BUFS, :].rearrange("c (i q) -> c i q", i=SUB),
                                          q_t[:, n % BUFS, :].rearrange("c (i q) -> c i q", i=SUB),
                                          q_decay[:, :].unsqueeze(1).broadcast_to([C, SUB, P]),
                                          ALU.mult).then_inc(qd_ready, 1)
                    if 1 <= n <= NBL:
                        m = n - 1
                        dve.wait_ge(scored, m + 1)
                        if m >= 2:
                            dve.wait_ge(out_mm, m - 1)
                        dve.tensor_tensor(pr[:, m % 2, :, :], sc_ps[:, :, :],
                                          decay[:, :].unsqueeze(1).broadcast_to([P, SUB, P]),
                                          ALU.mult).then_inc(pr_ready, 1)
                        dve.wait_ge(st_mm, m + 1)
                        for i in range(SUB):
                            c = (m // B) * SUB + i
                            ins = dve.scalar_tensor_tensor(out=state[:, m % B, c + 1, :], in0=state[:, m % B, c, :],
                                                           scalar=float(ALPHA ** P), in1=st_ps[:, i, :],
                                                           op0=ALU.mult, op1=ALU.add)
                            if i < SUB - 1:
                                ins.then_inc(zeroed, 1)
                                dve.wait_ge(zeroed, m * (SUB - 1) + i + 2)
                        ins.then_inc(st_ready, 1)
                    if n >= 2:
                        m = n - 2
                        dve.wait_ge(out_mm, m + 1)
                        tile = first(m) // P
                        dve.tensor_tensor(H[:, tile:tile + SUB, :], H[:, tile:tile + SUB, :], out_ps[:, :, :],
                                          ALU.add).then_inc(out_read, 1)


def tower(nc, t, out):
    with ExitStack() as ctx:
        sb = lambda n, s, d=F32: ctx.enter_context(nc.sbuf_tensor(n, s, d))
        H = sb("H", [P, T, C])
        ident = sb("ident", [P, P])
        identb = sb("identb", [P, P], BF16)
        gains = sb("gains", [C, 2])
        ident_in, gains_in, ident_cast = (
            ctx.enter_context(nc.semaphore(n)) for n in ("ident_in", "gains_in", "ident_cast"))
        with nc.Block() as block:
            @block.sync
            def _(sp):
                sp.dma_start(ident[:, :], t["ident"]).then_inc(ident_in, 16)
                sp.dma_start(gains[:, :], t["gains"]).then_inc(gains_in, 16)
                sp.wait_ge(gains_in, 16)

            @block.vector
            def _(dve):
                dve.wait_ge(ident_in, 16)
                dve.tensor_copy(identb[:, :], ident[:, :]).then_inc(ident_cast, 1)
                dve.wait_ge(ident_cast, 1)

        involution_stage(nc, t, H)
        with ExitStack() as c2:
            XT = c2.enter_context(nc.sbuf_tensor("XT", [C, T * P], F32))
            norm_stage(nc, "ln1_", H, XT, ident, True, 1e-5)
            attention0_stage(nc, t, H, XT, ident, identb)
        with ExitStack() as c2:
            parts = [c2.enter_context(nc.sbuf_tensor(f"XT2_{i}", [P, T * P], BF16)) for i in range(2)]
            norm_stage(nc, "ln2_", H, None, ident, True, 1e-5, parts=parts)
            moe_stage(nc, "moe0_", t, H, parts, ident, F0, 1, False, 0.0)
        with ExitStack() as c2:
            XT = c2.enter_context(nc.sbuf_tensor("XT3", [C, T * P], F32))
            norm_stage(nc, "ln3_", H, XT, ident, True, 1e-5)
            linear_attention_stage(nc, t, H, XT)
        final_stages(nc, t, H, ident, identb, gains, out)


def final_stages(nc, t, H, ident, identb, gains, out):
    with ExitStack() as ctx:
        U = ctx.enter_context(nc.sbuf_tensor("U", [P, T, C], F32))
        norm_stage(nc, "ln4_", H, None, ident, True, 1e-5, U=U)
        with ExitStack() as c2:
            XT = c2.enter_context(nc.sbuf_tensor("XT4", [C, T * P], F32))
            norm_stage(nc, "rms1_", U, XT, ident, False, 1e-6, gain=gains[:, 0:1])
            attention1_stage(nc, t, U, XT, ident, identb)
        with ExitStack() as c2:
            parts = [c2.enter_context(nc.sbuf_tensor(f"XT5_{i}", [P, T * P], BF16)) for i in range(2)]
            norm_stage(nc, "rms2_", U, None, ident, False, 1e-6, gain=gains[:, 1:2], parts=parts)
            moe_stage(nc, "moe1_", t, U, parts, ident, F1, 0, True, 1e-9, residual=H, out=out)


def bias_table():
    n = np.arange(N, dtype=np.float64)
    return np.stack([f(2 * np.pi * n / period) for period in (24.0, 720.0) for f in (np.cos, np.sin)]
                    ).astype(np.float32)


def key_bias_rows():
    table = bias_table()
    low_type = mybir.dt.np(BF16)
    high = table.astype(low_type)
    low = (table - high.astype(np.float32)).astype(low_type)
    rows = np.zeros((M_ROW + 1 - C, N), np.float32)
    rows[0:4], rows[-1] = table, 1
    return {"at0_k_rows": rows, "at0_k_parts": np.concatenate([high, low, high, low])}


def decay_tables():
    n = np.arange(P, dtype=np.float64)
    between = n[None, :] - n[:, None]
    return {"lin_decay": np.where(between >= 0, ALPHA ** np.maximum(between, 0), 0.0).astype(np.float32),
            "lin_q_decay": (ALPHA ** (n + 1)).astype(np.float32)[None],
            "lin_k_decay": (ALPHA ** (P - 1 - n)).astype(np.float32)[:, None]}


def rotary_tables():
    inv = 1.0 / 10000.0 ** (np.arange(0, HD, 2, dtype=np.float32) / HD)
    angle = np.outer(np.arange(N, dtype=np.float32), inv).reshape(NT, P, HD // 2).transpose(1, 0, 2)
    return {"at1_cos": np.cos(angle), "at1_sin": np.sin(angle)}


def causal_masks():
    n = np.arange(P)
    after = (n[None, :] > n[:, None]) * np.float32(NEG)
    return np.stack([after, after.T], 1).astype(mybir.dt.np(BF16))


def output_rows(wo):
    a = np.zeros((NH, 32, NH, C + 1), np.float32)
    for h in range(NH):
        a[h, :HD, h, :C] = wo[:, h * HD:(h + 1) * HD].T
        a[h, HD, h, C] = 1
    return a.reshape(P, NH * (C + 1))


def joined_units(w):
    w = w.reshape(C, -1)
    return np.pad(w, ((0, 0), (0, -w.shape[1] % P)))


def expert_rows(w2):
    plan, blocks = hidden_plan(*w2.shape[:2])
    a = np.zeros((blocks, P, C), np.float32)
    for k, tile in enumerate(plan):
        for e, n, _, _ in tile:
            first, last = max(e * w2.shape[1], k * P), min((e + 1) * w2.shape[1], (k + 1) * P)
            a[n, first - k * P:last - k * P] = w2[e, first - e * w2.shape[1]:last - e * w2.shape[1]]
    return a.transpose(1, 0, 2)


def layouts(i):
    f = lambda n: np.asarray(i[n])
    x = f("x")
    a = {
        "x_rows": x.reshape(B, NT, 2, S, S).transpose(2, 3, 0, 1, 4),
        "x_chan": x.reshape(B, C, N).transpose(1, 0, 2).reshape(C, B * N),
        "conv1T": f("L0_tok_conv1_w").T,
        "conv2T": f("L0_tok_conv2_w").T,
        "bn": np.stack([f("L0_tok_conv1_b"), f("L0_tok_bn_gamma"), f("L0_tok_bn_beta"),
                        f("L0_tok_bn_mean"), f("L0_tok_bn_var")], 1),
        "conv2_b": f("L0_tok_conv2_b")[:, None],
        "ident": np.eye(P, dtype=np.float32),
        "at0_w": np.concatenate([f("L0_attn_Wq").T, f("L0_attn_Wk").T, f("L0_attn_Wv").T], 1),
        "at0_b": np.stack([f("L0_attn_bq"), f("L0_attn_bk")], 1),
        "at0_bv": f("L0_attn_bv")[None],
        "at0_beta": np.repeat(f("L0_attn_beta"), P // 2)[:, None],
        "at0_table": bias_table().reshape(P, -1),
        **key_bias_rows(),
        "rank": np.arange(NE, 0, -1, dtype=np.float32)[None],
        "moe0_router": f("L0_ffn_Wr"),
        "moe0_w1": joined_units(np.concatenate([f("L0_ffn_W1s")[None], f("L0_ffn_W1p")]).transpose(1, 0, 2)),
        "moe0_w2": expert_rows(np.concatenate([f("L0_ffn_W2s")[None], f("L0_ffn_W2p")])),
        "moe0_b1": np.concatenate([f("L0_ffn_b1s")[None], f("L0_ffn_b1p")]).reshape(-1, P).T,
        "moe0_b2": np.concatenate([f("L0_ffn_b2p"), f("L0_ffn_b2s")[None]]),
        "lin_w": f("L1_attn_Wqkv"),
        "lin_b_qk": f("L1_attn_bqkv")[:2 * C, None],
        "lin_b_kv": f("L1_attn_bqkv")[None, C:],
        **decay_tables(),
        "gains": np.stack([f("L1_ffn_ln1_w"), f("L1_ffn_ln2_w")], 1),
        "at1_w": np.concatenate([f("L1_ffn_wq"), f("L1_ffn_wk"), f("L1_ffn_wv")]).T,
        "at1_wo": output_rows(f("L1_ffn_wo")),
        **rotary_tables(),
        "causal_mask": causal_masks(),
        "moe1_router": f("L1_ffn_router_w").T,
        "moe1_w1": joined_units(f("L1_ffn_w1").transpose(2, 0, 1)),
        "moe1_w3": joined_units(f("L1_ffn_w3").transpose(2, 0, 1)),
        "moe1_w2": expert_rows(f("L1_ffn_w2").transpose(0, 2, 1)),
    }
    a["x_rows"] = a["x_rows"].reshape(P, B, NT, S)
    return {k: np.ascontiguousarray(v) for k, v in a.items()}


def kernel(**inputs):
    import concourse.bacc as _bacc
    from concourse.bass_utils import run_bass_kernel_spmd as _run

    nc = _bacc.Bacc("TRN2", target_bir_lowering=False, num_devices=1)
    arrays = layouts(inputs)
    t = {n: nc.dram_tensor(n + "_dram", a.shape, mybir.dt.from_np(a.dtype), kind="ExternalInput").ap()
         for n, a in arrays.items()}
    t["wd_dram"] = nc.dram_tensor("wd_scratch", (TAPS, B * N), F32, kind="Internal").ap()
    out = nc.dram_tensor("out_0_dram", (P, T * C), F32, kind="ExternalOutput").ap()
    tower(nc, t, out)
    r = _run(nc, [{n + "_dram": a for n, a in arrays.items()}], core_ids=[0])
    got = r.results[0]["out_0_dram"]
    return got.reshape(P, B, NT, C).transpose(1, 2, 0, 3).reshape(B, N, C)
```
